# Optimizing a Trainium2 kernel written in Bass

```python
import numpy as np
import jax
import jax.numpy as jnp

def _softmax(x, axis=-1):
    return jax.nn.softmax(x, axis=axis)

def _gelu(x):
    return jax.nn.gelu(x, approximate=True)

def _silu(x):
    return jax.nn.silu(x)

def _sigmoid(x):
    return jax.nn.sigmoid(x)

def _layernorm(x, axis=-1, eps=1e-05):
    m = jnp.mean(x, axis=axis, keepdims=True)
    v = jnp.var(x, axis=axis, keepdims=True)
    return (x - m) / jnp.sqrt(v + eps)

def _scatter_add(tgt, idx, src, axis=0):
    return tgt.at[idx].add(src)

def _segment_sum(src, seg, n):
    return jax.ops.segment_sum(src, seg, n)
kernel_name = 'mk_flamingo_gated_d2_seqx_r8_d88a8e'

def setup_inputs(seed: int=0):
    np.random.seed(seed)
    _w = jnp.asarray

    def _rec_inputs():
        import jax
        import jax.numpy as jnp
        _rk = jax.random.key(seed)
        x = 2.818e-05 + 1 * jax.random.normal(jax.random.fold_in(_rk, 1), (4, 256, 256), jnp.float32)
        _lenS = 256 - jax.random.randint(jax.random.fold_in(_rk, 7), (4,), 0, max(1, 256 // 4) + 1, jnp.int32)
        _lenS2 = 256 - jax.random.randint(jax.random.fold_in(_rk, 8), (4,), 0, max(1, 256 // 4) + 1, jnp.int32)
        _ctx_1024P = jax.random.normal(jax.random.fold_in(_rk, 11), (4, 16, 128), jnp.float32)
        _ctx_1024c = jax.random.dirichlet(jax.random.fold_in(_rk, 511), 0.3 * jnp.ones((16,), jnp.float32), (4, 256))
        _ctx_1024t = jnp.einsum('bsk,bkd->bsd', _ctx_1024c, _ctx_1024P)
        _ctx_1024t = _ctx_1024t * jax.lax.rsqrt(jnp.mean(jnp.square(_ctx_1024t)) + 1e-12) * 0.953939
        ctx_1024 = 7.22013e-05 + 1.00017 * (_ctx_1024t + 0.3 * jax.random.normal(jax.random.fold_in(_rk, 611), (4, 256, 128), jnp.float32))
        _validS = jnp.arange(256)[None, :] < _lenS[:, None]
        _validS2 = jnp.arange(256)[None, :] < _lenS2[:, None]
        _causal = jnp.tril(jnp.ones((256, 256), dtype=bool))
        mask_BxS2_bf1 = jnp.ones((4, 256), dtype=bool)
        _g = jax.random.normal(jax.random.fold_in(_rk, 9001), (2, 2), jnp.float32)
        _g = jnp.sign(_g) * jnp.maximum(jnp.abs(_g), 1.0) + (_g == 0) * 1.0
        g_xattn = _g[0]
        g_ffn = _g[1]
        return (x, ctx_1024, mask_BxS2_bf1, g_xattn, g_ffn)
    x, ctx_1024, mask_BxS2_bf1, g_xattn, g_ffn = _rec_inputs()

    def _L0_xattn_setup():
        import jax, jax.numpy as jnp
        import numpy as np
        B_, L_, D_MODEL = (4, 256, 128)
        D_STATE, D_CONV, EXPAND = (16, 4, 2)
        D_INNER = EXPAND * D_MODEL
        DT_RANK = (D_MODEL + 15) // 16

        def silu(x):
            return x * jax.nn.sigmoid(x)
        key = jax.random.key(seed)
        ks = jax.random.split(key, 10)
        f32 = jnp.float32
        hidden_states = jax.random.normal(ks[0], (B_, L_, D_MODEL), dtype=f32)
        z = jax.random.normal(ks[1], (B_, D_INNER, L_), dtype=f32)
        in_proj_w = jax.random.normal(ks[2], (D_INNER, D_MODEL), dtype=f32) * 0.02
        conv_w = jax.random.normal(ks[3], (D_INNER, 1, D_CONV), dtype=f32) * 0.1
        conv_b = jax.random.normal(ks[4], (D_INNER,), dtype=f32) * 0.02
        x_proj_w = jax.random.normal(ks[5], (DT_RANK + 2 * D_STATE, D_INNER), dtype=f32) * 0.02
        dt_proj_w = jax.random.uniform(ks[6], (D_INNER, DT_RANK), dtype=f32, minval=-DT_RANK ** (-0.5), maxval=DT_RANK ** (-0.5))
        dt = jnp.exp(jax.random.uniform(ks[7], (D_INNER,), dtype=f32, minval=np.log(0.001), maxval=np.log(0.1)))
        dt_proj_b = jnp.log(jnp.expm1(dt))
        A_log = jnp.log(jnp.broadcast_to(jnp.arange(1, D_STATE + 1, dtype=f32), (D_INNER, D_STATE)))
        D = jnp.ones((D_INNER,), f32)
        return {'hidden_states': hidden_states, 'z': z, 'in_proj_w': in_proj_w, 'conv_w': conv_w, 'conv_b': conv_b, 'x_proj_w': x_proj_w, 'dt_proj_w': dt_proj_w, 'dt_proj_b': dt_proj_b, 'A_log': A_log, 'D': D}
    _L0_xattn_all = _L0_xattn_setup()
    _L0_xattn_in = {k: v for k, v in _L0_xattn_all.items() if k in ('in_proj_w', 'conv_w', 'conv_b', 'x_proj_w', 'dt_proj_w', 'dt_proj_b', 'A_log', 'D')}
    del _L0_xattn_all

    def _L0_ffn_setup():
        import jax, jax.numpy as jnp
        import numpy as np
        EPS = 1e-05
        NUM_BITS = 8

        def _round_ste(x):
            return x + jax.lax.stop_gradient(jnp.round(x) - x)

        def _clamp_ste(x, lo=-1.0, hi=1.0):
            return x + jax.lax.stop_gradient(jnp.clip(x, lo, hi) - x)

        def ternary_quantize(w):
            scale = jnp.maximum(jnp.mean(jnp.abs(w)), EPS)
            q = _clamp_ste(_round_ste(w / scale))
            return scale * q

        def quantized_relu2(x, num_bits=NUM_BITS, eps=EPS):
            x = jnp.square(jax.nn.relu(x))
            xmax = jnp.maximum(jnp.max(x, axis=-1, keepdims=True), eps)
            num_steps = 2 ** num_bits - 1
            return _round_ste(x / xmax * num_steps) / num_steps * xmax
        key = jax.random.key(seed)
        k1, k2, k3 = jax.random.split(key, 3)
        B, S, D = (4, 256, 256)
        H = 4 * D
        std = 0.5 * D ** (-0.5)
        x = jax.random.normal(k1, (B, S, D), dtype=jnp.float32)
        c_fc = jax.random.normal(k2, (D, H), dtype=jnp.float32) * std
        c_proj = jax.random.normal(k3, (D, H), dtype=jnp.float32) * std
        return {'x': x, 'c_fc': c_fc, 'c_proj': c_proj}
    _L0_ffn_all = _L0_ffn_setup()
    _L0_ffn_in = {k: v for k, v in _L0_ffn_all.items() if k in ('c_fc', 'c_proj')}
    del _L0_ffn_all

    def _L1_xattn_setup():
        import jax, jax.numpy as jnp
        import numpy as np
        N_HEADS = 16
        N_KV_HEADS = 8
        HEAD_DIM = 128
        D_TEXT = 256
        D_VISION = 128
        GROUPS = N_HEADS // N_KV_HEADS
        key = jax.random.key(seed)
        ks = jax.random.split(key, 6)
        B, T_text, T_vis = (4, 256, 72)
        text_hidden = jax.random.normal(ks[0], (B, T_text, D_TEXT), dtype=jnp.float32)
        vision_tokens = jax.random.normal(ks[1], (B, T_vis, D_VISION), dtype=jnp.float32)
        vision_mask = jnp.ones((B, T_vis), dtype=bool)
        s = 0.02
        Wq = jax.random.normal(ks[2], (D_TEXT, N_HEADS * HEAD_DIM), dtype=jnp.float32) * s
        Wk = jax.random.normal(ks[3], (D_VISION, N_KV_HEADS * HEAD_DIM), dtype=jnp.float32) * s
        Wv = jax.random.normal(ks[4], (D_VISION, N_KV_HEADS * HEAD_DIM), dtype=jnp.float32) * s
        Wo = jax.random.normal(ks[5], (N_HEADS * HEAD_DIM, D_TEXT), dtype=jnp.float32) * s
        return {'text_hidden': text_hidden, 'vision_tokens': vision_tokens, 'vision_mask': vision_mask, 'Wq': Wq, 'Wk': Wk, 'Wv': Wv, 'Wo': Wo}
    _L1_xattn_all = _L1_xattn_setup()
    _L1_xattn_in = {k: v for k, v in _L1_xattn_all.items() if k in ('Wq', 'Wk', 'Wv', 'Wo')}
    del _L1_xattn_all

    def _L1_ffn_setup():
        import jax, jax.numpy as jnp
        import numpy as np
        B, S, D = (2, 256, 256)
        F = 128
        E = 64
        K = 8
        C = 128
        NORM_TOPK = False

        def _moe(x, gate_w, w_gate, w_up, w_down):
            b, s, d = x.shape
            T = b * s
            x2 = x.reshape(T, d)
            logits = x2 @ gate_w.T
            probs = jax.nn.softmax(logits.astype(jnp.float32), axis=-1)
            top_w, top_i = jax.lax.top_k(probs, K)
            if NORM_TOPK:
                top_w = top_w / jnp.sum(top_w, axis=-1, keepdims=True)
            top_w = top_w.astype(x.dtype)
            flat_e = top_i.reshape(-1)
            flat_w = top_w.reshape(-1)
            tok = jnp.arange(T * K) // K
            onehot = jax.nn.one_hot(flat_e, E, dtype=jnp.int32)
            pos = jnp.sum(jnp.cumsum(onehot, axis=0) * onehot, axis=-1) - 1
            valid = pos < C
            loc = flat_e * C + jnp.minimum(pos, C - 1)
            flat_w = jnp.where(valid, flat_w, 0.0)
            safe_loc = jnp.where(valid, loc, E * C)
            xg = jnp.zeros((E * C + 1, d), dtype=x.dtype).at[safe_loc].set(x2[tok])[:E * C]
            xg = xg.reshape(E, C, d)
            h = jax.nn.silu(jnp.einsum('ecd,edf->ecf', xg, w_gate)) * jnp.einsum('ecd,edf->ecf', xg, w_up)
            y = jnp.einsum('ecf,efd->ecd', h, w_down).reshape(E * C, d)
            y_tok = y[loc] * flat_w[:, None]
            out = jnp.zeros((T, d), dtype=x.dtype).at[tok].add(y_tok)
            return out.reshape(b, s, d)
        key = jax.random.key(seed)
        ks = jax.random.split(key, 5)
        scale = 0.02
        return {'hidden_states': jax.random.normal(ks[0], (B, S, D), dtype=jnp.float32), 'gate_w': jax.random.normal(ks[1], (E, D), dtype=jnp.float32) * scale, 'w_gate': jax.random.normal(ks[2], (E, D, F), dtype=jnp.float32) * scale, 'w_up': jax.random.normal(ks[3], (E, D, F), dtype=jnp.float32) * scale, 'w_down': jax.random.normal(ks[4], (E, F, D), dtype=jnp.float32) * scale}
    _L1_ffn_all = _L1_ffn_setup()
    _L1_ffn_in = {k: v for k, v in _L1_ffn_all.items() if k in ('gate_w', 'w_gate', 'w_up', 'w_down')}
    del _L1_ffn_all
    return {'x': x, 'ctx_1024': ctx_1024, 'mask_BxS2_bf1': mask_BxS2_bf1, 'g_xattn': g_xattn, 'g_ffn': g_ffn, 'L0_xattn_in_proj_w': _L0_xattn_in['in_proj_w'], 'L0_xattn_conv_w': _L0_xattn_in['conv_w'], 'L0_xattn_conv_b': _L0_xattn_in['conv_b'], 'L0_xattn_x_proj_w': _L0_xattn_in['x_proj_w'], 'L0_xattn_dt_proj_w': _L0_xattn_in['dt_proj_w'], 'L0_xattn_dt_proj_b': _L0_xattn_in['dt_proj_b'], 'L0_xattn_A_log': _L0_xattn_in['A_log'], 'L0_xattn_D': _L0_xattn_in['D'], 'L0_ffn_c_fc': _L0_ffn_in['c_fc'], 'L0_ffn_c_proj': _L0_ffn_in['c_proj'], 'L1_xattn_Wq': _L1_xattn_in['Wq'], 'L1_xattn_Wk': _L1_xattn_in['Wk'], 'L1_xattn_Wv': _L1_xattn_in['Wv'], 'L1_xattn_Wo': _L1_xattn_in['Wo'], 'L1_ffn_gate_w': _L1_ffn_in['gate_w'], 'L1_ffn_w_gate': _L1_ffn_in['w_gate'], 'L1_ffn_w_up': _L1_ffn_in['w_up'], 'L1_ffn_w_down': _L1_ffn_in['w_down']}

def reference(x, ctx_1024, mask_BxS2_bf1, g_xattn, g_ffn, L0_xattn_in_proj_w, L0_xattn_conv_w, L0_xattn_conv_b, L0_xattn_x_proj_w, L0_xattn_dt_proj_w, L0_xattn_dt_proj_b, L0_xattn_A_log, L0_xattn_D, L0_ffn_c_fc, L0_ffn_c_proj, L1_xattn_Wq, L1_xattn_Wk, L1_xattn_Wv, L1_xattn_Wo, L1_ffn_gate_w, L1_ffn_w_gate, L1_ffn_w_up, L1_ffn_w_down):
    import jax
    import jax.numpy as jnp

    def _L0_xattn_ref(hidden_states, z, in_proj_w, conv_w, conv_b, x_proj_w, dt_proj_w, dt_proj_b, A_log, D):
        import jax, jax.numpy as jnp
        import numpy as np
        B_, L_, D_MODEL = (4, 256, 128)
        D_STATE, D_CONV, EXPAND = (16, 4, 2)
        D_INNER = EXPAND * D_MODEL
        DT_RANK = (D_MODEL + 15) // 16

        def silu(x):
            return x * jax.nn.sigmoid(x)
        Bsz, L, _ = hidden_states.shape
        d_inner, _, d_conv = conv_w.shape
        dt_rank = dt_proj_w.shape[1]
        d_state = A_log.shape[1]
        x = jnp.einsum('bld,ed->bel', hidden_states, in_proj_w)
        xc = jax.lax.conv_general_dilated(x, conv_w, window_strides=(1,), padding=[(d_conv - 1, 0)], feature_group_count=d_inner, dimension_numbers=('NCH', 'OIH', 'NCH'))
        x = silu(xc + conv_b[None, :, None])
        x_dbl = jnp.einsum('bdl,ed->bel', x, x_proj_w)
        dt_low, Bm, Cm = jnp.split(x_dbl, [dt_rank, dt_rank + d_state], axis=1)
        dt = jnp.einsum('brl,dr->bdl', dt_low, dt_proj_w)
        dt = jax.nn.softplus(dt + dt_proj_b[None, :, None])
        A = -jnp.exp(A_log)
        dt_t = jnp.moveaxis(dt, -1, 0)
        B_t = jnp.moveaxis(Bm, -1, 0)
        C_t = jnp.moveaxis(Cm, -1, 0)
        u_t = jnp.moveaxis(x, -1, 0)

        def step(state, inp):
            d, b, c, u = inp
            dA = jnp.exp(d[..., None] * A)
            state = state * dA + (d * u)[..., None] * b[:, None, :]
            y = jnp.einsum('bdn,bn->bd', state, c)
            return (state, y)
        state0 = jnp.zeros((Bsz, d_inner, d_state), x.dtype)
        _, ys = jax.lax.scan(step, state0, (dt_t, B_t, C_t, u_t))
        y = jnp.moveaxis(ys, 0, 2)
        y = y + D[None, :, None] * x
        y = y * silu(z)
        return jnp.swapaxes(y, 1, 2)

    def _L0_ffn_ref(x, c_fc, c_proj):
        import jax, jax.numpy as jnp
        import numpy as np
        EPS = 1e-05
        NUM_BITS = 8

        def _round_ste(x):
            return x + jax.lax.stop_gradient(jnp.round(x) - x)

        def _clamp_ste(x, lo=-1.0, hi=1.0):
            return x + jax.lax.stop_gradient(jnp.clip(x, lo, hi) - x)

        def ternary_quantize(w):
            scale = jnp.maximum(jnp.mean(jnp.abs(w)), EPS)
            q = _clamp_ste(_round_ste(w / scale))
            return scale * q

        def quantized_relu2(x, num_bits=NUM_BITS, eps=EPS):
            x = jnp.square(jax.nn.relu(x))
            xmax = jnp.maximum(jnp.max(x, axis=-1, keepdims=True), eps)
            num_steps = 2 ** num_bits - 1
            return _round_ste(x / xmax * num_steps) / num_steps * xmax
        w1 = ternary_quantize(c_fc)
        h = jnp.einsum('bsd,dh->bsh', x, w1)
        h = quantized_relu2(h, num_bits=NUM_BITS)
        w2 = ternary_quantize(c_proj)
        out = jnp.einsum('bsh,dh->bsd', h, w2)
        return out

    def _L1_xattn_ref(text_hidden, vision_tokens, vision_mask, Wq, Wk, Wv, Wo):
        import jax, jax.numpy as jnp
        import numpy as np
        N_HEADS = 16
        N_KV_HEADS = 8
        HEAD_DIM = 128
        D_TEXT = 256
        D_VISION = 128
        GROUPS = N_HEADS // N_KV_HEADS
        B, T_text, _ = text_hidden.shape
        T_vis = vision_tokens.shape[1]
        scale = jnp.float32(np.sqrt(HEAD_DIM))
        q = (text_hidden @ Wq).reshape(B, T_text, N_HEADS, HEAD_DIM).transpose(0, 2, 1, 3)
        k = (vision_tokens @ Wk).reshape(B, T_vis, N_KV_HEADS, HEAD_DIM).transpose(0, 2, 1, 3)
        v = (vision_tokens @ Wv).reshape(B, T_vis, N_KV_HEADS, HEAD_DIM).transpose(0, 2, 1, 3)
        k = jnp.repeat(k, GROUPS, axis=1)
        v = jnp.repeat(v, GROUPS, axis=1)
        scores = jnp.einsum('bhtd,bhsd->bhts', q, k) / scale
        mask = vision_mask[:, None, None, :]
        scores = jnp.where(mask, scores, -jnp.inf)
        attn = jax.nn.softmax(scores, axis=-1)
        attn = jnp.nan_to_num(attn, nan=0.0)
        out = jnp.einsum('bhts,bhsd->bhtd', attn, v)
        out = out.transpose(0, 2, 1, 3).reshape(B, T_text, N_HEADS * HEAD_DIM)
        return out @ Wo

    def _L1_ffn_ref(hidden_states, gate_w, w_gate, w_up, w_down):
        import jax, jax.numpy as jnp
        import numpy as np
        B, S, D = (2, 256, 256)
        F = 128
        E = 64
        K = 8
        C = 128
        NORM_TOPK = False

        def _moe(x, gate_w, w_gate, w_up, w_down):
            b, s, d = x.shape
            T = b * s
            x2 = x.reshape(T, d)
            logits = x2 @ gate_w.T
            probs = jax.nn.softmax(logits.astype(jnp.float32), axis=-1)
            top_w, top_i = jax.lax.top_k(probs, K)
            if NORM_TOPK:
                top_w = top_w / jnp.sum(top_w, axis=-1, keepdims=True)
            top_w = top_w.astype(x.dtype)
            flat_e = top_i.reshape(-1)
            flat_w = top_w.reshape(-1)
            tok = jnp.arange(T * K) // K
            onehot = jax.nn.one_hot(flat_e, E, dtype=jnp.int32)
            pos = jnp.sum(jnp.cumsum(onehot, axis=0) * onehot, axis=-1) - 1
            valid = pos < C
            loc = flat_e * C + jnp.minimum(pos, C - 1)
            flat_w = jnp.where(valid, flat_w, 0.0)
            safe_loc = jnp.where(valid, loc, E * C)
            xg = jnp.zeros((E * C + 1, d), dtype=x.dtype).at[safe_loc].set(x2[tok])[:E * C]
            xg = xg.reshape(E, C, d)
            h = jax.nn.silu(jnp.einsum('ecd,edf->ecf', xg, w_gate)) * jnp.einsum('ecd,edf->ecf', xg, w_up)
            y = jnp.einsum('ecf,efd->ecd', h, w_down).reshape(E * C, d)
            y_tok = y[loc] * flat_w[:, None]
            out = jnp.zeros((T, d), dtype=x.dtype).at[tok].add(y_tok)
            return out.reshape(b, s, d)
        return _moe(hidden_states, gate_w, w_gate, w_up, w_down)
    x = x + jnp.tanh(g_xattn[0]) * _L0_xattn_ref(ctx_1024, _layernorm(x, axis=-1), L0_xattn_in_proj_w, L0_xattn_conv_w, L0_xattn_conv_b, L0_xattn_x_proj_w, L0_xattn_dt_proj_w, L0_xattn_dt_proj_b, L0_xattn_A_log, L0_xattn_D)
    x = x + jnp.tanh(g_ffn[0]) * _L0_ffn_ref(_layernorm(x, axis=-1), L0_ffn_c_fc, L0_ffn_c_proj)
    x = x + jnp.tanh(g_xattn[1]) * _L1_xattn_ref(_layernorm(x, axis=-1), ctx_1024, mask_BxS2_bf1, L1_xattn_Wq, L1_xattn_Wk, L1_xattn_Wv, L1_xattn_Wo)
    x = x + jnp.tanh(g_ffn[1]) * _L1_ffn_ref(_layernorm(x, axis=-1), L1_ffn_gate_w, L1_ffn_w_gate, L1_ffn_w_up, L1_ffn_w_down)
    return x

_drawn_inputs = setup_inputs


def setup_inputs(seed=0):
    import zlib

    import numpy as np

    out = dict(_drawn_inputs(seed))
    spreads = {'g_ffn': (-1.0, 0.6), 'L0_xattn_D': (1.0, 0.6)}
    factors = {'L0_xattn_in_proj_w': 5.648,
     'L0_xattn_conv_w': 5.892,
     'L0_xattn_conv_b': 8.0,
     'L0_xattn_x_proj_w': 8.0,
     'L0_xattn_dt_proj_w': 8.0,
     'L0_xattn_dt_proj_b': 8.0,
     'L0_xattn_A_log': 8.0,
     'L1_xattn_Wq': 8.0,
     'L1_xattn_Wk': 8.0,
     'L1_ffn_gate_w': 8.0,
     'L1_ffn_w_gate': 8.0,
     'L1_ffn_w_up': 8.0,
     'L1_ffn_w_down': 8.0}
    for name, (base, spread) in spreads.items():
        noise = np.random.default_rng([zlib.crc32(name.encode()), seed]).standard_normal(out[name].shape)
        drawn = base * np.exp(spread * noise) if base else spread * noise
        out[name] = jnp.asarray(drawn.astype(out[name].dtype))
    for name, factor in factors.items():
        out[name] = (out[name] * factor).astype(out[name].dtype)
    return out
```

```python
from contextlib import ExitStack

import concourse.bass as bass
from concourse import mybir

F32 = mybir.dt.float32
BF16 = mybir.dt.bfloat16
U32 = mybir.dt.uint32
U8 = mybir.dt.uint8
ALU = mybir.AluOpType
ACT = mybir.ActivationFunctionType
AX = mybir.AxisListType

P = 128
NB, L, DM = 4, 256, 256
NT = NB * L // P
T = NB * L
DC = 128
ND = 2
NST, NTAP, RANK = 16, 4, 8
NPROJ = RANK + 2 * NST
HID = 1024
NH, NKV, HD = 16, 8, 128
NE, TOPK, CAP, FE = 64, 8, 128, 128
REC = DM + 2 * TOPK + 1
EPS = 1e-5
ROUND = 12582912.0
SLOTW = 3 * DM
NSLOT = 32
PRE = 10
WCOLS = NSLOT * SLOTW
KVCOL = WCOLS - 2 * NKV * T


def wait(eng, sem, value):
    if isinstance(value, int) and value <= 0:
        return
    eng.wait_ge(sem, value)


def run_steps(eng, count, unroll, stages, cuts=()):
    depth = max(lag for lag, _ in stages)

    def straight(steps):
        for s in steps:
            for lag, fn in stages:
                t = s - lag
                if 0 <= t < count:
                    fn(t, t % unroll, t // unroll, t)

    up = lambda n: -(-n // unroll) * unroll
    at = 0
    for end in (*cuts, count):
        head = min(at + up(depth + (unroll if at == 0 else 0)), end)
        straight(range(at, head))
        if head < end:
            with eng.Fori(0, (end - head) // unroll) as i:
                for base in range(head, end, 1)[:unroll]:
                    for lag, fn in stages:
                        r = (base - lag) % unroll
                        fn(i * unroll + (base - lag), r, i + (base - lag - r) // unroll, base - lag)
        at = end
    straight(range(count, count + depth))


def flamingo_kernel(
    nc, x, ctx_tokens, mask, g_xattn, g_ffn, in_proj_w, conv_w, conv_b, x_proj_w, dt_proj_w, dt_proj_b,
    A_log, D_skip, c_fc, c_proj, Wq, Wk, Wv, Wo, gate_w, w_gate, w_up, w_down, out,
):
    stack = ExitStack()
    with stack:
        sem = lambda name: stack.enter_context(nc.semaphore(name))
        sbuf = lambda name, shape, dt=F32: stack.enter_context(nc.sbuf_tensor(name, shape, dt))

        NREC = NE * CAP
        xg_dram = nc.dram_tensor("dispatched", [NREC + T * TOPK, REC], F32, kind="Internal").ap()
        yk_dram = nc.dram_tensor("expert_out", [T * TOPK + NREC, DM], F32, kind="Internal").ap()

        ident = sbuf("ident", [P, P])
        identb = sbuf("identb", [P, P], BF16)
        tri = sbuf("tri", [P, P])
        ones = sbuf("ones", [P, P])
        iota_e = sbuf("iota_e", [P, NE])
        rank1 = sbuf("rank1", [P, TOPK])
        drop_row = sbuf("drop_row", [P, NT * TOPK])
        empty_row = sbuf("empty_row", [P, NE])
        nhalf = sbuf("nhalf", [P, 8])
        gates = sbuf("gates", [P, 4])
        tg = sbuf("tg", [P, 4])
        xres = sbuf("xres", [P, NT, DM])
        gateT = sbuf("gateT", [P, ND, NE])
        weights = sbuf("weights", [P, WCOLS])
        kT = weights[:, KVCOL:KVCOL + NKV * T].rearrange("p (j t) -> p j t", j=NKV)
        vS = weights[:, KVCOL + NKV * T:WCOLS].rearrange("p (s c) -> p s c", s=NT)
        NTMP = 23000
        NTAIL = 2700
        tmp = sbuf("tmp", [P, NTMP])

        def carver(area, size):
            at = [0]

            def take(cols, dt=F32, parts=P):
                n = cols if dt in (F32, U32) else (cols + 1) // 2 if dt == BF16 else (cols + 3) // 4
                a = at[0]
                at[0] += n
                assert at[0] <= size, (at[0], size)
                v = area[0:parts, a:a + n]
                return v if dt == F32 else v.bitcast(dt)

            return take

        v2 = lambda ap, a: ap.rearrange("p (a b) -> p a b", a=a)

        mw = carver(weights, KVCOL)
        mt = carver(tmp, NTMP)
        conv_acc = v2(mw(ND * T), ND)
        dA = conv_acc
        sp_z = v2(mw(ND * T), ND)
        dBu = sp_z
        sp_d = v2(mw(ND * T), ND)
        hst = sp_d
        sp_l = v2(mw(ND * T), ND)
        prod = sp_l
        wk_sb = mt(NKV * HD)
        wv_sb = mt(NKV * HD)
        ctxT = mt(T)
        upad = mt(ND * NB * (L + NTAP - 1)).rearrange("p (e b l) -> p e b l", e=ND, b=NB)
        u = v2(mt(ND * T), ND)
        dt = v2(mt(ND * T), ND)
        dtu = v2(mt(ND * T), ND)
        zs = v2(mt(NT * DM), NT)
        sel = mt(2 * NST * P, BF16)
        bc_stack = mt(T, BF16)
        bc_mid = mt(T, BF16)
        bc_lo = mt(T, BF16)
        xdbl = mt(T)
        xdbl_r = sp_d[:, 0]
        in_n = v2(mt(ND * DC), ND)
        inT = mt(ND * P)
        xp_n = mt(DM)
        xpT = v2(mt(ND * NPROJ), ND)
        dtp_n = v2(mt(ND * RANK), ND)
        dtpT = mt(ND * P)
        gate_n = mt(DM)
        cw = v2(mt(ND * NTAP), ND)
        cb = mt(ND)
        dtb = mt(ND)
        dsk = mt(ND)
        dskm = v2(mt(ND * P), ND)
        alog = v2(mt(ND * NST), ND)
        aneg = v2(mt(ND * NST), ND)
        st6 = v2(mt(NT * 6), NT)
        mv1 = v2(mt(NT * 2), NT)
        rs1 = mt(NT)
        nb1 = mt(NT)
        aexp = v2(mt(ND * NST), ND)
        csb = v2(mt(2 * T), 2)
        ctxn = v2(mt(NT * DC), NT)

        ft = carver(tmp, NTMP - NTAIL)
        wraw = v2(ft(2 * ND * HID), 2)
        wneg = ft(ND * HID, BF16)
        xn = v2(ft(2 * DM), 2)
        xhi = ft(2 * DM, BF16).rearrange("p (r c t) -> p r c t", r=2, c=ND)
        xmid = ft(2 * DM, BF16).rearrange("p (r c t) -> p r c t", r=2, c=ND)
        xlo = ft(2 * DM, BF16).rearrange("p (r c t) -> p r c t", r=2, c=ND)
        xr1 = v2(ft(2 * DM), 2)
        rl = v2(ft(2 * HID), 2)
        sq = v2(ft(2 * HID), 2)
        qf = v2(ft(2 * HID), 2)
        qb = v2(ft(2 * HID, BF16), 2)
        qT = ft(2 * HID, BF16).rearrange("p (r h t) -> p r h t", r=2, h=HID // P)
        w1q = v2(ft(ND * HID, BF16), ND)
        w2q = v2(rl[:, 0].bitcast(BF16), ND)
        w2T = v2(ft(HID // P * DM, BF16), HID // P)
        stf, mvf, rsf, sml, wsc = ft(16), ft(8), ft(4), ft(16), ft(16)
        tail = carver(tmp[:, NTMP - NTAIL:NTMP], NTAIL)
        xT = v2(tail(ND * T), ND)
        xn3 = v2(tail(2 * DM), 2)
        st3, mv3, rs3 = tail(16), tail(8), tail(4)

        ab = carver(tmp, NTMP - NTAIL)
        vbuf = ab(NB * 2 * HD).rearrange("p (b s d) -> p b s d", b=NB, s=2)
        Pn = ab(2 * 512).rearrange("p (r a s) -> p r a s", r=2, a=2)
        qTh = v2(ab(2 * T), 2)
        sm = ab(2 * 512).rearrange("p (r a s) -> p r a s", r=2, a=2)
        pe_ = ab(2 * 512).rearrange("p (r a s) -> p r a s", r=2, a=2)
        pT = ab(2 * 512).rearrange("p (r a s) -> p r a s", r=2, a=2)
        attT = ab(4 * L).rearrange("p (b u t) -> p b u t", b=2, u=2)
        wq_sb = ab(2 * ND * HD).rearrange("p (u c d) -> p u c d", u=2, c=ND)
        wo_sb = v2(ab(2 * DM), 2)
        mx, nm, sume, rc = v2(ab(4), 2), v2(ab(4), 2), v2(ab(4), 2), v2(ab(4), 2)
        mask_sb = ab(NB * L, U8)
        maskb = v2(ab(NB * L), NB)
        valid = ab(NB)

        ra = carver(tmp, NTMP)
        rec = v2(ra(NT * REC), NT)
        xTr = ra(2 * DM).rearrange("p (r c t) -> p r c t", r=2, c=ND)
        rp = v2(ra(2 * NE), 2)
        oh = v2(ra(2 * TOPK * NE), 2)
        ohp = ra(TOPK * NE)
        fl = v2(ra(2 * NE), 2)
        cum = v2(ra(NT * NE), NT)
        idxu = v2(ra(2 * TOPK, U32), 2)
        posk = ra(TOPK)
        locf = ra(TOPK)
        loc2 = ra(TOPK)
        loc = v2(ra(NT * TOPK, U32), NT)
        rsm = ra(32)
        xg = v2(ra(8 * REC), 8)
        xgT = ra(2 * DM).rearrange("p (r c t) -> p r c t", r=2, c=ND)
        sil = v2(ra(2 * FE), 2)
        hh = v2(ra(2 * FE), 2)
        hT = v2(ra(2 * CAP), 2)
        ysb = v2(ra(8 * DM), 8)
        wsl = v2(ra(8), 8)
        msc = v2(ra(8 * 2), 8)
        junk = v2(ra(2 * 16), 2)
        row = v2(ra(8, U32), 8)
        yall = v2(weights[:, 0:4 * TOPK * DM], 4)
        ysum = v2(ra(2 * DM), 2)
        initrec = sbuf("initrec", [P, REC])
        zeros = sbuf("zeros", [P, 1024])

        ps = stack.enter_context(nc.psum_tensor("ps", [P, 8 * 512], F32))
        bank = lambda k, n=1: ps[:, 512 * k:512 * (k + n)]

        ld_ctx, ld_small, ld_x, ld_kv = sem("ld_ctx"), sem("ld_small"), sem("ld_x"), sem("ld_kv")
        ld_vec = sem("ld_vec")
        ld_gates, ld_mask, ld_mlp = sem("ld_gates"), sem("ld_mask"), sem("ld_mlp")
        ld_wq, ld_wo, ld_preA, ld_preB = sem("ld_wq"), sem("ld_wo"), sem("ld_preA"), sem("ld_preB")
        init_done = sem("init_done")
        consts, sel_done = sem("consts"), sem("sel_done")
        tanh_done = sem("tanh_done")
        ctxT_ps, smallT_ps, ctxT_sb, smallT_sb = sem("ctxT_ps"), sem("smallT_ps"), sem("ctxT_sb"), sem("smallT_sb")
        xin_ps, upad_sb, conv_done, u_sb = sem("xin_ps"), sem("upad_sb"), sem("conv_done"), sem("u_sb")
        xdbl_ps, xdbl_sb, split_done, stacked = sem("xdbl_ps"), sem("xdbl_sb"), sem("split_done"), sem("stacked")
        dt_ps, sp_act, dt_done, dtu_done = sem("dt_ps"), sem("sp_act"), sem("dt_done"), sem("dtu_done")
        act_sp = sem("act_sp")
        a_exp, a_neg, dskm_done = sem("a_exp"), sem("a_neg"), sem("dskm_done")
        ln1_stats, ln1_rstd, ln1_nb, zs_done = sem("ln1_stats"), sem("ln1_rstd"), sem("ln1_nb"), sem("zs_done")
        kv_ps, kv_sb = sem("kv_ps"), sem("kv_sb")
        b_rdy, dbu_done, da_rdy, c_rdy, c_sb = sem("b_rdy"), sem("dbu_done"), sem("da_rdy"), sem("c_rdy"), sem("c_sb")
        scan_done, prod_done, prod_used, y_init = sem("scan_done"), sem("prod_done"), sem("prod_used"), sem("y_init")
        yz_done, yT_ps, x1_done = sem("yz_done"), sem("yT_ps"), sem("x1_done")
        dve_chain, pool_chain = sem("dve_chain"), sem("pool_chain")
        wabs_done, wsum_ps, w1_done, w2_done, w2T_ps, w2T_sb = (sem("wabs_done"), sem("wsum_ps"), sem("w1_done"),
                                                                 sem("w2_done"), sem("w2T_ps"), sem("w2T_sb"))
        st_done, rstd_done, xn_done, xT_ps, hi_done, r1_done = (sem("st_done"), sem("rstd_done"), sem("xn_done"),
                                                                sem("xT_ps"), sem("hi_done"), sem("r1_done"))
        mid_done, lo_done, h_ps, relu_done, sq_done, rs_done = (sem("mid_done"), sem("lo_done"), sem("h_ps"),
                                                                sem("relu_done"), sem("sq_done"), sem("rs_done"))
        qf_done, qb_done, qT_ps, qT_sb, o_ps, x2_done = (sem("qf_done"), sem("qb_done"), sem("qT_ps"),
                                                         sem("qT_sb"), sem("o_ps"), sem("x2_done"))
        st3_done, rstd3_done, xn3_done, xT3_ps, xT3_sb = (sem("st3_done"), sem("rstd3_done"), sem("xn3_done"),
                                                          sem("xT3_ps"), sem("xT3_sb"))
        mask_done = sem("mask_done")
        q_ps, q_sb, vb_done = sem("q_ps"), sem("q_sb"), sem("vb_done")
        s_ps, smax_done, nm_done, exp_done, rc_done = (sem("s_ps"), sem("smax_done"), sem("nm_done"),
                                                       sem("exp_done"), sem("rc_done"))
        pn_done, pT_ps, pT_sb, pv_ps, att_sb, ao_ps, x3_done = (sem("pn_done"), sem("pT_ps"), sem("pT_sb"),
                                                                sem("pv_ps"), sem("att_sb"), sem("ao_ps"), sem("x3_done"))
        rc_raw, smax_go = sem("rc_raw"), sem("smax_go")
        st4_done, rstd4_done, rec_done = sem("st4_done"), sem("rstd4_done"), sem("rec_done")
        rT_ps, rT_sb, lg_ps, rmax_done, rexp_done = (sem("rT_ps"), sem("rT_sb"), sem("lg_ps"),
                                                     sem("rmax_done"), sem("rexp_done"))
        fl_done, pos_ps, pos_used, loc_done, dispatched = (sem("fl_done"), sem("pos_ps"), sem("pos_used"),
                                                           sem("loc_done"), sem("dispatched"))
        xg_ld = [sem(f"xg_ld{r}") for r in range(4)]
        w_ld = [sem(f"w_ld{r}") for r in range(4)]
        scattered = [sem(f"scattered{r}") for r in range(4)]
        xgT_ps, xgT_sb, gu_ps, sil_done, h_done = (sem("xgT_ps"), sem("xgT_sb"), sem("gu_ps"), sem("sil_done"),
                                                   sem("h_done"))
        hT_ps, hT_sb, yd_ps, ysb_done = sem("hT_ps"), sem("hT_sb"), sem("yd_ps"), sem("ysb_done")
        msc1, msc2, msc3, row_done = sem("msc1"), sem("msc2"), sem("msc3"), sem("row_done")
        scatter_go = sem("scatter_go")
        yk_ld = [sem(f"yk_ld{r}") for r in range(4)]
        ysum_done, out_done, stored = sem("ysum_done"), sem("out_done"), sem("stored")

        block = stack.enter_context(nc.Block())

        NCONST = 17

        @block.sync
        def _(sp):
            sp.dma_start(ctxn, ctx_tokens.rearrange("b (h p) c -> p (b h) c", p=P)).then_inc(ld_ctx, 16)
            sp.dma_start(in_n, in_proj_w.rearrange("(e p) c -> p e c", p=P)).then_inc(ld_ctx, 16)
            sp.dma_start(xres[:, :, :], x.rearrange("b (h p) d -> p (b h) d", p=P)).then_inc(ld_x, 16)
            sp.dma_start(xp_n[0:NPROJ, :], x_proj_w).then_inc(ld_small, 16)
            sp.dma_start(dtp_n, dt_proj_w.rearrange("(e p) r -> p e r", p=P)).then_inc(ld_small, 16)
            sp.dma_start(gate_n[0:NE, :], gate_w).then_inc(ld_small, 16)
            sp.dma_start(wk_sb, Wk).then_inc(ld_kv, 16)
            sp.dma_start(wv_sb, Wv).then_inc(ld_kv, 16)
            sp.wait_ge(split_done, 3)
            sp.dma_start(bc_stack[NPROJ:2 * NPROJ, :], bc_mid[0:NPROJ, :]).then_inc(stacked, 16)
            sp.dma_start(bc_stack[2 * NPROJ:3 * NPROJ, :], bc_lo[0:NPROJ, :]).then_inc(stacked, 16)
            sp.wait_ge(consts, NCONST)
            sp.wait_ge(pool_chain, 6)
            sp.dma_start(xg_dram[0:NREC, :].rearrange("(e c) f -> c e f", c=CAP),
                         initrec[:, :].unsqueeze(1).to_broadcast([P, NE, REC])).then_inc(init_done, 16)
            ykz = yk_dram[0:T * TOPK, :].rearrange("(p i r) d -> p i (r d)", p=P, r=4)
            sp.dma_start(ykz, zeros[:, :].unsqueeze(1).to_broadcast([P, T * TOPK // P // 4, 4 * DM])
                         ).then_inc(init_done, 16)

            sp.wait_ge(kv_sb, 32)
            sp.wait_ge(conv_done, 2)
            for w, src in enumerate((c_fc, c_proj)):
                sp.dma_start(v2(wraw[:, w], ND), src.rearrange("(c p) h -> p c h", p=P)).then_inc(ld_mlp, 16)

            def load_experts(e, slot, signal):
                dst = weights[:, bass.ds(slot * SLOTW, 2 * SLOTW)]
                gu = dst[:, 0:4 * DM].rearrange("p (w g f) -> p w g f", g=2, f=FE)
                for g, w in enumerate((w_gate, w_up)):
                    sp.dma_start(gu[:, :, g, :], w[bass.ds(e, 2)].rearrange("a (c p) f -> p (a c) f", p=P)
                                 ).then_inc(signal, 16)
                sp.dma_start(v2(dst[:, 4 * DM:], 2), w_down[bass.ds(e, 2)].rearrange("a p f -> p a f")
                             ).then_inc(signal, 16)

            def load_wq(j):
                wqv = Wq.rearrange("(c p) (h d) -> p h c d", p=P, d=HD)
                for n in range(2):
                    src = (wqv[:, 2 * j + n] if isinstance(j, int)
                           else wqv[:, bass.ds(2 * j + n, 1)].rearrange("p a c d -> p (a c) d"))
                    sp.dma_start(wq_sb[:, n], src).then_inc(ld_wq, 16)

            def load_wo(j):
                src = Wo[bass.ds(j * 2 * HD, 2 * HD), :].rearrange("(u d) n -> d u n", d=HD)
                sp.dma_start(wo_sb, src).then_inc(ld_wo, 16)

            sp.wait_ge(x1_done, NB)
            for e in range(0, PRE, 2):
                load_experts(e, e, ld_preA)
            sp.wait_ge(x2_done, NT)
            load_wq(0)
            load_wo(0)
            sp.dma_start(mask_sb, mask.rearrange("b s -> (b s)").partition_broadcast(P)).then_inc(ld_mask, 16)

            def next_wq(t, r, j, low):
                if r == 2:
                    sp.wait_ge(q_ps, 4 * j + 4)
                    load_wq(j + 1)

            def next_wo(t, r, j, low):
                if r == 7:
                    sp.wait_ge(ao_ps, 4 * j + 4)
                    load_wo(j + 1)

            run_steps(sp, 8 * (NKV - 1), 8, [(0, next_wq), (2, next_wo)])
            sp.wait_ge(x3_done, NB * NKV)
            for e in range(PRE, NSLOT, 2):
                load_experts(e, e, ld_preB)
            sp.wait_ge(init_done, 32)
            sp.wait_ge(dispatched, 16 * NT * TOPK)

            def load_xg(t, r, q, low):
                if r % 2:
                    return
                if low >= 8:
                    sp.wait_ge(xgT_ps, t - 6)
                    sp.wait_ge(row_done, t - 6)
                src = xg_dram[bass.ds(t * CAP, 2 * CAP), :].rearrange("(a p) f -> p a f", p=P)
                sp.dma_start(xg[:, r:r + 2, :], src).then_inc(xg_ld[r // 2], 16)

            def load_next(t, r, q, low):
                if low + NSLOT >= NE or r % 2 == 0:
                    return
                sp.wait_ge(yd_ps, t + 1)
                if low >= 8:
                    sp.wait_ge(w_ld[r // 2], 48 * q)
                load_experts(t - 1 + NSLOT, t - 1, w_ld[r // 2])

            run_steps(sp, NE, 8, [(0, load_xg), (8, load_next)], cuts=(NSLOT,))

            sp.wait_ge(yd_ps, NE)
            for r in range(4):
                sp.wait_ge(scattered[r], 16 * (NE // 4))
            for t in range(NT):
                if t >= 4:
                    sp.wait_ge(ysum_done, t - 3)
                sp.dma_start(yall[:, t % 4, :],
                             yk_dram[t * P * TOPK:(t + 1) * P * TOPK, :].rearrange("(p k) d -> p (k d)", k=TOPK)
                             ).then_inc(yk_ld[t % 4], 16)
            for t in range(NT):
                sp.wait_ge(out_done, t + 1)
                b, h = t // 2, t % 2
                sp.dma_start(out[b, h * P:(h + 1) * P, :], xres[:, t, :]).then_inc(stored, 16)
            sp.wait_ge(stored, 16 * NT)

        @block.gpsimd
        def _(pool):
            def unit(out_ap, step):
                return pool.affine_select(out=out_ap, in_=out_ap, compare_op=ALU.not_equal, fill=1.0, base=0,
                                          pattern=[[-1, P]], channel_multiplier=1)

            pool.dma_start(cw, conv_w.rearrange("(e p) a k -> p e (a k)", p=P)).then_inc(ld_vec, 16)
            pool.dma_start(cb, conv_b.rearrange("(e p) -> p e", p=P), allow_slow_non_contiguous=True).then_inc(ld_vec, 16)
            pool.dma_start(dtb, dt_proj_b.rearrange("(e p) -> p e", p=P), allow_slow_non_contiguous=True).then_inc(ld_vec, 16)
            pool.dma_start(dsk, D_skip.rearrange("(e p) -> p e", p=P), allow_slow_non_contiguous=True).then_inc(ld_vec, 16)
            pool.dma_start(alog, A_log.rearrange("(e p) n -> p e n", p=P)).then_inc(ld_vec, 16)
            pool.dma_start(gates[:, 0:2], g_xattn.partition_broadcast(P)).then_inc(ld_gates, 16)
            pool.dma_start(gates[:, 2:4], g_ffn.partition_broadcast(P)).then_inc(ld_gates, 16)

            pool.memset(ident[:, :], 0.0).then_inc(consts, 1)
            pool.memset(identb[:, :], 0.0).then_inc(consts, 1)
            pool.wait_ge(consts, 2)
            unit(ident[:, :], 1).then_inc(consts, 1)
            unit(identb[:, :], 1).then_inc(consts, 1)
            pool.memset(upad[:, :, :, 0:NTAP - 1], 0.0).then_inc(consts, 1)
            pool.memset(nhalf[:, :], -0.5).then_inc(consts, 1)
            pool.wait_ge(ln1_stats, 1)
            pool.wait_ge(consts, 6)
            pool.tensor_scalar(rs1, mv1[:, :, 1], EPS, None, ALU.add).then_inc(pool_chain, 1)
            pool.wait_ge(pool_chain, 1)
            pool.tensor_tensor(rs1, rs1, nhalf[:, :], ALU.pow).then_inc(ln1_rstd, 1)
            selv = sel.rearrange("p (n m) -> p n m", m=P)[0:3 * NPROJ]
            pool.memset(sel.bitcast(F32), 0.0).then_inc(pool_chain, 1)
            for n in range(3):
                pool.wait_ge(pool_chain, 2 + n)
                pool.affine_select(out=selv, in_=selv, compare_op=ALU.not_equal, fill=1.0,
                                   base=-(RANK + n * NPROJ), pattern=[[-1, 2 * NST], [0, P]],
                                   channel_multiplier=1).then_inc(pool_chain, 1)
            pool.wait_ge(pool_chain, 5)
            pool.wait_ge(u_sb, 2)
            for e in range(ND):
                pool.memset(dA[:, e].rearrange("p (b l) -> p b l", b=NB)[:, :, 0:1], 0.0).then_inc(sel_done, 1)
            pool.memset(ones[:, :], 1.0).then_inc(consts, 1)
            pool.memset(tri[:, :], 1.0).then_inc(consts, 1)
            pool.wait_ge(consts, 8)
            pool.affine_select(out=tri[:, :], in_=tri[:, :], compare_op=ALU.is_gt, fill=0.0, base=0,
                               pattern=[[1, P]], channel_multiplier=-1).then_inc(consts, 1)
            io = dict(allow_small_or_imprecise_dtypes=True)
            pool.iota(iota_e[:, :], [[1, NE]], base=0, channel_multiplier=0, **io).then_inc(consts, 1)
            pool.iota(rank1[:, :], [[1, TOPK]], base=1, channel_multiplier=0, **io).then_inc(consts, 1)
            pool.iota(drop_row[:, :], [[P, NT * TOPK]], base=NREC, channel_multiplier=1, **io).then_inc(consts, 1)
            pool.iota(empty_row[:, :], [[CAP, NE]], base=T * TOPK + 1, channel_multiplier=1, **io).then_inc(consts, 1)
            pool.memset(initrec[:, 0:DM], 0.0).then_inc(consts, 1)
            pool.memset(initrec[:, DM:DM + TOPK], -1.0).then_inc(consts, 1)
            pool.memset(initrec[:, DM + TOPK:REC - 1], 0.0).then_inc(consts, 1)
            pool.memset(initrec[:, REC - 1:REC], -1.0).then_inc(consts, 1)
            pool.memset(zeros[:, :], 0.0).then_inc(pool_chain, 1)
            pool.wait_ge(pool_chain, 6)

            def prods(t, r, q, low):
                for e in range(ND):
                    m = 2 * t + e
                    pool.wait_ge(scan_done, m + 1)
                    if e == 0:
                        pool.wait_ge(c_sb, t + 1)
                    wait(pool, prod_used, m - 1 if low > 0 or e > 0 else 0)
                    pool.tensor_tensor(prod[:, e], hst[:, e], csb[:, r], ALU.mult).then_inc(prod_done, 1)

            run_steps(pool, NST, 2, [(0, prods)])

            def rstd(src, dst, stats, tmp_count, signal, t):
                pool.wait_ge(stats, t + 1)
                pool.tensor_scalar(dst, src, EPS, None, ALU.add).then_inc(pool_chain, 1)
                tmp_count[0] += 1
                pool.wait_ge(pool_chain, tmp_count[0])
                pool.tensor_tensor(dst, dst, nhalf[:, 0:1], ALU.pow).then_inc(signal, 1)

            chain = [6]
            for s in range(NT + 6):
                if s < NT:
                    r = s % 2
                    if s >= 2:
                        pool.wait_ge(xn_done, s - 1)
                    rstd(mvf[:, 2 * r + 1:2 * r + 2], rsf[:, r:r + 1], st_done, chain, rstd_done, s)
                if 0 <= s - 2 < NT:
                    t, r = s - 2, (s - 2) % 2
                    pool.wait_ge(relu_done, t + 1)
                    wait(pool, qf_done, t - 1)
                    pool.tensor_tensor(sq[:, r], rl[:, r], rl[:, r], ALU.mult).then_inc(sq_done, 1)
                if 0 <= s - 5 < NT:
                    t, r = s - 5, (s - 5) % 2
                    if t >= 2:
                        pool.wait_ge(xn3_done, t - 1)
                    rstd(mv3[:, 2 * r + 1:2 * r + 2], rs3[:, r:r + 1], st3_done, chain, rstd3_done, t)

            def vcopy(j, b):
                src = (vS[:, 2 * b:2 * b + 2, bass.ds(j * HD, HD)])
                pool.tensor_copy(vbuf[:, b], src).then_inc(vb_done, 1)

            pool.wait_ge(kv_sb, 32)
            pool.wait_ge(x2_done, NT)
            for b in range(NB):
                vcopy(0, b)

            def norm(t, r, j, low):
                r2 = r % 2
                pool.wait_ge(rc_done, t + 1)
                if low >= 2:
                    pool.wait_ge(pT_ps, t - 1)
                pool.tensor_tensor(Pn[:, r2], pe_[:, r2], rc[:, r2].unsqueeze(2).to_broadcast([P, 2, L]),
                                   ALU.mult).then_inc(pn_done, 1)

            def next_v(t, r, j, low):
                if r % 2 == 1 and low < 8 * (NKV - 1):
                    pool.wait_ge(pv_ps, t + 1)
                    vcopy(j + 1, r // 2)

            run_steps(pool, 8 * NKV, 8, [(0, norm), (3, next_v)], cuts=(8 * (NKV - 1),))

            def dispatch(t):
                pool.wait_ge(loc_done, t + 1)
                for k in range(TOPK):
                    pool.indirect_dma_start(xg_dram, bass.IndirectOffsetOnAxis(loc[:, t, k:k + 1], 0), rec[:, t, :],
                                            None).then_inc(dispatched, 16)

            for s in range(NT):
                r = s % 2
                if s == 0:
                    pool.wait_ge(x3_done, NB * NKV)
                    pool.iota(rec[:, :, REC - 1], [[P * TOPK, NT]], base=-1, channel_multiplier=TOPK,
                              **io).then_inc(pool_chain, 1)
                    chain[0] += 1
                if s >= 2:
                    pool.wait_ge(rec_done, s - 1)
                rstd(rsm[:, 4 * r + 1:4 * r + 2], rsm[:, 4 * r + 2:4 * r + 3], st4_done, chain, rstd4_done, s)
                if s == 0:
                    pool.wait_ge(init_done, 32)
                if s >= 1:
                    dispatch(s - 1)
            dispatch(NT - 1)

            def scatter(t, r, q, low):
                if low >= 4:
                    pool.wait_ge(scattered[r % 4], 16 * (2 * q + r // 4))
                pool.wait_ge(ysb_done, t + 1)
                pool.sem_inc(scatter_go, 1)
                pool.indirect_dma_start(yk_dram, bass.IndirectOffsetOnAxis(row[:, r], 0), ysb[:, r, :],
                                        None).then_inc(scattered[r % 4], 16)

            run_steps(pool, NE, 8, [(0, scatter)])

        @block.scalar
        def _(act):
            act.wait_ge(ld_gates, 32)
            act.activation(tg[:, :], gates[:, :], ACT.Tanh).then_inc(tanh_done, 1)
            act.wait_ge(ld_small, 16 * 3)
            act.wait_ge(ld_vec, 16 * 5)
            act.activation(aexp, alog, ACT.Exp).then_inc(a_exp, 1)
            for n in range(2):
                act.wait_ge(ctxT_ps, n + 1)
                act.activation(ctxT[:, 512 * n:512 * n + 512], bank(n), ACT.Copy).then_inc(ctxT_sb, 1)
            act.wait_ge(consts, 5)
            for g in range(4):
                e, h = g // 2, g % 2
                act.wait_ge(xin_ps, g + 1)
                act.activation(upad[:, e, 2 * h:2 * h + 2, NTAP - 1:], v2(bank(4 + g), 2), ACT.Copy).then_inc(upad_sb, 1)

            def kv_evac(g):
                act.wait_ge(kv_ps, g + 1)
                n, h = (g % 16) // 2, g % 2
                dst = kT if g < 16 else vS
                act.activation(dst[:, n, 512 * h:512 * h + 512], bank(2 + g % 2), ACT.Copy).then_inc(kv_sb, 1)

            act.wait_ge(ln1_nb, 1)
            for t in range(NT):
                act.activation(zs[:, t], xres[:, t, :], ACT.Silu, bias=nb1[:, t:t + 1],
                               scale=rs1[:, t:t + 1]).then_inc(zs_done, 1)
            for g in range(6):
                kv_evac(g)
            for e in range(ND):
                act.wait_ge(conv_done, e + 1)
                act.activation(u[:, e], conv_acc[:, e], ACT.Silu).then_inc(u_sb, 1)
                for g in range(6 + 3 * e, 9 + 3 * e):
                    kv_evac(g)
            for h in range(2):
                act.wait_ge(xdbl_ps, h + 1)
                act.activation(xdbl[0:NPROJ, 512 * h:512 * h + 512], bank(h)[0:NPROJ, :],
                               ACT.Copy).then_inc(xdbl_sb, 1)
            n = 0
            for e in range(ND):
                act.wait_ge(dt_ps, 2 * e + 2)
                act.activation(sp_z[:, e], bank(4 + 2 * e, 2), ACT.Abs, bias=dtb[:, e:e + 1]).then_inc(act_sp, 1)
                act.activation(dt[:, e], bank(4 + 2 * e, 2), ACT.Relu, bias=dtb[:, e:e + 1]).then_inc(act_sp, 1)
            for e in range(ND):
                act.wait_ge(act_sp, 2 * e + 2 if e else 4)
                act.activation(sp_z[:, e], sp_z[:, e], ACT.Exp, scale=-1.0).then_inc(act_sp, 1)
                act.wait_ge(act_sp, 5 + 2 * e)
                act.activation(sp_l[:, e], sp_z[:, e], ACT.Ln, bias=1.0).then_inc(act_sp, 1)
            for g in range(12, 32):
                kv_evac(g)
            act.wait_ge(a_neg, 1)
            act.wait_ge(sel_done, 2)
            act.preload_act_table(ACT.Exp)

            def da(t, r, q, low):
                for e in range(ND):
                    m = 2 * t + e
                    wait(act, scan_done, m - 1 if low > 0 or e > 0 else 0)
                    if low == 0:
                        act.wait_ge(dt_done, e + 1)
                    bl = lambda ap: ap.rearrange("p (b l) -> p b l", b=NB)[:, :, 1:]
                    act.activation(bl(dA[:, e]), bl(dt[:, e]), ACT.Exp,
                                   scale=aneg[:, e, bass.ds(t, 1)]).then_inc(da_rdy, 1)

            def ccopy(t, r, q, low):
                act.wait_ge(c_rdy, t + 1)
                wait(act, prod_done, 2 * t - 2 if low > 1 else 0)
                act.activation(csb[:, r], bank(2, 2), ACT.Copy).then_inc(c_sb, 1)

            run_steps(act, NST, 2, [(0, da), (0, ccopy)])

            act.preload_act_table(ACT.Exp)
            for g in range(4):
                act.wait_ge(w2T_ps, g + 1)
                act.activation(w2T[:, 2 * g:2 * g + 2, :].rearrange("p a d -> p (a d)"),
                               bank(6).bitcast(BF16)[:, 0:512], ACT.Copy).then_inc(w2T_sb, 1)
            for s in range(NT + 7):
                t = s - 1
                if 0 <= t < NT:
                    r = t % 2
                    act.wait_ge(xT_ps, t + 1)
                    wait(act, h_ps, t - 1)
                    act.activation(xhi[:, r].rearrange("p c t -> p (c t)"), bank(0)[:, 0:DM], ACT.Copy).then_inc(hi_done, 1)
                t = s - 2
                if 0 <= t < NT:
                    r = t % 2
                    act.wait_ge(h_ps, t + 1)
                    wait(act, rs_done, t - 1)
                    wait(act, sq_done, t - 1)
                    act.activation(rl[:, r], bank(2 + 2 * r, 2), ACT.Relu).then_inc(relu_done, 1)
                t = s - 1
                if 0 <= t < NT:
                    r = t % 2
                    act.wait_ge(r1_done, t + 1)
                    act.activation(xmid[:, r].rearrange("p c t -> p (c t)"), xr1[:, r], ACT.Copy).then_inc(mid_done, 1)
                t = s - 4
                if 0 <= t < NT:
                    r = t % 2
                    act.wait_ge(qT_ps, t + 1)
                    wait(act, o_ps, t - 1)
                    act.activation(qT[:, r].rearrange("p h t -> p (h t)"), bank(6).bitcast(BF16), ACT.Copy).then_inc(qT_sb, 1)
                t = s - 3
                if 0 <= t < NT:
                    r = t % 2
                    act.wait_ge(rs_done, t + 1)
                    act.wait_ge(sq_done, t + 1)
                    wait(act, qb_done, t - 1)
                    act.activation(qf[:, r], sq[:, r], ACT.Identity, bias=wsc[:, 8:9],
                                   scale=sml[:, 8 * r + 3:8 * r + 4]).then_inc(qf_done, 1)
                t = s - 6
                if 0 <= t < NT:
                    act.wait_ge(xT3_ps, t + 1)
                    act.activation(xT[:, :, t * P:(t + 1) * P], v2(bank(1)[:, 0:DM], ND), ACT.Copy).then_inc(xT3_sb, 1)

            def q_evac(n, j, low):
                h, uu = n // 2, n % 2
                act.wait_ge(q_ps, 4 * j + n + 1)
                if low > 0:
                    act.wait_ge(s_ps, 8 * j - 8 + 4 * h + 4)
                act.activation(qTh[:, uu, 512 * h:512 * h + 512], bank(6), ACT.Copy).then_inc(q_sb, 1)

            def exps(t, r, j, low):
                r2 = r % 2
                act.wait_ge(nm_done, t + 1)
                if low >= 2:
                    act.wait_ge(pn_done, t - 1)
                for a in range(2):
                    act.activation(pe_[:, r2, a], sm[:, r2, a], ACT.Exp, bias=nm[:, r2, a:a + 1], scale=HD ** -0.5,
                                   accum_out=sume[:, r2, a:a + 1]).then_inc(exp_done, 1)

            def qs(t, r, j, low):
                if r in (0, 2):
                    q_evac(2 + r // 2, j, low - r)
                elif r in (4, 6) and low < 8 * (NKV - 1):
                    q_evac(r // 2 - 2, j + 1, 8)

            def pv_evac(t, r, j, low):
                b, uu = r // 2, r % 2
                act.wait_ge(pv_ps, t + 1)
                if low >= 4:
                    act.wait_ge(ao_ps, t // 2 - 1 if isinstance(t, int) else 4 * j + b - 1)
                act.activation(attT[:, b % 2, uu], bank(4 + r % 2)[:, 0:L], ACT.Copy).then_inc(att_sb, 1)

            act.preload_act_table(ACT.Exp)
            q_evac(0, 0, 0)
            q_evac(1, 0, 0)
            run_steps(act, 8 * NKV, 8, [(0, exps), (0, qs), (1, pv_evac)], cuts=(8 * (NKV - 1),))

            for s in range(NT + 1):
                t = s
                if t < NT:
                    r = t % 2
                    act.wait_ge(rT_ps, t + 1)
                    wait(act, lg_ps, t - 1)
                    act.activation(xTr[:, r].rearrange("p c t -> p (c t)"), bank(r)[:, 0:DM], ACT.Copy).then_inc(rT_sb, 1)
                t = s
                if t < NT:
                    r = t % 2
                    act.wait_ge(rmax_done, t + 1)
                    act.activation(rp[:, r], bank(2 + r)[:, 0:NE], ACT.Exp, bias=rsm[:, 8 + 4 * r:9 + 4 * r],
                                   accum_out=rsm[:, 9 + 4 * r:10 + 4 * r]).then_inc(rexp_done, 1)

            def xgT_evac(t, r, q, low):
                act.wait_ge(xgT_ps, t + 1)
                if low >= 2:
                    act.wait_ge(gu_ps, t - 1)
                act.activation(xgT[:, r % 2].rearrange("p c t -> p (c t)"), bank(r % 2)[:, 0:DM], ACT.Copy
                               ).then_inc(xgT_sb, 1)

            def silu(t, r, q, low):
                act.wait_ge(gu_ps, t + 1)
                if low >= 2:
                    act.wait_ge(h_done, t - 1)
                act.activation(sil[:, r % 2], bank(2 + r % 2)[:, 0:FE], ACT.Silu).then_inc(sil_done, 1)

            def hT_evac(t, r, q, low):
                act.wait_ge(hT_ps, t + 1)
                if low >= 2:
                    act.wait_ge(yd_ps, t - 1)
                act.activation(hT[:, r % 2], bank(4 + r % 2)[:, 0:CAP], ACT.Copy).then_inc(hT_sb, 1)

            act.preload_act_table(ACT.Silu)
            run_steps(act, NE, 8, [(0, xgT_evac), (1, silu), (2, hT_evac)])

        @block.tensor
        def _(pe):
            mm = lambda o, a, b, s, e, **k: pe.matmul(o, a, b, start=s, stop=e, **k)
            pe.wait_ge(consts, 4)
            pe.wait_ge(ld_ctx, 32)
            for t in range(NT):
                ins = pe.transpose(bank(t // 4)[:, (t % 4) * P:(t % 4 + 1) * P], ctxn[:, t], ident[:, :])
                if t % 4 == 3:
                    ins.then_inc(ctxT_ps, 1)
            for e in range(ND):
                ins = pe.transpose(bank(2)[:, e * P:(e + 1) * P], in_n[:, e], ident[:, :])
            ins.then_inc(smallT_ps, 1)
            pe.wait_ge(ld_small, 16 * 3)
            pe.wait_ge(ld_vec, 16 * 5)
            for e in range(ND):
                pe.transpose(bank(3)[:, e * NPROJ:(e + 1) * NPROJ], xp_n[0:NPROJ, e * P:(e + 1) * P],
                             ident[0:NPROJ, 0:NPROJ])
                pe.transpose(bank(3)[0:RANK, 128 + e * P:128 + (e + 1) * P], dtp_n[:, e], ident[:, :])
                ins = pe.transpose(bank(3)[:, 384 + e * NE:384 + (e + 1) * NE], gate_n[0:NE, e * P:(e + 1) * P],
                                   ident[0:NE, 0:NE])
            ins.then_inc(smallT_ps, 1)
            pe.wait_ge(ctxT_sb, 2)
            pe.wait_ge(smallT_sb, 1)
            for g in range(4):
                e, h = g // 2, g % 2
                mm(bank(4 + g), inT[:, e * P:(e + 1) * P], ctxT[:, 512 * h:512 * h + 512], True, True).then_inc(xin_ps, 1)

            def kv(g):
                if g == 0:
                    pe.wait_ge(ld_kv, 32)
                if g < 2:
                    pe.wait_ge(smallT_sb, 2)
                else:
                    pe.wait_ge(kv_sb, g - 1)
                n, h = (g % 16) // 2, g % 2
                if g < 16:
                    a, b = wk_sb[:, n * HD:(n + 1) * HD], ctxT[:, 512 * h:512 * h + 512]
                else:
                    a, b = ctxT[:, n * P:(n + 1) * P], wv_sb[:, 512 * h:512 * h + 512]
                mm(bank(2 + g % 2), a, b, True, True).then_inc(kv_ps, 1)

            for g in range(12):
                kv(g)
            pe.wait_ge(u_sb, 2)
            for h in range(2):
                for e in range(ND):
                    ins = mm(bank(h)[0:NPROJ, :], xpT[:, e], u[:, e, 512 * h:512 * h + 512], e == 0, e == 1)
                ins.then_inc(xdbl_ps, 1)
            pe.wait_ge(upad_sb, 4)
            pe.wait_ge(xdbl_sb, 2)
            for g in range(4):
                e, h = g // 2, g % 2
                mm(bank(4 + g), dtpT[0:RANK, e * P:(e + 1) * P], xdbl[0:RANK, 512 * h:512 * h + 512], True, True
                   ).then_inc(dt_ps, 1)
            for g in range(12, 32):
                kv(g)
            pe.wait_ge(dskm_done, 1)
            pe.wait_ge(act_sp, 4)
            for g in range(4):
                e, h = g // 2, g % 2
                mm(bank(4 + g), dskm[:, e], u[:, e, 512 * h:512 * h + 512], True, False, skip_group_check=True)
            pe.wait_ge(stacked, 32)
            pe.wait_ge(kv_sb, 32)
            pe.wait_ge(pool_chain, 5)

            def bc(t, r, q, low):
                if low > 0:
                    pe.wait_ge(dbu_done, 2 * t)
                for h in range(2):
                    ins = mm(bank(h), sel[0:3 * NPROJ, bass.ds(t * P, P)],
                             bc_stack[0:3 * NPROJ, 512 * h:512 * h + 512], True, True)
                ins.then_inc(b_rdy, 1)
                if low > 0:
                    pe.wait_ge(c_sb, t)
                for h in range(2):
                    ins = mm(bank(2 + h), sel[0:3 * NPROJ, bass.ds(t * P + NST * P, P)],
                             bc_stack[0:3 * NPROJ, 512 * h:512 * h + 512], True, True)
                ins.then_inc(c_rdy, 1)

            def y_add(t, r, q, low):
                for e in range(ND):
                    pe.wait_ge(prod_done, 2 * t + e + 1)
                    for h in range(2):
                        ins = mm(bank(4 + 2 * e + h), ident[:, :], prod[:, e, 512 * h:512 * h + 512], False,
                                 low == NST - 1,
                                 skip_group_check=True)
                    ins.then_inc(prod_used, 1)

            run_steps(pe, NST, 2, [(0, bc), (1, y_add)])
            pe.wait_ge(dbu_done, 2 * NST)
            pe.wait_ge(c_sb, NST)
            pe.wait_ge(yz_done, 2)
            for b in range(NB):
                for h in range(2):
                    for e in range(ND):
                        ins = pe.transpose(bank(b)[:, h * DM + e * P:h * DM + (e + 1) * P],
                                           dtu[:, e, b * L + h * P:b * L + (h + 1) * P], ident[:, :])
                ins.then_inc(yT_ps, 1)
            pe.wait_ge(wabs_done, 1)
            mm(bank(7)[:, 0:2], ones[:, :], wsc[:, 0:2], True, True).then_inc(wsum_ps, 1)
            pe.wait_ge(w2_done, 1)
            for g in range(4):
                wait(pe, w2T_sb, g)
                for n in range(2):
                    for c in range(ND):
                        h = 2 * g + n
                        ins = pe.transpose(bank(6).bitcast(BF16)[:, n * DM + c * P:n * DM + (c + 1) * P],
                                           w2q[:, c, h * P:(h + 1) * P], identb[:, :])
                ins.then_inc(w2T_ps, 1)
            pe.wait_ge(w1_done, 1)
            pe.wait_ge(w2T_sb, 4)
            pe.wait_ge(x1_done, NB)
            for s in range(NT + 7):
                t = s - 1
                if 0 <= t < NT:
                    r = t % 2
                    pe.wait_ge(xn_done, t + 1)
                    wait(pe, r1_done, t)
                    for c in range(ND):
                        ins = pe.transpose(bank(0)[:, c * P:(c + 1) * P], xn[:, r, c * P:(c + 1) * P], ident[:, :])
                    ins.then_inc(xT_ps, 1)
                t = s - 2
                if 0 <= t < NT:
                    r = t % 2
                    pe.wait_ge(lo_done, t + 1)
                    wait(pe, relu_done, t - 1)
                    for h in range(2):
                        n = 0
                        for part in (xhi, xmid, xlo):
                            for c in range(ND):
                                ins = mm(bank(2 + 2 * r + h), part[:, r, c], w1q[:, c, 512 * h:512 * h + 512],
                                         n == 0, n == 5)
                                n += 1
                    ins.then_inc(h_ps, 1)
                t = s - 4
                if 0 <= t < NT:
                    r = t % 2
                    pe.wait_ge(qb_done, t + 1)
                    wait(pe, qT_sb, t)
                    for h in range(HID // P):
                        ins = pe.transpose(bank(6).bitcast(BF16)[:, h * P:(h + 1) * P], qb[:, r, h * P:(h + 1) * P],
                                           identb[:, :])
                    ins.then_inc(qT_ps, 1)
                    pe.wait_ge(qT_sb, t + 1)
                    wait(pe, x2_done, t)
                    for h in range(HID // P):
                        ins = mm(bank(7)[:, 0:DM], qT[:, r, h], w2T[:, h], h == 0, h == HID // P - 1)
                    ins.then_inc(o_ps, 1)
                t = s - 6
                if 0 <= t < NT:
                    r = t % 2
                    pe.wait_ge(xn3_done, t + 1)
                    wait(pe, xT3_sb, t)
                    for c in range(ND):
                        ins = pe.transpose(bank(1)[:, c * P:(c + 1) * P], xn3[:, r, c * P:(c + 1) * P], ident[:, :])
                    ins.then_inc(xT3_ps, 1)

            def q_proj(n, j, low):
                h, uu = n // 2, n % 2
                pe.wait_ge(ld_wq, 32 * (j + 1))
                if low > 0 or n > 0:
                    pe.wait_ge(q_sb, 4 * j + n)
                for c in range(ND):
                    ins = mm(bank(6), wq_sb[:, uu, c], xT[:, c, 512 * h:512 * h + 512], c == 0, c == 1)
                ins.then_inc(q_ps, 1)

            def scores(t, r, j, low):
                b, uu = r // 2, r % 2
                pe.wait_ge(q_sb, 4 * j + 2 * (b // 2) + uu + 1)
                if low >= 2:
                    pe.wait_ge(smax_done, 2 * t - 2)
                for a in range(2):
                    ins = mm(bank(r % 2)[:, a * L:(a + 1) * L], qTh[:, uu, b * L + a * P:b * L + (a + 1) * P],
                             kT[:, j, b * L:(b + 1) * L] if isinstance(j, int)
                             else kT[:, bass.ds(j, 1), b * L:(b + 1) * L].rearrange("p a s -> p (a s)"), True, True)
                ins.then_inc(s_ps, 1)

            def p_turn(t, r, j, low):
                pe.wait_ge(pn_done, t + 1)
                if low >= 2:
                    pe.wait_ge(pT_sb, t - 1)
                for a in range(2):
                    for c in range(2):
                        ins = pe.transpose(bank(2 + r % 2)[:, c * L + a * P:c * L + (a + 1) * P],
                                           Pn[:, r % 2, a, c * P:(c + 1) * P], ident[:, :])
                ins.then_inc(pT_ps, 1)

            def q_groups(t, r, j, low):
                if r in (0, 2):
                    q_proj(2 + r // 2, j, 1)
                elif r in (4, 6) and low < 8 * (NKV - 1):
                    q_proj(r // 2 - 2, j + 1, 1)

            def pv(t, r, j, low):
                b = r // 2
                pe.wait_ge(pT_sb, t + 1)
                pe.wait_ge(vb_done, 4 * j + b + 1)
                if low >= 2:
                    pe.wait_ge(att_sb, t - 1)
                for c in range(2):
                    ins = mm(bank(4 + r % 2)[:, 0:L], vbuf[:, b, c], pT[:, r % 2, c], c == 0, c == 1)
                ins.then_inc(pv_ps, 1)

            def att_out(t, r, j, low):
                if r % 2 == 0:
                    return
                b = r // 2
                pe.wait_ge(ld_wo, 16 * (j + 1))
                pe.wait_ge(att_sb, t + 1)
                if low > 1:
                    pe.wait_ge(x3_done, 4 * j + b)
                for a in range(2):
                    for uu in range(2):
                        ins = mm(bank(7)[:, a * DM:(a + 1) * DM], attT[:, b % 2, uu, a * P:(a + 1) * P], wo_sb[:, uu],
                                 uu == 0, uu == 1)
                ins.then_inc(ao_ps, 1)

            pe.wait_ge(xT3_sb, NT)
            q_proj(0, 0, 0)
            q_proj(1, 0, 1)
            run_steps(pe, 8 * NKV, 8, [(0, scores), (1, p_turn), (0, q_groups), (2, att_out), (1, pv)],
                      cuts=(8 * (NKV - 1),))

            for t in range(NT + 1):
                if t < NT:
                    r = t % 2
                    pe.wait_ge(rec_done, t + 1)
                    wait(pe, rT_sb, t - 1)
                    for c in range(ND):
                        ins = pe.transpose(bank(r)[:, c * P:(c + 1) * P], rec[:, t, c * P:(c + 1) * P], ident[:, :])
                    ins.then_inc(rT_ps, 1)
                    pe.wait_ge(rT_sb, t + 1)
                    wait(pe, rexp_done, t - 1)
                    for c in range(ND):
                        ins = mm(bank(2 + r)[:, 0:NE], xTr[:, r, c], gateT[:, c], c == 0, c == 1)
                    ins.then_inc(lg_ps, 1)
                if t >= 1:
                    k = t - 1
                    r = k % 2
                    pe.wait_ge(fl_done, k + 1)
                    wait(pe, pos_used, k - 1)
                    mm(bank(4 + r)[:, 0:NE], tri[:, :], fl[:, r], True, False)
                    mm(bank(4 + r)[:, 0:NE], ones[:, :], cum[:, k], False, True).then_inc(pos_ps, 1)

            def xg_turn(t, r, q, low):
                pe.wait_ge(xg_ld[r // 2], 16 * (q + 1))
                if low >= 2:
                    pe.wait_ge(xgT_sb, t - 1)
                for c in range(ND):
                    ins = pe.transpose(bank(r % 2)[:, c * P:(c + 1) * P], xg[:, r, c * P:(c + 1) * P], ident[:, :])
                ins.then_inc(xgT_ps, 1)

            def pair_at(t, r, low):
                return (t - r % 2 - (NSLOT if low >= NSLOT else 0)) * SLOTW

            def gate_up(t, r, q, low):
                if low >= NSLOT:
                    pe.wait_ge(w_ld[r // 2], 48 * (q - NSLOT // 8 + 1))
                pe.wait_ge(xgT_sb, t + 1)
                if low >= 2:
                    pe.wait_ge(h_done, t - 1)
                at = pair_at(t, r, low) + r % 2 * 2 * DM
                for c in range(ND):
                    ins = mm(bank(2 + r % 2)[:, 0:2 * FE], xgT[:, r % 2, c],
                             weights[:, bass.ds(at + c * 2 * FE, 2 * FE)], c == 0, c == 1)
                ins.then_inc(gu_ps, 1)

            def h_turn(t, r, q, low):
                pe.wait_ge(h_done, t + 1)
                if low >= 2:
                    pe.wait_ge(hT_sb, t - 1)
                pe.transpose(bank(4 + r % 2)[:, 0:CAP], hh[:, r % 2], ident[:, :]).then_inc(hT_ps, 1)

            def down(t, r, q, low):
                pe.wait_ge(hT_sb, t + 1)
                if low >= 2:
                    pe.wait_ge(ysb_done, t - 1)
                mm(bank(6 + r % 2)[:, 0:DM], hT[:, r % 2],
                   weights[:, bass.ds(pair_at(t, r, low) + 4 * DM + r % 2 * DM, DM)], True, True).then_inc(yd_ps, 1)

            pe.wait_ge(pos_used, NT)
            pe.wait_ge(ld_preA, 24 * PRE)
            pe.wait_ge(ld_preB, 24 * (NSLOT - PRE))
            run_steps(pe, NE, 8, [(0, xg_turn), (1, gate_up), (2, h_turn), (3, down)], cuts=(NSLOT,))

        @block.vector
        def _(dve):
            chain = [0]

            def link(ins):
                chain[0] += 1
                ins.then_inc(dve_chain, 1)
                dve.wait_ge(dve_chain, chain[0])

            dve.wait_ge(ld_x, 16)
            for t in range(NT):
                ins = dve.bn_stats(st6[:, t], xres[:, t, :])
            link(ins)
            for t in range(NT):
                ins = dve.bn_aggr(mv1[:, t], st6[:, t])
            ins.then_inc(ln1_stats, 1)
            dve.wait_ge(smallT_ps, 1)
            dve.tensor_copy(inT, bank(2)[:, 0:ND * P]).then_inc(smallT_sb, 1)
            dve.wait_ge(smallT_ps, 2)
            dve.tensor_copy(xpT.rearrange("p e k -> p (e k)"), bank(3)[:, 0:ND * NPROJ])
            dve.tensor_copy(dtpT[0:RANK, :], bank(3)[0:RANK, 128:384])
            dve.tensor_copy(gateT[:, :, :].rearrange("p e k -> p (e k)"), bank(3)[:, 384:384 + ND * NE]
                            ).then_inc(smallT_sb, 1)
            dve.wait_ge(ln1_rstd, 1)
            dve.scalar_tensor_tensor(out=nb1, in0=mv1[:, :, 0], scalar=-1.0, in1=rs1, op0=ALU.mult,
                                     op1=ALU.mult).then_inc(ln1_nb, 1)
            tap = lambda e, j: upad[:, e, :, j:j + L]
            cav = lambda e: conv_acc[:, e].rearrange("p (b l) -> p b l", b=NB)
            dve.wait_ge(ld_small, 16 * 3)
            dve.wait_ge(ld_vec, 16 * 5)
            dve.wait_ge(consts, 6)
            for e in range(ND):
                dve.wait_ge(upad_sb, 2 * e + 2)
                link(dve.tensor_scalar(cav(e), tap(e, NTAP - 1), cw[:, e, NTAP - 1:NTAP], cb[:, e:e + 1], ALU.mult,
                                       ALU.add))
                for j in range(NTAP - 1):
                    ins = dve.scalar_tensor_tensor(out=cav(e), in0=tap(e, j), scalar=cw[:, e, j:j + 1], in1=cav(e),
                                                   op0=ALU.mult, op1=ALU.add)
                    if j < NTAP - 2:
                        link(ins)
                ins.then_inc(conv_done, 1)
            dve.wait_ge(a_exp, 1)
            dve.tensor_scalar(aneg, aexp, -1.0, None, ALU.mult).then_inc(a_neg, 1)
            for e in range(ND):
                ins = dve.tensor_scalar(dskm[:, e], ident[:, :], dsk[:, e:e + 1], None, ALU.mult)
            ins.then_inc(dskm_done, 1)
            dve.wait_ge(xdbl_sb, 2)
            n = slice(0, NPROJ)
            dve.tensor_copy(bc_stack[n, :], xdbl[n, :]).then_inc(split_done, 1)
            dve.wait_ge(split_done, 1)
            link(dve.tensor_tensor(xdbl_r[n, :], xdbl[n, :], bc_stack[n, :], ALU.subtract))
            dve.tensor_copy(bc_mid[n, :], xdbl_r[n, :]).then_inc(split_done, 1)
            dve.wait_ge(split_done, 2)
            dve.tensor_tensor(bc_lo[n, :], xdbl_r[n, :], bc_mid[n, :], ALU.subtract).then_inc(split_done, 1)
            dve.wait_ge(split_done, 3)
            for e in range(ND):
                dve.wait_ge(act_sp, 5 + 2 * e)
                link(dve.tensor_scalar(sp_d[:, e], sp_z[:, e], 1.0, -1.0, ALU.add, ALU.add))
                link(dve.tensor_tensor(sp_d[:, e], sp_z[:, e], sp_d[:, e], ALU.subtract))
                dve.wait_ge(act_sp, 6 + 2 * e)
                link(dve.tensor_tensor(sp_d[:, e], sp_d[:, e], sp_l[:, e], ALU.add))
                dve.tensor_tensor(dt[:, e], dt[:, e], sp_d[:, e], ALU.add).then_inc(dt_done, 1)
                dve.wait_ge(dt_done, e + 1)
                link(dve.tensor_tensor(dtu[:, e], dt[:, e], u[:, e], ALU.mult))

            def dbu(t, r, q, low):
                dve.wait_ge(b_rdy, t + 1)
                for e in range(ND):
                    wait(dve, scan_done, 2 * t + e - 1 if low > 0 else 0)
                    dve.tensor_tensor(dBu[:, e], dtu[:, e], bank(0, 2), ALU.mult).then_inc(dbu_done, 1)

            def scan(t, r, q, low):
                for e in range(ND):
                    dve.wait_ge(dbu_done, 2 * t + e + 1)
                    dve.wait_ge(da_rdy, 2 * t + e + 1)
                    wait(dve, prod_done, 2 * t + e - 1 if low > 0 else 0)
                    dve.tensor_tensor_scan(hst[:, e], dA[:, e], dBu[:, e], 0.0, ALU.mult, ALU.add).then_inc(scan_done, 1)

            run_steps(dve, NST, 2, [(0, dbu), (0, scan)])
            dve.wait_ge(zs_done, NT)
            for e in range(ND):
                dve.wait_ge(prod_used, 2 * NST - 1 + e)
                dve.tensor_tensor(v2(dtu[:, e], NB), v2(bank(4 + 2 * e, 2), NB), zs[:, e:NT:2, :], ALU.mult
                                  ).then_inc(yz_done, 1)
            dve.wait_ge(ld_mlp, 32)
            for w in range(2):
                ins = dve.tensor_reduce(wsc[:, w:w + 1], wraw[:, w], AX.X, ALU.add, apply_absolute_value=True)
            ins.then_inc(wabs_done, 1)
            dve.wait_ge(tanh_done, 1)
            for b in range(NB):
                dve.wait_ge(yT_ps, b + 1)
                xv = xres[:, 2 * b:2 * b + 2, :].rearrange("p a d -> p (a d)")
                dve.scalar_tensor_tensor(out=xv, in0=bank(b), scalar=tg[:, 0:1], in1=xv, op0=ALU.mult,
                                         op1=ALU.add).then_inc(x1_done, 1)
            dve.wait_ge(wsum_ps, 1)
            link(dve.tensor_scalar(wsc[:, 2:4], bank(7)[:, 0:2], 1.0 / (DM * HID), EPS, ALU.mult, ALU.max))
            link(dve.reciprocal(wsc[:, 4:6], wsc[:, 2:4]))
            link(dve.tensor_tensor(wsc[:, 9:10], wsc[:, 2:3], wsc[:, 2:3], ALU.mult))
            link(dve.tensor_scalar(wsc[:, 6:7], wsc[:, 9:10], 255.0, None, ALU.mult))
            link(dve.tensor_tensor(wsc[:, 10:11], wsc[:, 3:4], tg[:, 2:3], ALU.mult))
            link(dve.tensor_scalar(wsc[:, 7:8], wsc[:, 10:11], 1.0 / 255.0, None, ALU.mult))
            link(dve.memset(wsc[:, 8:9], ROUND))
            for w, dst, signal in ((1, w2q, w2_done), (0, w1q, w1_done)):
                link(dve.tensor_scalar(wraw[:, w], wraw[:, w], wsc[:, 4 + w:5 + w], None, ALU.mult))
                link(dve.tensor_scalar(wneg, wraw[:, w], -0.5, None, ALU.is_lt))
                dve.scalar_tensor_tensor(out=dst.rearrange("p c h -> p (c h)"), in0=wraw[:, w], scalar=0.5,
                                         in1=wneg, op0=ALU.is_gt, op1=ALU.subtract).then_inc(signal, 1)
            dve.wait_ge(w1_done, 1)

            for s in range(NT + 7):
                t = s - 1
                if 0 <= t < NT:
                    r = t % 2
                    dve.wait_ge(rstd_done, t + 1)
                    wait(dve, xT_ps, t - 1)
                    dve.tensor_scalar(xn[:, r], xres[:, t, :], mvf[:, 2 * r:2 * r + 1], rsf[:, r:r + 1], ALU.subtract,
                                      ALU.mult).then_inc(xn_done, 1)
                t = s
                if t < NT:
                    r = t % 2
                    link(dve.bn_stats(stf[:, 8 * r:8 * r + 6], xres[:, t, :]))
                    wait(dve, xn_done, t - 1)
                    dve.bn_aggr(mvf[:, 2 * r:2 * r + 2], stf[:, 8 * r:8 * r + 6]).then_inc(st_done, 1)
                t = s - 1
                if 0 <= t < NT:
                    r = t % 2
                    dve.wait_ge(hi_done, t + 1)
                    wait(dve, mid_done, t - 1)
                    dve.tensor_tensor(xr1[:, r], bank(0)[:, 0:DM], xhi[:, r].rearrange("p c t -> p (c t)"),
                                      ALU.subtract).then_inc(r1_done, 1)
                t = s - 3
                if 0 <= t < NT:
                    r = t % 2
                    v = lambda k: sml[:, 8 * r + k:8 * r + k + 1]
                    dve.wait_ge(relu_done, t + 1)
                    wait(dve, qf_done, t - 1)
                    link(dve.tensor_reduce(v(0), rl[:, r], AX.X, ALU.max))
                    link(dve.tensor_tensor(v(1), v(0), v(0), ALU.mult))
                    link(dve.tensor_scalar(v(1), v(1), wsc[:, 9:10], EPS, ALU.mult, ALU.max))
                    link(dve.reciprocal(v(2), v(1)))
                    wait(dve, x2_done, t - 1)
                    dve.tensor_scalar(v(4), v(1), wsc[:, 7:8], None, ALU.mult)
                    dve.tensor_scalar(v(3), v(2), wsc[:, 6:7], None, ALU.mult).then_inc(rs_done, 1)
                t = s - 1
                if 0 <= t < NT:
                    r = t % 2
                    dve.wait_ge(mid_done, t + 1)
                    wait(dve, h_ps, t - 1)
                    dve.tensor_tensor(xlo[:, r].rearrange("p c t -> p (c t)"), xr1[:, r],
                                      xmid[:, r].rearrange("p c t -> p (c t)"), ALU.subtract).then_inc(lo_done, 1)
                t = s - 3
                if 0 <= t < NT:
                    r = t % 2
                    dve.wait_ge(qf_done, t + 1)
                    wait(dve, qT_ps, t - 1)
                    dve.tensor_scalar(qb[:, r], qf[:, r], -ROUND, None, ALU.add).then_inc(qb_done, 1)
                t = s - 4
                if 0 <= t < NT:
                    r = t % 2
                    dve.wait_ge(o_ps, t + 1)
                    dve.scalar_tensor_tensor(out=xres[:, t, :], in0=bank(7)[:, 0:DM], scalar=sml[:, 8 * r + 4:8 * r + 5],
                                             in1=xres[:, t, :], op0=ALU.mult, op1=ALU.add).then_inc(x2_done, 1)
                t = s - 5
                if 0 <= t < NT:
                    r = t % 2
                    dve.wait_ge(x2_done, t + 1)
                    link(dve.bn_stats(st3[:, 8 * r:8 * r + 6], xres[:, t, :]))
                    dve.bn_aggr(mv3[:, 2 * r:2 * r + 2], st3[:, 8 * r:8 * r + 6]).then_inc(st3_done, 1)
                    dve.wait_ge(rstd3_done, t + 1)
                    wait(dve, xT3_ps, t - 1)
                    dve.tensor_scalar(xn3[:, r], xres[:, t, :], mv3[:, 2 * r:2 * r + 1], rs3[:, r:r + 1],
                                      ALU.subtract, ALU.mult).then_inc(xn3_done, 1)

            dve.wait_ge(ld_mask, 16)
            link(dve.tensor_scalar(maskb.rearrange("p b s -> p (b s)"), mask_sb, -1.0, 1e30, ALU.add, ALU.mult))
            link(dve.tensor_reduce(valid, maskb, AX.X, ALU.max))
            link(dve.tensor_scalar(valid, valid, -1.0, None, ALU.is_gt))

            def smax(t, r, j, low):
                b, r2 = r // 2, r % 2
                dve.wait_ge(s_ps, t + 1)
                if low >= 2:
                    dve.wait_ge(exp_done, 2 * t - 2)
                dve.sem_inc(smax_go, 1)
                for a in range(2):
                    dve.tensor_tensor_reduce(sm[:, r2, a], bank(r2)[:, a * L:(a + 1) * L], maskb[:, b], 1.0, -3e38,
                                             ALU.add, ALU.max, mx[:, r2, a:a + 1]).then_inc(smax_done, 1)
                dve.wait_ge(smax_done, 2 * t + 2)
                dve.tensor_scalar(nm[:, r2], mx[:, r2], -(HD ** -0.5), None, ALU.mult).then_inc(nm_done, 1)

            def pT_evac(t, r, j, low):
                dve.wait_ge(pT_ps, t + 1)
                if low >= 2:
                    dve.wait_ge(pv_ps, t - 1)
                dve.tensor_copy(pT[:, r % 2].rearrange("p a s -> p (a s)"), bank(2 + r % 2)).then_inc(pT_sb, 1)

            def recips(t, r, j, low):
                b, r2 = r // 2, r % 2
                dve.wait_ge(exp_done, 2 * t + 2)
                if low >= 2:
                    dve.wait_ge(pn_done, t - 1)
                dve.reciprocal(rc[:, r2], sume[:, r2]).then_inc(rc_raw, 1)
                dve.wait_ge(rc_raw, t + 1)
                dve.tensor_scalar(rc[:, r2], rc[:, r2], valid[:, b:b + 1], None, ALU.mult).then_inc(rc_done, 1)

            def x3(t, r, j, low):
                if r % 2 == 0:
                    return
                b = r // 2
                dve.wait_ge(ao_ps, 4 * j + b + 1)
                if low >= 8:
                    dve.wait_ge(x3_done, 4 * j + b - 3)
                xv = xres[:, 2 * b:2 * b + 2, :].rearrange("p a d -> p (a d)")
                dve.scalar_tensor_tensor(out=xv, in0=bank(7), scalar=tg[:, 1:2], in1=xv, op0=ALU.mult,
                                         op1=ALU.add).then_inc(x3_done, 1)

            run_steps(dve, 8 * NKV, 8, [(0, smax), (1, pT_evac), (0, recips), (2, x3)], cuts=(8 * (NKV - 1),))

            dve.wait_ge(x3_done, NB * NKV)
            link(dve.memset(cum[:, 0], 0.0))
            dve.wait_ge(consts, NCONST)
            for s in range(NT + 1):
                t = s
                if t < NT:
                    r = t % 2
                    v = lambda k: rsm[:, 4 * r + k:4 * r + k + 1]
                    st = locf[:, 0:6]
                    link(dve.bn_stats(rsm[:, 16 + 8 * r:22 + 8 * r], xres[:, t, :]))
                    dve.bn_aggr(rsm[:, 4 * r:4 * r + 2], rsm[:, 16 + 8 * r:22 + 8 * r]).then_inc(st4_done, 1)
                    dve.wait_ge(rstd4_done, t + 1)
                    dve.tensor_scalar(rec[:, t, 0:DM], xres[:, t, :], v(0), v(2), ALU.subtract, ALU.mult
                                      ).then_inc(rec_done, 1)
                if t >= 1:
                    k, rk = t - 1, (t - 1) % 2
                    dve.wait_ge(pos_ps, k + 1)
                    dve.tensor_tensor(v2(ohp, TOPK), v2(oh[:, rk], TOPK),
                                      bank(4 + rk)[:, 0:NE].unsqueeze(1).to_broadcast([P, TOPK, NE]), ALU.mult
                                      ).then_inc(pos_used, 1)
                    dve.wait_ge(pos_used, k + 1)
                    drop = drop_row[:, k * TOPK:(k + 1) * TOPK]
                    link(dve.tensor_reduce(posk, v2(ohp, TOPK), AX.X, ALU.add))
                    link(dve.scalar_tensor_tensor(out=locf, in0=rec[:, k, DM:DM + TOPK], scalar=float(CAP), in1=posk,
                                                  op0=ALU.mult, op1=ALU.add))
                    link(dve.tensor_tensor(loc2, locf, drop, ALU.subtract))
                    link(dve.scalar_tensor_tensor(out=locf, in0=posk, scalar=float(CAP), in1=loc2, op0=ALU.is_lt,
                                                  op1=ALU.mult))
                    dve.tensor_tensor(loc[:, k], locf, drop, ALU.add).then_inc(loc_done, 1)
                if t < NT:
                    r = t % 2
                    w = lambda k: rsm[:, 8 + 4 * r + k:9 + 4 * r + k]
                    dve.wait_ge(lg_ps, t + 1)
                    dve.tensor_reduce(w(0), bank(2 + r)[:, 0:NE], AX.X, ALU.max, negate=True).then_inc(rmax_done, 1)
                    dve.wait_ge(rexp_done, t + 1)
                    link(dve.reciprocal(w(2), w(1)))
                    link(dve.tensor_scalar(rp[:, r], rp[:, r], w(2), None, ALU.mult))
                    top_w = rec[:, t, DM + TOPK:DM + 2 * TOPK]
                    top_i = rec[:, t, DM:DM + TOPK]
                    link(dve.max(top_w, rp[:, r]))
                    link(dve.max_index(idxu[:, r], top_w, rp[:, r]))
                    link(dve.tensor_copy(top_i, idxu[:, r]))
                    ohv = v2(oh[:, r], TOPK)
                    link(dve.tensor_tensor(ohv, iota_e[:, :].unsqueeze(1).to_broadcast([P, TOPK, NE]),
                                           top_i.unsqueeze(2).to_broadcast([P, TOPK, NE]), ALU.is_equal))
                    dve.tensor_reduce(fl[:, r], oh[:, r].rearrange("p (k e) -> p e k", k=TOPK), AX.X, ALU.add
                                      ).then_inc(fl_done, 1)
                    dve.wait_ge(fl_done, t + 1)
                    if t + 1 < NT:
                        link(dve.tensor_tensor(cum[:, t + 1], cum[:, t], fl[:, r], ALU.add))

            def rows(t, r, q, low):
                ru = r % 2
                top_i, top_w = xg[:, r, DM:DM + TOPK], xg[:, r, DM + TOPK:DM + 2 * TOPK]
                me = iota_e[:, bass.ds(t, 1)]
                dve.wait_ge(xg_ld[r // 2], 16 * (q + 1))
                if low >= 8:
                    dve.wait_ge(scattered[r % 4], 16 * (2 * q + r // 4 - 1))
                    dve.wait_ge(ysb_done, t - 7)
                if low >= 2:
                    dve.wait_ge(msc1, 2 * t - 2)
                dve.scalar_tensor_tensor(out=junk[:, ru, 0:8], in0=top_i, scalar=me, in1=top_w, op0=ALU.is_equal,
                                         op1=ALU.mult, accum_out=wsl[:, r]).then_inc(msc1, 1)
                dve.scalar_tensor_tensor(out=junk[:, ru, 8:16], in0=top_i, scalar=me, in1=rank1[:, :],
                                         op0=ALU.is_equal, op1=ALU.mult, accum_out=msc[:, r, 0:1]).then_inc(msc1, 1)
                dve.wait_ge(msc1, 2 * t + 2)
                dve.scalar_tensor_tensor(out=msc[:, r, 1:2], in0=msc[:, r, 0:1], scalar=0.0,
                                         in1=empty_row[:, bass.ds(t, 1)], op0=ALU.is_equal, op1=ALU.mult
                                         ).then_inc(msc2, 1)
                dve.wait_ge(msc2, t + 1)
                dve.scalar_tensor_tensor(out=row[:, r], in0=xg[:, r, REC - 1:REC], scalar=msc[:, r, 0:1],
                                         in1=msc[:, r, 1:2], op0=ALU.add, op1=ALU.add).then_inc(row_done, 1)

            def gated(t, r, q, low):
                dve.wait_ge(sil_done, t + 1)
                if low >= 2:
                    dve.wait_ge(hT_ps, t - 1)
                dve.tensor_tensor(hh[:, r % 2], sil[:, r % 2], bank(2 + r % 2)[:, FE:2 * FE], ALU.mult
                                  ).then_inc(h_done, 1)

            def weigh(t, r, q, low):
                dve.wait_ge(yd_ps, t + 1)
                dve.wait_ge(row_done, t + 1)
                dve.tensor_scalar(ysb[:, r], bank(6 + r % 2)[:, 0:DM], wsl[:, r], None, ALU.mult).then_inc(ysb_done, 1)

            run_steps(dve, NE, 8, [(1, gated), (2, rows), (3, weigh)])

            for t in range(NT):
                dve.wait_ge(yk_ld[t % 4], 16 * (t // 4 + 1))
                dve.tensor_reduce(ysum[:, t % 2], yall[:, t % 4].rearrange("p (k d) -> p d k", k=TOPK), AX.X, ALU.add
                                  ).then_inc(ysum_done, 1)
                dve.wait_ge(ysum_done, t + 1)
                dve.scalar_tensor_tensor(out=xres[:, t, :], in0=ysum[:, t % 2], scalar=tg[:, 3:4], in1=xres[:, t, :],
                                         op0=ALU.mult, op1=ALU.add).then_inc(out_done, 1)



_INS = ['x', 'ctx_1024', 'mask_BxS2_bf1', 'g_xattn', 'g_ffn', 'L0_xattn_in_proj_w', 'L0_xattn_conv_w',
        'L0_xattn_conv_b', 'L0_xattn_x_proj_w', 'L0_xattn_dt_proj_w', 'L0_xattn_dt_proj_b', 'L0_xattn_A_log',
        'L0_xattn_D', 'L0_ffn_c_fc', 'L0_ffn_c_proj', 'L1_xattn_Wq', 'L1_xattn_Wk', 'L1_xattn_Wv', 'L1_xattn_Wo',
        'L1_ffn_gate_w', 'L1_ffn_w_gate', 'L1_ffn_w_up', 'L1_ffn_w_down']


def kernel(**inputs):
    import numpy as _np
    import concourse.bacc as _bacc
    from concourse import mybir as _mybir
    from concourse.bass_utils import run_bass_kernel_spmd as _run

    nc = _bacc.Bacc("TRN2", target_bir_lowering=False, num_devices=1)
    arrays, args = {}, []
    for name in _INS:
        a = _np.ascontiguousarray(inputs[name])
        arrays[f"in_{name}"] = a
        args.append(nc.dram_tensor(f"in_{name}", a.shape, _mybir.dt.from_np(a.dtype), kind="ExternalInput").ap())
    args.append(nc.dram_tensor("out_0", (NB, L, DM), F32, kind="ExternalOutput").ap())
    flamingo_kernel(nc, *args)
    r = _run(nc, [arrays], core_ids=[0])
    return r.results[0]["out_0"]
```

```python
from contextlib import ExitStack

import concourse.bass as bass
from concourse import mybir

F32 = mybir.dt.float32
BF16 = mybir.dt.bfloat16
U32 = mybir.dt.uint32
U8 = mybir.dt.uint8
ALU = mybir.AluOpType
ACT = mybir.ActivationFunctionType
AX = mybir.AxisListType

P = 128
NB, L, DM = 4, 256, 256
NT = NB * L // P
T = NB * L
DC = 128
ND = 2
NST, NTAP, RANK = 16, 4, 8
NPROJ = RANK + 2 * NST
HID = 1024
NH, NKV, HD = 16, 8, 128
NE, TOPK, CAP, FE = 64, 8, 128, 128
REC = DM + 2 * TOPK + 1
EPS = 1e-5
ROUND = 12582912.0
SLOTW = 3 * DM
NSLOT = 32
PRE = 10
WCOLS = NSLOT * SLOTW
KVCOL = WCOLS - 2 * NKV * T


def wait(eng, sem, value):
    if isinstance(value, int) and value <= 0:
        return
    eng.wait_ge(sem, value)


def run_steps(eng, count, unroll, stages, cuts=(), first=None):
    depth = max(lag for lag, _ in stages)

    def straight(steps):
        for s in steps:
            for lag, fn in stages:
                t = s - lag
                if 0 <= t < count:
                    fn(t, t % unroll, t // unroll, t)

    up = lambda n: -(-n // unroll) * unroll
    at = 0
    for end in (*cuts, count):
        head = min(first if first is not None else at + up(depth + (unroll if at == 0 else 0)), end)
        straight(range(at, head))
        if head < end:
            with eng.Fori(0, (end - head) // unroll) as i:
                for base in range(head, end, 1)[:unroll]:
                    for lag, fn in stages:
                        r = (base - lag) % unroll
                        fn(i * unroll + (base - lag), r, i + (base - lag - r) // unroll, base - lag)
        at = end
    straight(range(count, count + depth))


def flamingo_kernel(
    nc, x, ctx_tokens, mask, g_xattn, g_ffn, in_proj_w, conv_w, conv_b, x_proj_w, dt_proj_w, dt_proj_b,
    A_log, D_skip, c_fc, c_proj, Wq, Wk, Wv, Wo, gate_w, w_gate, w_up, w_down, out,
):
    stack = ExitStack()
    with stack:
        sem = lambda name: stack.enter_context(nc.semaphore(name))
        sbuf = lambda name, shape, dt=F32: stack.enter_context(nc.sbuf_tensor(name, shape, dt))

        NREC = NE * CAP
        xg_dram = nc.dram_tensor("dispatched", [NREC + T * TOPK, REC], F32, kind="Internal").ap()
        yk_dram = nc.dram_tensor("expert_out", [T * TOPK + NREC, DM], F32, kind="Internal").ap()

        ident = sbuf("ident", [P, P])
        identb = sbuf("identb", [P, P], BF16)
        tri = sbuf("tri", [P, P])
        ones = sbuf("ones", [P, P])
        iota_e = sbuf("iota_e", [P, NE])
        rank1 = sbuf("rank1", [P, TOPK])
        drop_row = sbuf("drop_row", [P, NT * TOPK])
        empty_row = sbuf("empty_row", [P, NE])
        tok8 = sbuf("tok8", [P, NT])
        nhalf = sbuf("nhalf", [P, 8])
        gates = sbuf("gates", [P, 4])
        tg = sbuf("tg", [P, 4])
        xres = sbuf("xres", [P, NT, DM])
        gateT = sbuf("gateT", [P, ND, NE])
        weights = sbuf("weights", [P, WCOLS])
        kT = weights[:, KVCOL:KVCOL + NKV * T].rearrange("p (j t) -> p j t", j=NKV)
        vS = weights[:, KVCOL + NKV * T:WCOLS].rearrange("p (s c) -> p s c", s=NT)
        NTMP = 23000
        NTAIL = 2700
        tmp = sbuf("tmp", [P, NTMP])

        def carver(area, size):
            at = [0]

            def take(cols, dt=F32, parts=P):
                n = cols if dt in (F32, U32) else (cols + 1) // 2 if dt == BF16 else (cols + 3) // 4
                a = at[0]
                at[0] += n
                assert at[0] <= size, (at[0], size)
                v = area[0:parts, a:a + n]
                return v if dt == F32 else v.bitcast(dt)

            return take

        v2 = lambda ap, a: ap.rearrange("p (a b) -> p a b", a=a)

        mw = carver(weights, KVCOL)
        mt = carver(tmp, NTMP)
        conv_acc = v2(mw(ND * T), ND)
        dA = conv_acc
        sp_z = v2(mw(ND * T), ND)
        dBu = sp_z
        sp_d = v2(mw(ND * T), ND)
        hst = sp_d
        sp_l = v2(mw(ND * T), ND)
        prod = sp_l
        wk_sb = mt(NKV * HD)
        wv_sb = mt(NKV * HD)
        ctxT = mt(T)
        upad = mt(ND * NB * (L + NTAP - 1)).rearrange("p (e b l) -> p e b l", e=ND, b=NB)
        u = v2(mt(ND * T), ND)
        dt = v2(mt(ND * T), ND)
        dtu = v2(mt(ND * T), ND)
        zs = v2(mt(NT * DM), NT)
        sel = mt(2 * NST * P, BF16)
        bc_stack = mt(T, BF16)
        bc_mid = mt(T, BF16)
        bc_lo = mt(T, BF16)
        xdbl = mt(T)
        xdbl_r = sp_d[:, 0]
        in_n = v2(mt(ND * DC), ND)
        inT = mt(ND * P)
        xp_n = mt(DM)
        xpT = v2(mt(ND * NPROJ), ND)
        dtp_n = v2(mt(ND * RANK), ND)
        dtpT = mt(ND * P)
        gate_n = mt(DM)
        cw = v2(mt(ND * NTAP), ND)
        cb = mt(ND)
        dtb = mt(ND)
        dsk = mt(ND)
        dskm = v2(mt(ND * P), ND)
        alog = v2(mt(ND * NST), ND)
        aneg = v2(mt(ND * NST), ND)
        st6 = v2(mt(NT * 6), NT)
        mv1 = v2(mt(NT * 2), NT)
        rs1 = mt(NT)
        nb1 = mt(NT)
        aexp = v2(mt(ND * NST), ND)
        csb = v2(mt(2 * T), 2)
        ctxn = v2(mt(NT * DC), NT)

        ft = carver(tmp, NTMP - NTAIL)
        wraw = v2(ft(2 * ND * HID), 2)
        wneg = ft(ND * HID, BF16)
        xn = v2(ft(2 * DM), 2)
        xhi = ft(2 * DM, BF16).rearrange("p (r c t) -> p r c t", r=2, c=ND)
        xmid = ft(2 * DM, BF16).rearrange("p (r c t) -> p r c t", r=2, c=ND)
        xlo = ft(2 * DM, BF16).rearrange("p (r c t) -> p r c t", r=2, c=ND)
        xr1 = v2(ft(2 * DM), 2)
        rl = v2(ft(2 * HID), 2)
        sq = v2(ft(2 * HID), 2)
        qf = v2(ft(2 * HID), 2)
        qb = v2(ft(2 * HID, BF16), 2)
        qT = ft(2 * HID, BF16).rearrange("p (r h t) -> p r h t", r=2, h=HID // P)
        w1q = v2(ft(ND * HID, BF16), ND)
        w2q = v2(rl[:, 0].bitcast(BF16), ND)
        w2T = v2(ft(HID // P * DM, BF16), HID // P)
        stf, mvf, rsf, sml, wsc = ft(16), ft(8), ft(4), ft(16), ft(16)
        tail = carver(tmp[:, NTMP - NTAIL:NTMP], NTAIL)
        xT = v2(tail(ND * T), ND)
        xn3 = v2(tail(2 * DM), 2)
        st3, mv3, rs3 = tail(16), tail(8), tail(4)

        ab = carver(tmp, NTMP - NTAIL)
        vbuf = ab(2 * 2 * HD).rearrange("p (m s d) -> p m s d", m=2, s=2)
        Pn = ab(2 * 512).rearrange("p (r a s) -> p r a s", r=2, a=2)
        qTh = ab(2 * 2 * L).rearrange("p (m u t) -> p m u t", m=2, u=2)
        sm = ab(2 * 512).rearrange("p (r a s) -> p r a s", r=2, a=2)
        pe_ = ab(2 * 512).rearrange("p (r a s) -> p r a s", r=2, a=2)
        pT = ab(2 * 512).rearrange("p (r a s) -> p r a s", r=2, a=2)
        attT = ab(4 * L).rearrange("p (m u t) -> p m u t", m=2, u=2)
        wq_sb = ab(2 * ND * 2 * HD).rearrange("p (m c d) -> p m c d", m=2, c=ND)
        wo_sb = v2(ab(NH * DM), NH)
        mx, nm, sume, rc = v2(ab(4), 2), v2(ab(4), 2), v2(ab(4), 2), v2(ab(4), 2)
        mask_sb = ab(NB * L, U8)
        maskb = v2(ab(NB * L), NB)
        mask_now = ab(L)
        valid = ab(NB)

        rec = v2(ab(2 * REC), 2)
        xTr = v2(ab(DM), ND)
        rp = v2(ab(2 * NE), 2)
        oh = v2(ab(2 * TOPK * NE), 2)
        ohp = ab(TOPK * NE)
        fl = v2(ab(2 * NE), 2)
        cum = ab(NE)
        idxu = v2(ab(2 * TOPK, U32), 2)
        posk = ab(TOPK)
        locf = ab(TOPK)
        loc2 = ab(TOPK)
        loc = v2(ab(2 * TOPK, U32), 2)
        rst = v2(ab(2 * 6), 2)
        rmv = v2(ab(2 * 4), 2)
        rsm = v2(ab(2 * 4), 2)

        ra = carver(tmp, NTMP)
        xg = v2(ra(8 * REC), 8)
        xgT = ra(2 * DM).rearrange("p (r c t) -> p r c t", r=2, c=ND)
        sil = v2(ra(2 * FE), 2)
        hh = v2(ra(2 * FE), 2)
        hT = v2(ra(2 * CAP), 2)
        ysb = v2(ra(8 * DM), 8)
        wsl = v2(ra(8), 8)
        msc = v2(ra(8 * 2), 8)
        junk = v2(ra(2 * 16), 2)
        row = v2(ra(8, U32), 8)
        yall = v2(weights[:, 0:4 * TOPK * DM], 4)
        ysum = v2(ra(2 * DM), 2)
        initrec = sbuf("initrec", [P, REC])
        zeros = sbuf("zeros", [P, 1024])

        ps = stack.enter_context(nc.psum_tensor("ps", [P, 8 * 512], F32))
        bank = lambda k, n=1: ps[:, 512 * k:512 * (k + n)]

        ld_ctx, ld_small, ld_x, ld_kv = sem("ld_ctx"), sem("ld_small"), sem("ld_x"), sem("ld_kv")
        ld_vec = sem("ld_vec")
        ld_gates, ld_mask, ld_mlp = sem("ld_gates"), sem("ld_mask"), sem("ld_mlp")
        ld_wo, ld_preA, ld_preB = sem("ld_wo"), sem("ld_preA"), sem("ld_preB")
        init_done = sem("init_done")
        consts, sel_done = sem("consts"), sem("sel_done")
        tanh_done = sem("tanh_done")
        ctxT_ps, smallT_ps, ctxT_sb, smallT_sb = sem("ctxT_ps"), sem("smallT_ps"), sem("ctxT_sb"), sem("smallT_sb")
        xin_ps, upad_sb, conv_done, u_sb = sem("xin_ps"), sem("upad_sb"), sem("conv_done"), sem("u_sb")
        xdbl_ps, xdbl_sb, split_done, stacked = sem("xdbl_ps"), sem("xdbl_sb"), sem("split_done"), sem("stacked")
        dt_ps, sp_act, dt_done, dtu_done = sem("dt_ps"), sem("sp_act"), sem("dt_done"), sem("dtu_done")
        act_sp = sem("act_sp")
        a_exp, a_neg, dskm_done = sem("a_exp"), sem("a_neg"), sem("dskm_done")
        ln1_stats, ln1_rstd, ln1_nb, zs_done = sem("ln1_stats"), sem("ln1_rstd"), sem("ln1_nb"), sem("zs_done")
        kv_ps, kv_sb = sem("kv_ps"), sem("kv_sb")
        b_rdy, dbu_done, da_rdy, c_rdy, c_sb = sem("b_rdy"), sem("dbu_done"), sem("da_rdy"), sem("c_rdy"), sem("c_sb")
        scan_done, prod_done, prod_used, y_init = sem("scan_done"), sem("prod_done"), sem("prod_used"), sem("y_init")
        yz_done, yT_ps, x1_done = sem("yz_done"), sem("yT_ps"), sem("x1_done")
        dve_chain, pool_chain = sem("dve_chain"), sem("pool_chain")
        wabs_done, wsum_ps, w1_done, w2_done, w2T_ps, w2T_sb = (sem("wabs_done"), sem("wsum_ps"), sem("w1_done"),
                                                                 sem("w2_done"), sem("w2T_ps"), sem("w2T_sb"))
        st_done, rstd_done, xn_done, xT_ps, hi_done, r1_done = (sem("st_done"), sem("rstd_done"), sem("xn_done"),
                                                                sem("xT_ps"), sem("hi_done"), sem("r1_done"))
        mid_done, lo_done, h_ps, relu_done, sq_done, rs_done = (sem("mid_done"), sem("lo_done"), sem("h_ps"),
                                                                sem("relu_done"), sem("sq_done"), sem("rs_done"))
        qf_done, qb_done, qT_ps, qT_sb, o_ps, x2_done = (sem("qf_done"), sem("qb_done"), sem("qT_ps"),
                                                         sem("qT_sb"), sem("o_ps"), sem("x2_done"))
        st3_done, rstd3_done, xn3_done, xT3_ps, xT3_sb = (sem("st3_done"), sem("rstd3_done"), sem("xn3_done"),
                                                          sem("xT3_ps"), sem("xT3_sb"))
        mask_done = sem("mask_done")
        q_ps, q_sb, vb_done = sem("q_ps"), sem("q_sb"), sem("vb_done")
        s_ps, smax_done, nm_done, exp_done, rc_done = (sem("s_ps"), sem("smax_done"), sem("nm_done"),
                                                       sem("exp_done"), sem("rc_done"))
        pn_done, pT_ps, pT_sb, pv_ps, att_sb, ao_ps, x3_done = (sem("pn_done"), sem("pT_ps"), sem("pT_sb"),
                                                                sem("pv_ps"), sem("att_sb"), sem("ao_ps"), sem("x3_done"))
        rc_raw, smax_go = sem("rc_raw"), sem("smax_go")
        ld_wq = [sem("ld_wq0"), sem("ld_wq1")]
        st4_done, rstd4_done, rec_done = sem("st4_done"), sem("rstd4_done"), sem("rec_done")
        rT_ps, rT_sb, lg_ps, rmax_done, rexp_done = (sem("rT_ps"), sem("rT_sb"), sem("lg_ps"),
                                                     sem("rmax_done"), sem("rexp_done"))
        fl_done, pos_ps, pos_used, loc_done, dispatched = (sem("fl_done"), sem("pos_ps"), sem("pos_used"),
                                                           sem("loc_done"), sem("dispatched"))
        route_chain, route_go, rstd4_sum, cum_done, rec_free = (sem("route_chain"), sem("route_go"), sem("rstd4_sum"),
                                                                sem("cum_done"), sem("rec_free"))
        xg_ld = [sem(f"xg_ld{r}") for r in range(4)]
        w_ld = [sem(f"w_ld{r}") for r in range(4)]
        scattered = [sem(f"scattered{r}") for r in range(4)]
        xgT_ps, xgT_sb, gu_ps, sil_done, h_done = (sem("xgT_ps"), sem("xgT_sb"), sem("gu_ps"), sem("sil_done"),
                                                   sem("h_done"))
        hT_ps, hT_sb, yd_ps, ysb_done = sem("hT_ps"), sem("hT_sb"), sem("yd_ps"), sem("ysb_done")
        msc1, msc2, msc3, row_done = sem("msc1"), sem("msc2"), sem("msc3"), sem("row_done")
        scatter_go = sem("scatter_go")
        yk_ld = [sem(f"yk_ld{r}") for r in range(4)]
        ysum_done, out_done, stored = sem("ysum_done"), sem("out_done"), sem("stored")

        block = stack.enter_context(nc.Block())

        NCONST = 18

        NU = 2 * NKV
        run_units = lambda eng, stages: run_steps(eng, NB * NU, NU, stages, first=NU)

        def tile_at(step, h, fn):
            return step - h, lambda t, r, q, low: fn(h, q, 2 * q + h) if r == h else None

        @block.sync
        def _(sp):
            sp.dma_start(ctxn, ctx_tokens.rearrange("b (h p) c -> p (b h) c", p=P)).then_inc(ld_ctx, 16)
            sp.dma_start(in_n, in_proj_w.rearrange("(e p) c -> p e c", p=P)).then_inc(ld_ctx, 16)
            sp.dma_start(xres[:, :, :], x.rearrange("b (h p) d -> p (b h) d", p=P)).then_inc(ld_x, 16)
            sp.dma_start(xp_n[0:NPROJ, :], x_proj_w).then_inc(ld_small, 16)
            sp.dma_start(dtp_n, dt_proj_w.rearrange("(e p) r -> p e r", p=P)).then_inc(ld_small, 16)
            sp.dma_start(gate_n[0:NE, :], gate_w).then_inc(ld_small, 16)
            sp.dma_start(wk_sb, Wk).then_inc(ld_kv, 16)
            sp.dma_start(wv_sb, Wv).then_inc(ld_kv, 16)
            sp.wait_ge(split_done, 3)
            sp.dma_start(bc_stack[NPROJ:2 * NPROJ, :], bc_mid[0:NPROJ, :]).then_inc(stacked, 16)
            sp.dma_start(bc_stack[2 * NPROJ:3 * NPROJ, :], bc_lo[0:NPROJ, :]).then_inc(stacked, 16)
            sp.wait_ge(consts, NCONST)
            sp.wait_ge(pool_chain, 6)
            sp.dma_start(xg_dram[0:NREC, :].rearrange("(e c) f -> c e f", c=CAP),
                         initrec[:, :].unsqueeze(1).to_broadcast([P, NE, REC])).then_inc(init_done, 16)
            ykz = yk_dram[0:T * TOPK, :].rearrange("(p i r) d -> p i (r d)", p=P, r=4)
            sp.dma_start(ykz, zeros[:, :].unsqueeze(1).to_broadcast([P, T * TOPK // P // 4, 4 * DM])
                         ).then_inc(init_done, 16)

            sp.wait_ge(kv_sb, 32)
            sp.wait_ge(conv_done, 2)
            for w, src in enumerate((c_fc, c_proj)):
                sp.dma_start(v2(wraw[:, w], ND), src.rearrange("(c p) h -> p c h", p=P)).then_inc(ld_mlp, 16)

            def load_experts(e, slot, signal):
                dst = weights[:, bass.ds(slot * SLOTW, 2 * SLOTW)]
                gu = dst[:, 0:4 * DM].rearrange("p (w g f) -> p w g f", g=2, f=FE)
                for g, w in enumerate((w_gate, w_up)):
                    sp.dma_start(gu[:, :, g, :], w[bass.ds(e, 2)].rearrange("a (c p) f -> p (a c) f", p=P)
                                 ).then_inc(signal, 16)
                sp.dma_start(v2(dst[:, 4 * DM:], 2), w_down[bass.ds(e, 2)].rearrange("a p f -> p a f")
                             ).then_inc(signal, 16)

            wq_cols = Wq.rearrange("(c p) n -> p c n", p=P)

            def load_wq(t, r, q, low):
                if r % 2:
                    return
                j = r // 2
                if low >= 4:
                    sp.wait_ge(q_ps, NKV * q + j - 1)
                sp.dma_start(wq_sb[:, j % 2], wq_cols[:, :, 2 * j * HD:(2 * j + 2) * HD]).then_inc(ld_wq[j % 2], 16)

            sp.wait_ge(x1_done, NB)
            for e in range(0, PRE, 2):
                load_experts(e, e, ld_preA)
            sp.wait_ge(x2_done, NT)
            sp.dma_start(mask_sb, mask.rearrange("b s -> (b s)").partition_broadcast(P)).then_inc(ld_mask, 16)
            sp.dma_start(wo_sb, Wo.rearrange("(h d) n -> d h n", d=HD)).then_inc(ld_wo, 16)
            run_units(sp, [(0, load_wq)])
            sp.wait_ge(x3_done, NB * NKV)
            for e in range(PRE, NSLOT, 2):
                load_experts(e, e, ld_preB)
            sp.wait_ge(init_done, 32)
            sp.wait_ge(dispatched, 16 * NT * TOPK)

            def load_xg(t, r, q, low):
                if r % 2:
                    return
                if low >= 8:
                    sp.wait_ge(xgT_ps, t - 6)
                    sp.wait_ge(row_done, t - 6)
                src = xg_dram[bass.ds(t * CAP, 2 * CAP), :].rearrange("(a p) f -> p a f", p=P)
                sp.dma_start(xg[:, r:r + 2, :], src).then_inc(xg_ld[r // 2], 16)

            def load_next(t, r, q, low):
                if low + NSLOT >= NE or r % 2 == 0:
                    return
                sp.wait_ge(yd_ps, t + 1)
                if low >= 8:
                    sp.wait_ge(w_ld[r // 2], 48 * q)
                load_experts(t - 1 + NSLOT, t - 1, w_ld[r // 2])

            run_steps(sp, NE, 8, [(0, load_xg), (8, load_next)], cuts=(NSLOT,))

            sp.wait_ge(yd_ps, NE)
            for r in range(4):
                sp.wait_ge(scattered[r], 16 * (NE // 4))
            for t in range(NT):
                if t >= 4:
                    sp.wait_ge(ysum_done, t - 3)
                sp.dma_start(yall[:, t % 4, :],
                             yk_dram[t * P * TOPK:(t + 1) * P * TOPK, :].rearrange("(p k) d -> p (k d)", k=TOPK)
                             ).then_inc(yk_ld[t % 4], 16)
            for t in range(NT):
                sp.wait_ge(out_done, t + 1)
                b, h = t // 2, t % 2
                sp.dma_start(out[b, h * P:(h + 1) * P, :], xres[:, t, :]).then_inc(stored, 16)
            sp.wait_ge(stored, 16 * NT)

        @block.gpsimd
        def _(pool):
            def unit(out_ap, step):
                return pool.affine_select(out=out_ap, in_=out_ap, compare_op=ALU.not_equal, fill=1.0, base=0,
                                          pattern=[[-1, P]], channel_multiplier=1)

            pool.dma_start(cw, conv_w.rearrange("(e p) a k -> p e (a k)", p=P)).then_inc(ld_vec, 16)
            pool.dma_start(cb, conv_b.rearrange("(e p) -> p e", p=P), allow_slow_non_contiguous=True).then_inc(ld_vec, 16)
            pool.dma_start(dtb, dt_proj_b.rearrange("(e p) -> p e", p=P), allow_slow_non_contiguous=True).then_inc(ld_vec, 16)
            pool.dma_start(dsk, D_skip.rearrange("(e p) -> p e", p=P), allow_slow_non_contiguous=True).then_inc(ld_vec, 16)
            pool.dma_start(alog, A_log.rearrange("(e p) n -> p e n", p=P)).then_inc(ld_vec, 16)
            pool.dma_start(gates[:, 0:2], g_xattn.partition_broadcast(P)).then_inc(ld_gates, 16)
            pool.dma_start(gates[:, 2:4], g_ffn.partition_broadcast(P)).then_inc(ld_gates, 16)

            pool.memset(ident[:, :], 0.0).then_inc(consts, 1)
            pool.memset(identb[:, :], 0.0).then_inc(consts, 1)
            pool.wait_ge(consts, 2)
            unit(ident[:, :], 1).then_inc(consts, 1)
            unit(identb[:, :], 1).then_inc(consts, 1)
            pool.memset(upad[:, :, :, 0:NTAP - 1], 0.0).then_inc(consts, 1)
            pool.memset(nhalf[:, :], -0.5).then_inc(consts, 1)
            pool.wait_ge(ln1_stats, 1)
            pool.wait_ge(consts, 6)
            pool.tensor_scalar(rs1, mv1[:, :, 1], EPS, None, ALU.add).then_inc(pool_chain, 1)
            pool.wait_ge(pool_chain, 1)
            pool.tensor_tensor(rs1, rs1, nhalf[:, :], ALU.pow).then_inc(ln1_rstd, 1)
            selv = sel.rearrange("p (n m) -> p n m", m=P)[0:3 * NPROJ]
            pool.memset(sel.bitcast(F32), 0.0).then_inc(pool_chain, 1)
            for n in range(3):
                pool.wait_ge(pool_chain, 2 + n)
                pool.affine_select(out=selv, in_=selv, compare_op=ALU.not_equal, fill=1.0,
                                   base=-(RANK + n * NPROJ), pattern=[[-1, 2 * NST], [0, P]],
                                   channel_multiplier=1).then_inc(pool_chain, 1)
            pool.wait_ge(pool_chain, 5)
            pool.wait_ge(u_sb, 2)
            for e in range(ND):
                pool.memset(dA[:, e].rearrange("p (b l) -> p b l", b=NB)[:, :, 0:1], 0.0).then_inc(sel_done, 1)
            pool.memset(ones[:, :], 1.0).then_inc(consts, 1)
            pool.memset(tri[:, :], 1.0).then_inc(consts, 1)
            pool.wait_ge(consts, 8)
            pool.affine_select(out=tri[:, :], in_=tri[:, :], compare_op=ALU.is_gt, fill=0.0, base=0,
                               pattern=[[1, P]], channel_multiplier=-1).then_inc(consts, 1)
            io = dict(allow_small_or_imprecise_dtypes=True)
            pool.iota(iota_e[:, :], [[1, NE]], base=0, channel_multiplier=0, **io).then_inc(consts, 1)
            pool.iota(rank1[:, :], [[1, TOPK]], base=1, channel_multiplier=0, **io).then_inc(consts, 1)
            pool.iota(drop_row[:, :], [[P, NT * TOPK]], base=NREC, channel_multiplier=1, **io).then_inc(consts, 1)
            pool.iota(tok8[:, :], [[P * TOPK, NT]], base=-1, channel_multiplier=TOPK, **io).then_inc(consts, 1)
            pool.iota(empty_row[:, :], [[CAP, NE]], base=T * TOPK + 1, channel_multiplier=1, **io).then_inc(consts, 1)
            pool.memset(initrec[:, 0:DM], 0.0).then_inc(consts, 1)
            pool.memset(initrec[:, DM:DM + TOPK], -1.0).then_inc(consts, 1)
            pool.memset(initrec[:, DM + TOPK:REC - 1], 0.0).then_inc(consts, 1)
            pool.memset(initrec[:, REC - 1:REC], -1.0).then_inc(consts, 1)
            pool.memset(zeros[:, :], 0.0).then_inc(pool_chain, 1)
            pool.wait_ge(pool_chain, 6)

            def prods(t, r, q, low):
                for e in range(ND):
                    m = 2 * t + e
                    pool.wait_ge(scan_done, m + 1)
                    if e == 0:
                        pool.wait_ge(c_sb, t + 1)
                    wait(pool, prod_used, m - 1 if low > 0 or e > 0 else 0)
                    pool.tensor_tensor(prod[:, e], hst[:, e], csb[:, r], ALU.mult).then_inc(prod_done, 1)

            run_steps(pool, NST, 2, [(0, prods)])

            def rstd(src, dst, stats, tmp_count, signal, t):
                pool.wait_ge(stats, t + 1)
                pool.tensor_scalar(dst, src, EPS, None, ALU.add).then_inc(pool_chain, 1)
                tmp_count[0] += 1
                pool.wait_ge(pool_chain, tmp_count[0])
                pool.tensor_tensor(dst, dst, nhalf[:, 0:1], ALU.pow).then_inc(signal, 1)

            chain = [6]
            for s in range(NT + 6):
                if s < NT:
                    r = s % 2
                    if s >= 2:
                        pool.wait_ge(xn_done, s - 1)
                    rstd(mvf[:, 2 * r + 1:2 * r + 2], rsf[:, r:r + 1], st_done, chain, rstd_done, s)
                if 0 <= s - 2 < NT:
                    t, r = s - 2, (s - 2) % 2
                    pool.wait_ge(relu_done, t + 1)
                    wait(pool, qf_done, t - 1)
                    pool.tensor_tensor(sq[:, r], rl[:, r], rl[:, r], ALU.mult).then_inc(sq_done, 1)
                if 0 <= s - 5 < NT:
                    t, r = s - 5, (s - 5) % 2
                    if t >= 2:
                        pool.wait_ge(xn3_done, t - 1)
                    rstd(mv3[:, 2 * r + 1:2 * r + 2], rs3[:, r:r + 1], st3_done, chain, rstd3_done, t)

            def vcopy(t, r, q, low):
                if r % 2:
                    return
                j = r // 2
                if low >= 4:
                    pool.wait_ge(pv_ps, t - 2)
                pool.tensor_copy(vbuf[:, j % 2], vS[:, bass.ds(2 * q, 2), j * HD:(j + 1) * HD]).then_inc(vb_done, 1)

            def rstd4(h, q, k):
                pool.wait_ge(st4_done, k + 1)
                pool.sem_inc(scatter_go, 1)
                pool.tensor_scalar(rmv[:, h, 2:3], rmv[:, h, 1:2], EPS, None, ALU.add).then_inc(rstd4_sum, 1)
                pool.wait_ge(rstd4_sum, k + 1)
                pool.tensor_tensor(rmv[:, h, 2:3], rmv[:, h, 2:3], nhalf[:, 0:1], ALU.pow).then_inc(rstd4_done, 1)

            def dispatch(ranks):
                def fn(h, q, k):
                    pool.wait_ge(loc_done, k + 1)
                    pool.sem_inc(scatter_go, 1)
                    for i in ranks:
                        pool.indirect_dma_start(xg_dram, bass.IndirectOffsetOnAxis(loc[:, h, i:i + 1], 0), rec[:, h, :],
                                                None).then_inc(dispatched, 16)
                    if h == 1 and ranks[-1] == TOPK - 1:
                        pool.wait_ge(dispatched, 16 * 2 * TOPK * (q + 1))
                        pool.sem_inc(rec_free, 1)

                return fn

            third = (range(0, 3), range(3, 6), range(6, TOPK))
            pool.wait_ge(kv_sb, 32)
            pool.wait_ge(x2_done, NT)
            pool.wait_ge(init_done, 32)
            pool.sem_inc(rec_free, 1)
            run_units(pool, [(1, vcopy), tile_at(20, 0, rstd4), tile_at(21, 1, rstd4),
                             *(tile_at(27 + i, 0, dispatch(third[i])) for i in range(3)),
                             *(tile_at(29 + i, 1, dispatch(third[i])) for i in range(3))])

            def scatter(t, r, q, low):
                if low >= 4:
                    pool.wait_ge(scattered[r % 4], 16 * (2 * q + r // 4))
                pool.wait_ge(ysb_done, t + 1)
                pool.sem_inc(scatter_go, 1)
                pool.indirect_dma_start(yk_dram, bass.IndirectOffsetOnAxis(row[:, r], 0), ysb[:, r, :],
                                        None).then_inc(scattered[r % 4], 16)

            run_steps(pool, NE, 8, [(0, scatter)])

        @block.scalar
        def _(act):
            act.wait_ge(ld_gates, 32)
            act.activation(tg[:, :], gates[:, :], ACT.Tanh).then_inc(tanh_done, 1)
            act.wait_ge(ld_small, 16 * 3)
            act.wait_ge(ld_vec, 16 * 5)
            act.activation(aexp, alog, ACT.Exp).then_inc(a_exp, 1)
            for n in range(2):
                act.wait_ge(ctxT_ps, n + 1)
                act.activation(ctxT[:, 512 * n:512 * n + 512], bank(n), ACT.Copy).then_inc(ctxT_sb, 1)
            act.wait_ge(consts, 5)
            for g in range(4):
                e, h = g // 2, g % 2
                act.wait_ge(xin_ps, g + 1)
                act.activation(upad[:, e, 2 * h:2 * h + 2, NTAP - 1:], v2(bank(4 + g), 2), ACT.Copy).then_inc(upad_sb, 1)

            def kv_evac(g):
                act.wait_ge(kv_ps, g + 1)
                n, h = (g % 16) // 2, g % 2
                dst = kT if g < 16 else vS
                act.activation(dst[:, n, 512 * h:512 * h + 512], bank(2 + g % 2), ACT.Copy).then_inc(kv_sb, 1)

            act.wait_ge(ln1_nb, 1)
            for t in range(NT):
                act.activation(zs[:, t], xres[:, t, :], ACT.Silu, bias=nb1[:, t:t + 1],
                               scale=rs1[:, t:t + 1]).then_inc(zs_done, 1)
            for g in range(6):
                kv_evac(g)
            for e in range(ND):
                act.wait_ge(conv_done, e + 1)
                act.activation(u[:, e], conv_acc[:, e], ACT.Silu).then_inc(u_sb, 1)
                for g in range(6 + 3 * e, 9 + 3 * e):
                    kv_evac(g)
            for h in range(2):
                act.wait_ge(xdbl_ps, h + 1)
                act.activation(xdbl[0:NPROJ, 512 * h:512 * h + 512], bank(h)[0:NPROJ, :],
                               ACT.Copy).then_inc(xdbl_sb, 1)
            n = 0
            for e in range(ND):
                act.wait_ge(dt_ps, 2 * e + 2)
                act.activation(sp_z[:, e], bank(4 + 2 * e, 2), ACT.Abs, bias=dtb[:, e:e + 1]).then_inc(act_sp, 1)
                act.activation(dt[:, e], bank(4 + 2 * e, 2), ACT.Relu, bias=dtb[:, e:e + 1]).then_inc(act_sp, 1)
            for e in range(ND):
                act.wait_ge(act_sp, 2 * e + 2 if e else 4)
                act.activation(sp_z[:, e], sp_z[:, e], ACT.Exp, scale=-1.0).then_inc(act_sp, 1)
                act.wait_ge(act_sp, 5 + 2 * e)
                act.activation(sp_l[:, e], sp_z[:, e], ACT.Ln, bias=1.0).then_inc(act_sp, 1)
            for g in range(12, 32):
                kv_evac(g)
            act.wait_ge(a_neg, 1)
            act.wait_ge(sel_done, 2)
            act.preload_act_table(ACT.Exp)

            def da(t, r, q, low):
                for e in range(ND):
                    m = 2 * t + e
                    wait(act, scan_done, m - 1 if low > 0 or e > 0 else 0)
                    if low == 0:
                        act.wait_ge(dt_done, e + 1)
                    bl = lambda ap: ap.rearrange("p (b l) -> p b l", b=NB)[:, :, 1:]
                    act.activation(bl(dA[:, e]), bl(dt[:, e]), ACT.Exp,
                                   scale=aneg[:, e, bass.ds(t, 1)]).then_inc(da_rdy, 1)

            def ccopy(t, r, q, low):
                act.wait_ge(c_rdy, t + 1)
                wait(act, prod_done, 2 * t - 2 if low > 1 else 0)
                act.activation(csb[:, r], bank(2, 2), ACT.Copy).then_inc(c_sb, 1)

            run_steps(act, NST, 2, [(0, da), (0, ccopy)])

            act.preload_act_table(ACT.Exp)
            for g in range(4):
                act.wait_ge(w2T_ps, g + 1)
                act.activation(w2T[:, 2 * g:2 * g + 2, :].rearrange("p a d -> p (a d)"),
                               bank(6).bitcast(BF16)[:, 0:512], ACT.Copy).then_inc(w2T_sb, 1)
            for s in range(NT + 7):
                t = s - 1
                if 0 <= t < NT:
                    r = t % 2
                    act.wait_ge(xT_ps, t + 1)
                    wait(act, h_ps, t - 1)
                    act.activation(xhi[:, r].rearrange("p c t -> p (c t)"), bank(0)[:, 0:DM], ACT.Copy).then_inc(hi_done, 1)
                t = s - 2
                if 0 <= t < NT:
                    r = t % 2
                    act.wait_ge(h_ps, t + 1)
                    wait(act, rs_done, t - 1)
                    wait(act, sq_done, t - 1)
                    act.activation(rl[:, r], bank(2 + 2 * r, 2), ACT.Relu).then_inc(relu_done, 1)
                t = s - 1
                if 0 <= t < NT:
                    r = t % 2
                    act.wait_ge(r1_done, t + 1)
                    act.activation(xmid[:, r].rearrange("p c t -> p (c t)"), xr1[:, r], ACT.Copy).then_inc(mid_done, 1)
                t = s - 4
                if 0 <= t < NT:
                    r = t % 2
                    act.wait_ge(qT_ps, t + 1)
                    wait(act, o_ps, t - 1)
                    act.activation(qT[:, r].rearrange("p h t -> p (h t)"), bank(6).bitcast(BF16), ACT.Copy).then_inc(qT_sb, 1)
                t = s - 3
                if 0 <= t < NT:
                    r = t % 2
                    act.wait_ge(rs_done, t + 1)
                    act.wait_ge(sq_done, t + 1)
                    wait(act, qb_done, t - 1)
                    act.activation(qf[:, r], sq[:, r], ACT.Identity, bias=wsc[:, 8:9],
                                   scale=sml[:, 8 * r + 3:8 * r + 4]).then_inc(qf_done, 1)
                t = s - 6
                if 0 <= t < NT:
                    act.wait_ge(xT3_ps, t + 1)
                    act.activation(xT[:, :, t * P:(t + 1) * P], v2(bank(1)[:, 0:DM], ND), ACT.Copy).then_inc(xT3_sb, 1)

            def q_evac(t, r, q, low):
                if r % 2:
                    return
                j = r // 2
                act.wait_ge(q_ps, NKV * q + j + 1)
                if low >= 4:
                    act.wait_ge(s_ps, t - 2)
                act.activation(qTh[:, j % 2].rearrange("p u t -> p (u t)"), bank(6), ACT.Copy).then_inc(q_sb, 1)

            def exps(t, r, q, low):
                r2 = r % 2
                act.wait_ge(nm_done, t + 1)
                if low >= 2:
                    act.wait_ge(pn_done, t - 1)
                for a in range(2):
                    act.activation(pe_[:, r2, a], sm[:, r2, a], ACT.Exp, bias=nm[:, r2, a:a + 1], scale=HD ** -0.5,
                                   accum_out=sume[:, r2, a:a + 1]).then_inc(exp_done, 1)

            def norm(t, r, q, low):
                r2 = r % 2
                act.wait_ge(rc_done, t + 1)
                if low >= 2:
                    act.wait_ge(pT_ps, t - 1)
                for a in range(2):
                    ins = act.activation(Pn[:, r2, a], pe_[:, r2, a], ACT.Copy, scale=rc[:, r2, a:a + 1])
                ins.then_inc(pn_done, 1)

            def pv_evac(t, r, q, low):
                j, uu = r // 2, r % 2
                act.wait_ge(pv_ps, t + 1)
                if low >= 4:
                    act.wait_ge(ao_ps, NKV * q + j - 1)
                act.activation(attT[:, j % 2, uu], bank(4)[:, uu * L:(uu + 1) * L], ACT.Copy).then_inc(att_sb, 1)

            def rT_evac(h, q, k):
                act.wait_ge(rT_ps, k + 1)
                if h == 1:
                    act.wait_ge(lg_ps, k)
                act.activation(xTr.rearrange("p c t -> p (c t)"), bank(5)[:, 0:DM], ACT.Copy).then_inc(rT_sb, 1)

            def rexp(h, q, k):
                act.wait_ge(rmax_done, k + 1)
                act.activation(rp[:, h], bank(5)[:, DM:DM + NE], ACT.Exp, bias=rsm[:, h, 0:1],
                               accum_out=rsm[:, h, 1:2]).then_inc(rexp_done, 1)

            act.preload_act_table(ACT.Exp)
            run_units(act, [(2, exps), (0, q_evac), (2, norm), (3, pv_evac), tile_at(22, 0, rT_evac),
                            tile_at(23, 0, rexp), tile_at(24, 1, rT_evac), tile_at(25, 1, rexp)])

            def xgT_evac(t, r, q, low):
                act.wait_ge(xgT_ps, t + 1)
                if low >= 2:
                    act.wait_ge(gu_ps, t - 1)
                act.activation(xgT[:, r % 2].rearrange("p c t -> p (c t)"), bank(r % 2)[:, 0:DM], ACT.Copy
                               ).then_inc(xgT_sb, 1)

            def silu(t, r, q, low):
                act.wait_ge(gu_ps, t + 1)
                if low >= 2:
                    act.wait_ge(h_done, t - 1)
                act.activation(sil[:, r % 2], bank(2 + r % 2)[:, 0:FE], ACT.Silu).then_inc(sil_done, 1)

            def hT_evac(t, r, q, low):
                act.wait_ge(hT_ps, t + 1)
                if low >= 2:
                    act.wait_ge(yd_ps, t - 1)
                act.activation(hT[:, r % 2], bank(4 + r % 2)[:, 0:CAP], ACT.Copy).then_inc(hT_sb, 1)

            act.preload_act_table(ACT.Silu)
            run_steps(act, NE, 8, [(0, xgT_evac), (1, silu), (2, hT_evac)])

        @block.tensor
        def _(pe):
            mm = lambda o, a, b, s, e, **k: pe.matmul(o, a, b, start=s, stop=e, **k)
            pe.wait_ge(consts, 4)
            pe.wait_ge(ld_ctx, 32)
            for t in range(NT):
                ins = pe.transpose(bank(t // 4)[:, (t % 4) * P:(t % 4 + 1) * P], ctxn[:, t], ident[:, :])
                if t % 4 == 3:
                    ins.then_inc(ctxT_ps, 1)
            for e in range(ND):
                ins = pe.transpose(bank(2)[:, e * P:(e + 1) * P], in_n[:, e], ident[:, :])
            ins.then_inc(smallT_ps, 1)
            pe.wait_ge(ld_small, 16 * 3)
            pe.wait_ge(ld_vec, 16 * 5)
            for e in range(ND):
                pe.transpose(bank(3)[:, e * NPROJ:(e + 1) * NPROJ], xp_n[0:NPROJ, e * P:(e + 1) * P],
                             ident[0:NPROJ, 0:NPROJ])
                pe.transpose(bank(3)[0:RANK, 128 + e * P:128 + (e + 1) * P], dtp_n[:, e], ident[:, :])
                ins = pe.transpose(bank(3)[:, 384 + e * NE:384 + (e + 1) * NE], gate_n[0:NE, e * P:(e + 1) * P],
                                   ident[0:NE, 0:NE])
            ins.then_inc(smallT_ps, 1)
            pe.wait_ge(ctxT_sb, 2)
            pe.wait_ge(smallT_sb, 1)
            for g in range(4):
                e, h = g // 2, g % 2
                mm(bank(4 + g), inT[:, e * P:(e + 1) * P], ctxT[:, 512 * h:512 * h + 512], True, True).then_inc(xin_ps, 1)

            def kv(g):
                if g == 0:
                    pe.wait_ge(ld_kv, 32)
                if g < 2:
                    pe.wait_ge(smallT_sb, 2)
                else:
                    pe.wait_ge(kv_sb, g - 1)
                n, h = (g % 16) // 2, g % 2
                if g < 16:
                    a, b = wk_sb[:, n * HD:(n + 1) * HD], ctxT[:, 512 * h:512 * h + 512]
                else:
                    a, b = ctxT[:, n * P:(n + 1) * P], wv_sb[:, 512 * h:512 * h + 512]
                mm(bank(2 + g % 2), a, b, True, True).then_inc(kv_ps, 1)

            for g in range(12):
                kv(g)
            pe.wait_ge(u_sb, 2)
            for h in range(2):
                for e in range(ND):
                    ins = mm(bank(h)[0:NPROJ, :], xpT[:, e], u[:, e, 512 * h:512 * h + 512], e == 0, e == 1)
                ins.then_inc(xdbl_ps, 1)
            pe.wait_ge(upad_sb, 4)
            pe.wait_ge(xdbl_sb, 2)
            for g in range(4):
                e, h = g // 2, g % 2
                mm(bank(4 + g), dtpT[0:RANK, e * P:(e + 1) * P], xdbl[0:RANK, 512 * h:512 * h + 512], True, True
                   ).then_inc(dt_ps, 1)
            for g in range(12, 32):
                kv(g)
            pe.wait_ge(dskm_done, 1)
            pe.wait_ge(act_sp, 4)
            for g in range(4):
                e, h = g // 2, g % 2
                mm(bank(4 + g), dskm[:, e], u[:, e, 512 * h:512 * h + 512], True, False, skip_group_check=True)
            pe.wait_ge(stacked, 32)
            pe.wait_ge(kv_sb, 32)
            pe.wait_ge(pool_chain, 5)

            def bc(t, r, q, low):
                if low > 0:
                    pe.wait_ge(dbu_done, 2 * t)
                for h in range(2):
                    ins = mm(bank(h), sel[0:3 * NPROJ, bass.ds(t * P, P)],
                             bc_stack[0:3 * NPROJ, 512 * h:512 * h + 512], True, True)
                ins.then_inc(b_rdy, 1)
                if low > 0:
                    pe.wait_ge(c_sb, t)
                for h in range(2):
                    ins = mm(bank(2 + h), sel[0:3 * NPROJ, bass.ds(t * P + NST * P, P)],
                             bc_stack[0:3 * NPROJ, 512 * h:512 * h + 512], True, True)
                ins.then_inc(c_rdy, 1)

            def y_add(t, r, q, low):
                for e in range(ND):
                    pe.wait_ge(prod_done, 2 * t + e + 1)
                    for h in range(2):
                        ins = mm(bank(4 + 2 * e + h), ident[:, :], prod[:, e, 512 * h:512 * h + 512], False,
                                 low == NST - 1,
                                 skip_group_check=True)
                    ins.then_inc(prod_used, 1)

            run_steps(pe, NST, 2, [(0, bc), (1, y_add)])
            pe.wait_ge(dbu_done, 2 * NST)
            pe.wait_ge(c_sb, NST)
            pe.wait_ge(yz_done, 2)
            for b in range(NB):
                for h in range(2):
                    for e in range(ND):
                        ins = pe.transpose(bank(b)[:, h * DM + e * P:h * DM + (e + 1) * P],
                                           dtu[:, e, b * L + h * P:b * L + (h + 1) * P], ident[:, :])
                ins.then_inc(yT_ps, 1)
            pe.wait_ge(wabs_done, 1)
            mm(bank(7)[:, 0:2], ones[:, :], wsc[:, 0:2], True, True).then_inc(wsum_ps, 1)
            pe.wait_ge(w2_done, 1)
            for g in range(4):
                wait(pe, w2T_sb, g)
                for n in range(2):
                    for c in range(ND):
                        h = 2 * g + n
                        ins = pe.transpose(bank(6).bitcast(BF16)[:, n * DM + c * P:n * DM + (c + 1) * P],
                                           w2q[:, c, h * P:(h + 1) * P], identb[:, :])
                ins.then_inc(w2T_ps, 1)
            pe.wait_ge(w1_done, 1)
            pe.wait_ge(w2T_sb, 4)
            pe.wait_ge(x1_done, NB)
            for s in range(NT + 7):
                t = s - 1
                if 0 <= t < NT:
                    r = t % 2
                    pe.wait_ge(xn_done, t + 1)
                    wait(pe, r1_done, t)
                    for c in range(ND):
                        ins = pe.transpose(bank(0)[:, c * P:(c + 1) * P], xn[:, r, c * P:(c + 1) * P], ident[:, :])
                    ins.then_inc(xT_ps, 1)
                t = s - 2
                if 0 <= t < NT:
                    r = t % 2
                    pe.wait_ge(lo_done, t + 1)
                    wait(pe, relu_done, t - 1)
                    for h in range(2):
                        n = 0
                        for part in (xhi, xmid, xlo):
                            for c in range(ND):
                                ins = mm(bank(2 + 2 * r + h), part[:, r, c], w1q[:, c, 512 * h:512 * h + 512],
                                         n == 0, n == 5)
                                n += 1
                    ins.then_inc(h_ps, 1)
                t = s - 4
                if 0 <= t < NT:
                    r = t % 2
                    pe.wait_ge(qb_done, t + 1)
                    wait(pe, qT_sb, t)
                    for h in range(HID // P):
                        ins = pe.transpose(bank(6).bitcast(BF16)[:, h * P:(h + 1) * P], qb[:, r, h * P:(h + 1) * P],
                                           identb[:, :])
                    ins.then_inc(qT_ps, 1)
                    pe.wait_ge(qT_sb, t + 1)
                    wait(pe, x2_done, t)
                    for h in range(HID // P):
                        ins = mm(bank(7)[:, 0:DM], qT[:, r, h], w2T[:, h], h == 0, h == HID // P - 1)
                    ins.then_inc(o_ps, 1)
                t = s - 6
                if 0 <= t < NT:
                    r = t % 2
                    pe.wait_ge(xn3_done, t + 1)
                    wait(pe, xT3_sb, t)
                    for c in range(ND):
                        ins = pe.transpose(bank(1)[:, c * P:(c + 1) * P], xn3[:, r, c * P:(c + 1) * P], ident[:, :])
                    ins.then_inc(xT3_ps, 1)

            def q_proj(t, r, q, low):
                if r % 2:
                    return
                j = r // 2
                pe.wait_ge(ld_wq[j % 2], 16 * (NKV // 2 * q + j // 2 + 1))
                if low >= 2:
                    pe.wait_ge(q_sb, NKV * q + j)
                for uu in range(2):
                    for c in range(ND):
                        ins = mm(bank(6)[:, uu * L:(uu + 1) * L], wq_sb[:, j % 2, c, uu * HD:(uu + 1) * HD],
                                 xT[:, c, bass.ds(q * L, L)], c == 0, c == 1)
                ins.then_inc(q_ps, 1)

            def scores(t, r, q, low):
                j, uu = r // 2, r % 2
                pe.wait_ge(q_sb, NKV * q + j + 1)
                if low >= 2:
                    pe.wait_ge(smax_done, 2 * t - 2)
                for a in range(2):
                    ins = mm(bank(r % 2)[:, a * L:(a + 1) * L], qTh[:, j % 2, uu, a * P:(a + 1) * P],
                             kT[:, j, bass.ds(q * L, L)], True, True)
                ins.then_inc(s_ps, 1)

            def p_turn(t, r, q, low):
                pe.wait_ge(pn_done, t + 1)
                if low >= 2:
                    pe.wait_ge(pT_sb, t - 1)
                for a in range(2):
                    for c in range(2):
                        ins = pe.transpose(bank(2 + r % 2)[:, c * L + a * P:c * L + (a + 1) * P],
                                           Pn[:, r % 2, a, c * P:(c + 1) * P], ident[:, :])
                ins.then_inc(pT_ps, 1)

            def pv(t, r, q, low):
                j, uu = r // 2, r % 2
                pe.wait_ge(pT_sb, t + 1)
                pe.wait_ge(vb_done, NKV * q + j + 1)
                if low >= 1:
                    pe.wait_ge(att_sb, t)
                for c in range(2):
                    ins = mm(bank(4)[:, uu * L:(uu + 1) * L], vbuf[:, j % 2, c], pT[:, r % 2, c], c == 0, c == 1)
                ins.then_inc(pv_ps, 1)

            def att_out(t, r, q, low):
                if r % 2 == 0:
                    return
                j = r // 2
                pe.wait_ge(att_sb, t + 1)
                if low >= 2:
                    pe.wait_ge(x3_done, NKV * q + j)
                for a in range(2):
                    for uu in range(2):
                        ins = mm(bank(7)[:, a * DM:(a + 1) * DM], attT[:, j % 2, uu, a * P:(a + 1) * P],
                                 wo_sb[:, 2 * j + uu], uu == 0, uu == 1)
                ins.then_inc(ao_ps, 1)

            def r_turn(h, q, k):
                pe.wait_ge(rec_done, k + 1)
                if h == 1:
                    pe.wait_ge(rexp_done, k)
                for c in range(ND):
                    ins = pe.transpose(bank(5)[:, c * P:(c + 1) * P], rec[:, h, c * P:(c + 1) * P], ident[:, :])
                ins.then_inc(rT_ps, 1)

            def logits(h, q, k):
                pe.wait_ge(rT_sb, k + 1)
                for c in range(ND):
                    ins = mm(bank(5)[:, DM:DM + NE], xTr[:, c], gateT[:, c], c == 0, c == 1)
                ins.then_inc(lg_ps, 1)

            def positions(h, q, k):
                pe.wait_ge(fl_done, k + 1)
                pe.wait_ge(cum_done, k + 1)
                if h == 0:
                    pe.wait_ge(rexp_done, k + 2)
                else:
                    pe.wait_ge(pos_used, k)
                mm(bank(5)[:, DM + NE:DM + 2 * NE], tri[:, :], fl[:, h], True, False)
                mm(bank(5)[:, DM + NE:DM + 2 * NE], ones[:, :], cum, False, True).then_inc(pos_ps, 1)

            pe.wait_ge(xT3_sb, NT)
            pe.wait_ge(ld_wo, 16)
            run_units(pe, [(2, scores), (3, p_turn), (0, q_proj), (4, att_out),
                           tile_at(22, 0, r_turn), tile_at(23, 0, logits), tile_at(24, 1, r_turn),
                           tile_at(25, 1, logits), tile_at(26, 0, positions), tile_at(28, 1, positions), (3, pv)])

            def xg_turn(t, r, q, low):
                pe.wait_ge(xg_ld[r // 2], 16 * (q + 1))
                if low >= 2:
                    pe.wait_ge(xgT_sb, t - 1)
                for c in range(ND):
                    ins = pe.transpose(bank(r % 2)[:, c * P:(c + 1) * P], xg[:, r, c * P:(c + 1) * P], ident[:, :])
                ins.then_inc(xgT_ps, 1)

            def pair_at(t, r, low):
                return (t - r % 2 - (NSLOT if low >= NSLOT else 0)) * SLOTW

            def gate_up(t, r, q, low):
                if low >= NSLOT:
                    pe.wait_ge(w_ld[r // 2], 48 * (q - NSLOT // 8 + 1))
                pe.wait_ge(xgT_sb, t + 1)
                if low >= 2:
                    pe.wait_ge(h_done, t - 1)
                at = pair_at(t, r, low) + r % 2 * 2 * DM
                for c in range(ND):
                    ins = mm(bank(2 + r % 2)[:, 0:2 * FE], xgT[:, r % 2, c],
                             weights[:, bass.ds(at + c * 2 * FE, 2 * FE)], c == 0, c == 1)
                ins.then_inc(gu_ps, 1)

            def h_turn(t, r, q, low):
                pe.wait_ge(h_done, t + 1)
                if low >= 2:
                    pe.wait_ge(hT_sb, t - 1)
                pe.transpose(bank(4 + r % 2)[:, 0:CAP], hh[:, r % 2], ident[:, :]).then_inc(hT_ps, 1)

            def down(t, r, q, low):
                pe.wait_ge(hT_sb, t + 1)
                if low >= 2:
                    pe.wait_ge(ysb_done, t - 1)
                mm(bank(6 + r % 2)[:, 0:DM], hT[:, r % 2],
                   weights[:, bass.ds(pair_at(t, r, low) + 4 * DM + r % 2 * DM, DM)], True, True).then_inc(yd_ps, 1)

            pe.wait_ge(pos_used, NT)
            pe.wait_ge(ld_preA, 24 * PRE)
            pe.wait_ge(ld_preB, 24 * (NSLOT - PRE))
            run_steps(pe, NE, 8, [(0, xg_turn), (1, gate_up), (2, h_turn), (3, down)], cuts=(NSLOT,))

        @block.vector
        def _(dve):
            chain = [0]

            def link(ins):
                chain[0] += 1
                ins.then_inc(dve_chain, 1)
                dve.wait_ge(dve_chain, chain[0])

            dve.wait_ge(ld_x, 16)
            for t in range(NT):
                ins = dve.bn_stats(st6[:, t], xres[:, t, :])
            link(ins)
            for t in range(NT):
                ins = dve.bn_aggr(mv1[:, t], st6[:, t])
            ins.then_inc(ln1_stats, 1)
            dve.wait_ge(smallT_ps, 1)
            dve.tensor_copy(inT, bank(2)[:, 0:ND * P]).then_inc(smallT_sb, 1)
            dve.wait_ge(smallT_ps, 2)
            dve.tensor_copy(xpT.rearrange("p e k -> p (e k)"), bank(3)[:, 0:ND * NPROJ])
            dve.tensor_copy(dtpT[0:RANK, :], bank(3)[0:RANK, 128:384])
            dve.tensor_copy(gateT[:, :, :].rearrange("p e k -> p (e k)"), bank(3)[:, 384:384 + ND * NE]
                            ).then_inc(smallT_sb, 1)
            dve.wait_ge(ln1_rstd, 1)
            dve.scalar_tensor_tensor(out=nb1, in0=mv1[:, :, 0], scalar=-1.0, in1=rs1, op0=ALU.mult,
                                     op1=ALU.mult).then_inc(ln1_nb, 1)
            tap = lambda e, j: upad[:, e, :, j:j + L]
            cav = lambda e: conv_acc[:, e].rearrange("p (b l) -> p b l", b=NB)
            dve.wait_ge(ld_small, 16 * 3)
            dve.wait_ge(ld_vec, 16 * 5)
            dve.wait_ge(consts, 6)
            for e in range(ND):
                dve.wait_ge(upad_sb, 2 * e + 2)
                link(dve.tensor_scalar(cav(e), tap(e, NTAP - 1), cw[:, e, NTAP - 1:NTAP], cb[:, e:e + 1], ALU.mult,
                                       ALU.add))
                for j in range(NTAP - 1):
                    ins = dve.scalar_tensor_tensor(out=cav(e), in0=tap(e, j), scalar=cw[:, e, j:j + 1], in1=cav(e),
                                                   op0=ALU.mult, op1=ALU.add)
                    if j < NTAP - 2:
                        link(ins)
                ins.then_inc(conv_done, 1)
            dve.wait_ge(a_exp, 1)
            dve.tensor_scalar(aneg, aexp, -1.0, None, ALU.mult).then_inc(a_neg, 1)
            for e in range(ND):
                ins = dve.tensor_scalar(dskm[:, e], ident[:, :], dsk[:, e:e + 1], None, ALU.mult)
            ins.then_inc(dskm_done, 1)
            dve.wait_ge(xdbl_sb, 2)
            n = slice(0, NPROJ)
            dve.tensor_copy(bc_stack[n, :], xdbl[n, :]).then_inc(split_done, 1)
            dve.wait_ge(split_done, 1)
            link(dve.tensor_tensor(xdbl_r[n, :], xdbl[n, :], bc_stack[n, :], ALU.subtract))
            dve.tensor_copy(bc_mid[n, :], xdbl_r[n, :]).then_inc(split_done, 1)
            dve.wait_ge(split_done, 2)
            dve.tensor_tensor(bc_lo[n, :], xdbl_r[n, :], bc_mid[n, :], ALU.subtract).then_inc(split_done, 1)
            dve.wait_ge(split_done, 3)
            for e in range(ND):
                dve.wait_ge(act_sp, 5 + 2 * e)
                link(dve.tensor_scalar(sp_d[:, e], sp_z[:, e], 1.0, -1.0, ALU.add, ALU.add))
                link(dve.tensor_tensor(sp_d[:, e], sp_z[:, e], sp_d[:, e], ALU.subtract))
                dve.wait_ge(act_sp, 6 + 2 * e)
                link(dve.tensor_tensor(sp_d[:, e], sp_d[:, e], sp_l[:, e], ALU.add))
                dve.tensor_tensor(dt[:, e], dt[:, e], sp_d[:, e], ALU.add).then_inc(dt_done, 1)
                dve.wait_ge(dt_done, e + 1)
                link(dve.tensor_tensor(dtu[:, e], dt[:, e], u[:, e], ALU.mult))

            def dbu(t, r, q, low):
                dve.wait_ge(b_rdy, t + 1)
                for e in range(ND):
                    wait(dve, scan_done, 2 * t + e - 1 if low > 0 else 0)
                    dve.tensor_tensor(dBu[:, e], dtu[:, e], bank(0, 2), ALU.mult).then_inc(dbu_done, 1)

            def scan(t, r, q, low):
                for e in range(ND):
                    dve.wait_ge(dbu_done, 2 * t + e + 1)
                    dve.wait_ge(da_rdy, 2 * t + e + 1)
                    wait(dve, prod_done, 2 * t + e - 1 if low > 0 else 0)
                    dve.tensor_tensor_scan(hst[:, e], dA[:, e], dBu[:, e], 0.0, ALU.mult, ALU.add).then_inc(scan_done, 1)

            run_steps(dve, NST, 2, [(0, dbu), (0, scan)])
            dve.wait_ge(zs_done, NT)
            for e in range(ND):
                dve.wait_ge(prod_used, 2 * NST - 1 + e)
                dve.tensor_tensor(v2(dtu[:, e], NB), v2(bank(4 + 2 * e, 2), NB), zs[:, e:NT:2, :], ALU.mult
                                  ).then_inc(yz_done, 1)
            dve.wait_ge(ld_mlp, 32)
            for w in range(2):
                ins = dve.tensor_reduce(wsc[:, w:w + 1], wraw[:, w], AX.X, ALU.add, apply_absolute_value=True)
            ins.then_inc(wabs_done, 1)
            dve.wait_ge(tanh_done, 1)
            for b in range(NB):
                dve.wait_ge(yT_ps, b + 1)
                xv = xres[:, 2 * b:2 * b + 2, :].rearrange("p a d -> p (a d)")
                dve.scalar_tensor_tensor(out=xv, in0=bank(b), scalar=tg[:, 0:1], in1=xv, op0=ALU.mult,
                                         op1=ALU.add).then_inc(x1_done, 1)
            dve.wait_ge(wsum_ps, 1)
            link(dve.tensor_scalar(wsc[:, 2:4], bank(7)[:, 0:2], 1.0 / (DM * HID), EPS, ALU.mult, ALU.max))
            link(dve.reciprocal(wsc[:, 4:6], wsc[:, 2:4]))
            link(dve.tensor_tensor(wsc[:, 9:10], wsc[:, 2:3], wsc[:, 2:3], ALU.mult))
            link(dve.tensor_scalar(wsc[:, 6:7], wsc[:, 9:10], 255.0, None, ALU.mult))
            link(dve.tensor_tensor(wsc[:, 10:11], wsc[:, 3:4], tg[:, 2:3], ALU.mult))
            link(dve.tensor_scalar(wsc[:, 7:8], wsc[:, 10:11], 1.0 / 255.0, None, ALU.mult))
            link(dve.memset(wsc[:, 8:9], ROUND))
            for w, dst, signal in ((1, w2q, w2_done), (0, w1q, w1_done)):
                link(dve.tensor_scalar(wraw[:, w], wraw[:, w], wsc[:, 4 + w:5 + w], None, ALU.mult))
                link(dve.tensor_scalar(wneg, wraw[:, w], -0.5, None, ALU.is_lt))
                dve.scalar_tensor_tensor(out=dst.rearrange("p c h -> p (c h)"), in0=wraw[:, w], scalar=0.5,
                                         in1=wneg, op0=ALU.is_gt, op1=ALU.subtract).then_inc(signal, 1)
            dve.wait_ge(w1_done, 1)

            for s in range(NT + 7):
                t = s - 1
                if 0 <= t < NT:
                    r = t % 2
                    dve.wait_ge(rstd_done, t + 1)
                    wait(dve, xT_ps, t - 1)
                    dve.tensor_scalar(xn[:, r], xres[:, t, :], mvf[:, 2 * r:2 * r + 1], rsf[:, r:r + 1], ALU.subtract,
                                      ALU.mult).then_inc(xn_done, 1)
                t = s
                if t < NT:
                    r = t % 2
                    link(dve.bn_stats(stf[:, 8 * r:8 * r + 6], xres[:, t, :]))
                    wait(dve, xn_done, t - 1)
                    dve.bn_aggr(mvf[:, 2 * r:2 * r + 2], stf[:, 8 * r:8 * r + 6]).then_inc(st_done, 1)
                t = s - 1
                if 0 <= t < NT:
                    r = t % 2
                    dve.wait_ge(hi_done, t + 1)
                    wait(dve, mid_done, t - 1)
                    dve.tensor_tensor(xr1[:, r], bank(0)[:, 0:DM], xhi[:, r].rearrange("p c t -> p (c t)"),
                                      ALU.subtract).then_inc(r1_done, 1)
                t = s - 3
                if 0 <= t < NT:
                    r = t % 2
                    v = lambda k: sml[:, 8 * r + k:8 * r + k + 1]
                    dve.wait_ge(relu_done, t + 1)
                    wait(dve, qf_done, t - 1)
                    link(dve.tensor_reduce(v(0), rl[:, r], AX.X, ALU.max))
                    link(dve.tensor_tensor(v(1), v(0), v(0), ALU.mult))
                    link(dve.tensor_scalar(v(1), v(1), wsc[:, 9:10], EPS, ALU.mult, ALU.max))
                    link(dve.reciprocal(v(2), v(1)))
                    wait(dve, x2_done, t - 1)
                    dve.tensor_scalar(v(4), v(1), wsc[:, 7:8], None, ALU.mult)
                    dve.tensor_scalar(v(3), v(2), wsc[:, 6:7], None, ALU.mult).then_inc(rs_done, 1)
                t = s - 1
                if 0 <= t < NT:
                    r = t % 2
                    dve.wait_ge(mid_done, t + 1)
                    wait(dve, h_ps, t - 1)
                    dve.tensor_tensor(xlo[:, r].rearrange("p c t -> p (c t)"), xr1[:, r],
                                      xmid[:, r].rearrange("p c t -> p (c t)"), ALU.subtract).then_inc(lo_done, 1)
                t = s - 3
                if 0 <= t < NT:
                    r = t % 2
                    dve.wait_ge(qf_done, t + 1)
                    wait(dve, qT_ps, t - 1)
                    dve.tensor_scalar(qb[:, r], qf[:, r], -ROUND, None, ALU.add).then_inc(qb_done, 1)
                t = s - 4
                if 0 <= t < NT:
                    r = t % 2
                    dve.wait_ge(o_ps, t + 1)
                    dve.scalar_tensor_tensor(out=xres[:, t, :], in0=bank(7)[:, 0:DM], scalar=sml[:, 8 * r + 4:8 * r + 5],
                                             in1=xres[:, t, :], op0=ALU.mult, op1=ALU.add).then_inc(x2_done, 1)
                t = s - 5
                if 0 <= t < NT:
                    r = t % 2
                    dve.wait_ge(x2_done, t + 1)
                    link(dve.bn_stats(st3[:, 8 * r:8 * r + 6], xres[:, t, :]))
                    dve.bn_aggr(mv3[:, 2 * r:2 * r + 2], st3[:, 8 * r:8 * r + 6]).then_inc(st3_done, 1)
                    dve.wait_ge(rstd3_done, t + 1)
                    wait(dve, xT3_ps, t - 1)
                    dve.tensor_scalar(xn3[:, r], xres[:, t, :], mv3[:, 2 * r:2 * r + 1], rs3[:, r:r + 1],
                                      ALU.subtract, ALU.mult).then_inc(xn3_done, 1)

            dve.wait_ge(ld_mask, 16)
            link(dve.tensor_scalar(maskb.rearrange("p b s -> p (b s)"), mask_sb, -1.0, 1e30, ALU.add, ALU.mult))
            link(dve.tensor_reduce(valid, maskb, AX.X, ALU.max))
            link(dve.tensor_scalar(valid, valid, -1.0, None, ALU.is_gt))

            dve.memset(cum, 0.0).then_inc(cum_done, 1)
            dve.wait_ge(consts, NCONST)

            def smax(t, r, q, low):
                r2 = r % 2
                if r == 0:
                    if low >= 2:
                        dve.wait_ge(smax_done, 2 * t)
                    dve.tensor_copy(mask_now, maskb[:, bass.ds(q, 1)].rearrange("p a s -> p (a s)")).then_inc(mask_done, 1)
                    dve.wait_ge(mask_done, q + 1)
                dve.wait_ge(s_ps, t + 1)
                if low >= 2:
                    dve.wait_ge(exp_done, 2 * t - 2)
                dve.sem_inc(smax_go, 1)
                for a in range(2):
                    dve.tensor_tensor_reduce(sm[:, r2, a], bank(r2)[:, a * L:(a + 1) * L], mask_now, 1.0, -3e38,
                                             ALU.add, ALU.max, mx[:, r2, a:a + 1]).then_inc(smax_done, 1)
                dve.wait_ge(smax_done, 2 * t + 2)
                dve.tensor_scalar(nm[:, r2], mx[:, r2], -(HD ** -0.5), None, ALU.mult).then_inc(nm_done, 1)

            def pT_evac(t, r, q, low):
                dve.wait_ge(pT_ps, t + 1)
                if low >= 2:
                    dve.wait_ge(pv_ps, t - 1)
                dve.tensor_copy(pT[:, r % 2].rearrange("p a s -> p (a s)"), bank(2 + r % 2)).then_inc(pT_sb, 1)

            def recips(t, r, q, low):
                r2 = r % 2
                dve.wait_ge(exp_done, 2 * t + 2)
                if low >= 2:
                    dve.wait_ge(pn_done, t - 1)
                dve.reciprocal(rc[:, r2], sume[:, r2]).then_inc(rc_raw, 1)
                dve.wait_ge(rc_raw, t + 1)
                dve.tensor_scalar(rc[:, r2], rc[:, r2], valid[:, bass.ds(q, 1)], None, ALU.mult).then_inc(rc_done, 1)

            def x3(t, r, q, low):
                if r % 2 == 0:
                    return
                j = r // 2
                dve.wait_ge(ao_ps, NKV * q + j + 1)
                if low >= 2:
                    dve.wait_ge(x3_done, NKV * q + j)
                xv = xres[:, bass.ds(2 * q, 2), :].rearrange("p a d -> p (a d)")
                dve.scalar_tensor_tensor(out=xv, in0=bank(7), scalar=tg[:, 1:2], in1=xv, op0=ALU.mult,
                                         op1=ALU.add).then_inc(x3_done, 1)

            LINKS = 24
            links = [0]

            def rlink(q, ins):
                links[0] += 1
                ins.then_inc(route_chain, 1)
                dve.wait_ge(route_chain, LINKS * q + links[0])

            xk = lambda k: xres[:, bass.ds(k, 1), :].rearrange("p a d -> p (a d)")

            def stats4(h, q, k):
                if h == 0:
                    links[0] = 0
                dve.wait_ge(rec_free, q + 1)
                dve.wait_ge(x3_done, NKV * (q + 1))
                dve.sem_inc(route_go, 1)
                rlink(q, dve.bn_stats(rst[:, h], xk(k)))
                dve.sem_inc(route_go, 1)
                dve.bn_aggr(rmv[:, h, 0:2], rst[:, h]).then_inc(st4_done, 1)

            def norm4(h, q, k):
                dve.wait_ge(rstd4_done, k + 1)
                dve.tensor_copy(rec[:, h, REC - 1:REC], tok8[:, bass.ds(k, 1)])
                dve.tensor_scalar(rec[:, h, 0:DM], xk(k), rmv[:, h, 0:1], rmv[:, h, 2:3], ALU.subtract, ALU.mult
                                  ).then_inc(rec_done, 1)

            def rmax(h, q, k):
                dve.wait_ge(lg_ps, k + 1)
                dve.tensor_reduce(rsm[:, h, 0:1], bank(5)[:, DM:DM + NE], AX.X, ALU.max, negate=True
                                  ).then_inc(rmax_done, 1)

            def choose(h, q, k):
                top_i, top_w = rec[:, h, DM:DM + TOPK], rec[:, h, DM + TOPK:DM + 2 * TOPK]
                dve.wait_ge(rexp_done, k + 1)
                rlink(q, dve.reciprocal(rsm[:, h, 2:3], rsm[:, h, 1:2]))
                rlink(q, dve.tensor_scalar(rp[:, h], rp[:, h], rsm[:, h, 2:3], None, ALU.mult))
                dve.sem_inc(route_go, 1)
                rlink(q, dve.max(top_w, rp[:, h]))
                dve.sem_inc(route_go, 1)
                rlink(q, dve.max_index(idxu[:, h], top_w, rp[:, h]))
                rlink(q, dve.tensor_copy(top_i, idxu[:, h]))

            def one_hot(h, q, k):
                top_i = rec[:, h, DM:DM + TOPK]
                rlink(q, dve.tensor_tensor(v2(oh[:, h], TOPK), iota_e[:, :].unsqueeze(1).to_broadcast([P, TOPK, NE]),
                                           top_i.unsqueeze(2).to_broadcast([P, TOPK, NE]), ALU.is_equal))
                dve.tensor_reduce(fl[:, h], oh[:, h].rearrange("p (k e) -> p e k", k=TOPK), AX.X, ALU.add
                                  ).then_inc(fl_done, 1)

            def place(h, q, k):
                dve.wait_ge(pos_ps, k + 1)
                dve.tensor_tensor(v2(ohp, TOPK), v2(oh[:, h], TOPK),
                                  bank(5)[:, DM + NE:DM + 2 * NE].unsqueeze(1).to_broadcast([P, TOPK, NE]), ALU.mult
                                  ).then_inc(pos_used, 1)
                dve.wait_ge(fl_done, k + 1)
                dve.tensor_tensor(cum, cum, fl[:, h], ALU.add).then_inc(cum_done, 1)
                dve.wait_ge(pos_used, k + 1)
                rlink(q, dve.tensor_reduce(posk, v2(ohp, TOPK), AX.X, ALU.add))

            def slots(h, q, k):
                drop = drop_row[:, bass.ds(k * TOPK, TOPK)]
                rlink(q, dve.scalar_tensor_tensor(out=locf, in0=rec[:, h, DM:DM + TOPK], scalar=float(CAP), in1=posk,
                                                  op0=ALU.mult, op1=ALU.add))
                rlink(q, dve.tensor_tensor(loc2, locf, drop, ALU.subtract))
                rlink(q, dve.scalar_tensor_tensor(out=locf, in0=posk, scalar=float(CAP), in1=loc2, op0=ALU.is_lt,
                                                  op1=ALU.mult))
                rlink(q, dve.tensor_tensor(loc[:, h], locf, drop, ALU.add))
                dve.sem_inc(loc_done, 1)

            run_units(dve, [(2, smax), (3, pT_evac), (2, recips),
                            tile_at(20, 0, stats4), tile_at(21, 0, norm4), tile_at(21, 1, stats4),
                            tile_at(22, 1, norm4), tile_at(23, 0, rmax), tile_at(24, 0, choose),
                            tile_at(25, 1, rmax), tile_at(25, 0, one_hot), tile_at(26, 0, place), tile_at(26, 1, choose),
                            tile_at(27, 0, slots), tile_at(27, 1, one_hot), tile_at(28, 1, place),
                            tile_at(29, 1, slots), (4, x3)])

            def rows(t, r, q, low):
                ru = r % 2
                top_i, top_w = xg[:, r, DM:DM + TOPK], xg[:, r, DM + TOPK:DM + 2 * TOPK]
                me = iota_e[:, bass.ds(t, 1)]
                dve.wait_ge(xg_ld[r // 2], 16 * (q + 1))
                if low >= 8:
                    dve.wait_ge(scattered[r % 4], 16 * (2 * q + r // 4 - 1))
                    dve.wait_ge(ysb_done, t - 7)
                if low >= 2:
                    dve.wait_ge(msc1, 2 * t - 2)
                dve.scalar_tensor_tensor(out=junk[:, ru, 0:8], in0=top_i, scalar=me, in1=top_w, op0=ALU.is_equal,
                                         op1=ALU.mult, accum_out=wsl[:, r]).then_inc(msc1, 1)
                dve.scalar_tensor_tensor(out=junk[:, ru, 8:16], in0=top_i, scalar=me, in1=rank1[:, :],
                                         op0=ALU.is_equal, op1=ALU.mult, accum_out=msc[:, r, 0:1]).then_inc(msc1, 1)
                dve.wait_ge(msc1, 2 * t + 2)
                dve.scalar_tensor_tensor(out=msc[:, r, 1:2], in0=msc[:, r, 0:1], scalar=0.0,
                                         in1=empty_row[:, bass.ds(t, 1)], op0=ALU.is_equal, op1=ALU.mult
                                         ).then_inc(msc2, 1)
                dve.wait_ge(msc2, t + 1)
                dve.scalar_tensor_tensor(out=row[:, r], in0=xg[:, r, REC - 1:REC], scalar=msc[:, r, 0:1],
                                         in1=msc[:, r, 1:2], op0=ALU.add, op1=ALU.add).then_inc(row_done, 1)

            def gated(t, r, q, low):
                dve.wait_ge(sil_done, t + 1)
                if low >= 2:
                    dve.wait_ge(hT_ps, t - 1)
                dve.tensor_tensor(hh[:, r % 2], sil[:, r % 2], bank(2 + r % 2)[:, FE:2 * FE], ALU.mult
                                  ).then_inc(h_done, 1)

            def weigh(t, r, q, low):
                dve.wait_ge(yd_ps, t + 1)
                dve.wait_ge(row_done, t + 1)
                dve.tensor_scalar(ysb[:, r], bank(6 + r % 2)[:, 0:DM], wsl[:, r], None, ALU.mult).then_inc(ysb_done, 1)

            run_steps(dve, NE, 8, [(1, gated), (2, rows), (3, weigh)])

            for t in range(NT):
                dve.wait_ge(yk_ld[t % 4], 16 * (t // 4 + 1))
                dve.tensor_reduce(ysum[:, t % 2], yall[:, t % 4].rearrange("p (k d) -> p d k", k=TOPK), AX.X, ALU.add
                                  ).then_inc(ysum_done, 1)
                dve.wait_ge(ysum_done, t + 1)
                dve.scalar_tensor_tensor(out=xres[:, t, :], in0=ysum[:, t % 2], scalar=tg[:, 3:4], in1=xres[:, t, :],
                                         op0=ALU.mult, op1=ALU.add).then_inc(out_done, 1)



_INS = ['x', 'ctx_1024', 'mask_BxS2_bf1', 'g_xattn', 'g_ffn', 'L0_xattn_in_proj_w', 'L0_xattn_conv_w',
        'L0_xattn_conv_b', 'L0_xattn_x_proj_w', 'L0_xattn_dt_proj_w', 'L0_xattn_dt_proj_b', 'L0_xattn_A_log',
        'L0_xattn_D', 'L0_ffn_c_fc', 'L0_ffn_c_proj', 'L1_xattn_Wq', 'L1_xattn_Wk', 'L1_xattn_Wv', 'L1_xattn_Wo',
        'L1_ffn_gate_w', 'L1_ffn_w_gate', 'L1_ffn_w_up', 'L1_ffn_w_down']


def kernel(**inputs):
    import numpy as _np
    import concourse.bacc as _bacc
    from concourse import mybir as _mybir
    from concourse.bass_utils import run_bass_kernel_spmd as _run

    nc = _bacc.Bacc("TRN2", target_bir_lowering=False, num_devices=1)
    arrays, args = {}, []
    for name in _INS:
        a = _np.ascontiguousarray(inputs[name])
        arrays[f"in_{name}"] = a
        args.append(nc.dram_tensor(f"in_{name}", a.shape, _mybir.dt.from_np(a.dtype), kind="ExternalInput").ap())
    args.append(nc.dram_tensor("out_0", (NB, L, DM), F32, kind="ExternalOutput").ap())
    flamingo_kernel(nc, *args)
    r = _run(nc, [arrays], core_ids=[0])
    return r.results[0]["out_0"]
```

```python
from contextlib import ExitStack

import concourse.bass as bass
from concourse import mybir

F32 = mybir.dt.float32
BF16 = mybir.dt.bfloat16
U32 = mybir.dt.uint32
U8 = mybir.dt.uint8
ALU = mybir.AluOpType
ACT = mybir.ActivationFunctionType
AX = mybir.AxisListType

P = 128
NB, L, DM = 4, 256, 256
NT = NB * L // P
T = NB * L
DC = 128
ND = 2
NST, NTAP, RANK = 16, 4, 8
NPROJ = RANK + 2 * NST
HID = 1024
NH, NKV, HD = 16, 8, 128
NE, TOPK, CAP, FE = 64, 8, 128, 128
REC = DM + 2 * TOPK + 1
EPS = 1e-5
ROUND = 12582912.0
SLOTW = 3 * DM
NSLOT = 32
PRE = 10
PREV = 8
NMORE = 16
WCOLS = NSLOT * SLOTW
KVCOL = WCOLS - 2 * NKV * T


def wait(eng, sem, value):
    if isinstance(value, int) and value <= 0:
        return
    eng.wait_ge(sem, value)


def run_steps(eng, count, unroll, stages, cuts=(), first=None):
    depth = max(lag for lag, _ in stages)

    def straight(steps):
        for s in steps:
            for lag, fn in stages:
                t = s - lag
                if 0 <= t < count:
                    fn(t, t % unroll, t // unroll, t)

    up = lambda n: -(-n // unroll) * unroll
    at = 0
    for end in (*cuts, count):
        head = min(first if first is not None else at + up(depth + (unroll if at == 0 else 0)), end)
        straight(range(at, head))
        if head < end:
            with eng.Fori(0, (end - head) // unroll) as i:
                for base in range(head, end, 1)[:unroll]:
                    for lag, fn in stages:
                        r = (base - lag) % unroll
                        fn(i * unroll + (base - lag), r, i + (base - lag - r) // unroll, base - lag)
        at = end
    straight(range(count, count + depth))


def flamingo_kernel(
    nc, x, ctx_tokens, mask, g_xattn, g_ffn, in_proj_w, conv_w, conv_b, x_proj_w, dt_proj_w, dt_proj_b,
    A_log, D_skip, c_fc, c_proj, Wq, Wk, Wv, Wo, gate_w, w_gate, w_up, w_down, out,
):
    stack = ExitStack()
    with stack:
        sem = lambda name: stack.enter_context(nc.semaphore(name))
        sbuf = lambda name, shape, dt=F32: stack.enter_context(nc.sbuf_tensor(name, shape, dt))

        NREC = NE * CAP
        xg_dram = nc.dram_tensor("dispatched", [NREC + T * TOPK, REC], F32, kind="Internal").ap()
        yk_dram = nc.dram_tensor("expert_out", [T * TOPK + NREC, DM], F32, kind="Internal").ap()

        ident = sbuf("ident", [P, P])
        identb = sbuf("identb", [P, P], BF16)
        tri = sbuf("tri", [P, P])
        ones = sbuf("ones", [P, P])
        iota_e = sbuf("iota_e", [P, NE])
        rank1 = sbuf("rank1", [P, TOPK])
        drop_row = sbuf("drop_row", [P, NT * TOPK])
        empty_row = sbuf("empty_row", [P, NE])
        tok8 = sbuf("tok8", [P, NT])
        nhalf = sbuf("nhalf", [P, 8])
        gates = sbuf("gates", [P, 4])
        tg = sbuf("tg", [P, 4])
        xres = sbuf("xres", [P, NT, DM])
        gateT = sbuf("gateT", [P, ND, NE])
        weights = sbuf("weights", [P, WCOLS])
        vS = weights[:, KVCOL:KVCOL + NKV * T].rearrange("p (s c) -> p s c", s=NT)
        kT = weights[:, KVCOL + NKV * T:WCOLS].rearrange("p (j t) -> p j t", j=NKV)
        NTMP = 23000
        NTAIL = 2700
        tmp = sbuf("tmp", [P, NTMP])

        def carver(area, size):
            at = [0]

            def take(cols, dt=F32, parts=P):
                n = cols if dt in (F32, U32) else (cols + 1) // 2 if dt == BF16 else (cols + 3) // 4
                a = at[0]
                at[0] += n
                assert at[0] <= size, (at[0], size)
                v = area[0:parts, a:a + n]
                return v if dt == F32 else v.bitcast(dt)

            return take

        v2 = lambda ap, a: ap.rearrange("p (a b) -> p a b", a=a)

        mw = carver(weights, KVCOL)
        mt = carver(tmp, NTMP)
        conv_acc = v2(mw(ND * T), ND)
        dA = conv_acc
        sp_z = v2(mw(ND * T), ND)
        dBu = sp_z
        sp_d = v2(mw(ND * T), ND)
        hst = sp_d
        sp_l = v2(mw(ND * T), ND)
        prod = sp_l
        upad = mt(ND * NB * (L + NTAP - 1)).rearrange("p (e b l) -> p e b l", e=ND, b=NB)
        xdbl = mt(T)
        ctxn = v2(mt(NT * DC), NT)
        wk_sb = mt(NKV * HD)
        wv_sb = mt(NKV * HD)
        ctxT = mt(T)
        u = v2(mt(ND * T), ND)
        dt = v2(mt(ND * T), ND)
        dtu = v2(mt(ND * T), ND)
        zs = v2(mt(NT * DM), NT)
        sel = mt(2 * NST * P, BF16)
        bc_stack = mt(T, BF16)
        bc_mid = mt(T, BF16)
        bc_lo = mt(T, BF16)
        xdbl_r = sp_d[:, 0]
        in_n = v2(mt(ND * DC), ND)
        inT = mt(ND * P)
        xp_n = mt(DM)
        xpT = v2(mt(ND * NPROJ), ND)
        dtp_n = v2(mt(ND * RANK), ND)
        dtpT = mt(ND * P)
        gate_n = mt(DM)
        cw = v2(mt(ND * NTAP), ND)
        cb = mt(ND)
        dtb = mt(ND)
        dsk = mt(ND)
        dskm = v2(mt(ND * P), ND)
        alog = v2(mt(ND * NST), ND)
        aneg = v2(mt(ND * NST), ND)
        st6 = v2(mt(NT * 6), NT)
        mv1 = v2(mt(NT * 2), NT)
        rs1 = mt(NT)
        nb1 = mt(NT)
        aexp = v2(mt(ND * NST), ND)
        csb = v2(mt(2 * T), 2)

        ft = carver(tmp, NTMP - NTAIL)
        wraw = v2(ft(2 * ND * HID), 2)
        wneg = ft(ND * HID, BF16)
        ft(NKV * HD + T + 64)
        xn = v2(ft(2 * DM), 2)
        xhi = ft(2 * DM, BF16).rearrange("p (r c t) -> p r c t", r=2, c=ND)
        xmid = ft(2 * DM, BF16).rearrange("p (r c t) -> p r c t", r=2, c=ND)
        xlo = ft(2 * DM, BF16).rearrange("p (r c t) -> p r c t", r=2, c=ND)
        xr1 = v2(ft(2 * DM), 2)
        rl = v2(ft(2 * HID), 2)
        sq = v2(ft(2 * HID), 2)
        qf = v2(ft(2 * HID), 2)
        qb = v2(ft(2 * HID, BF16), 2)
        qT = ft(2 * HID, BF16).rearrange("p (r h t) -> p r h t", r=2, h=HID // P)
        w1q = v2(ft(ND * HID, BF16), ND)
        w2q = v2(rl[:, 0].bitcast(BF16), ND)
        w2T = v2(ft(HID // P * DM, BF16), HID // P)
        stf, mvf, rsf, sml, wsc = ft(16), ft(8), ft(4), ft(32), ft(16)
        tail = carver(tmp[:, NTMP - NTAIL:NTMP], NTAIL)
        xT = v2(tail(ND * T), ND)
        xn3 = v2(tail(2 * DM), 2)
        st3, mv3, rs3 = tail(16), tail(8), tail(4)

        ab = carver(tmp, NTMP - NTAIL)
        rec = v2(ab(2 * REC), 2)
        xTr = v2(ab(DM), ND)
        rp = v2(ab(2 * NE), 2)
        oh = v2(ab(2 * TOPK * NE), 2)
        ohp = ab(TOPK * NE)
        fl = v2(ab(2 * NE), 2)
        cum = ab(NE)
        idxu = v2(ab(2 * TOPK, U32), 2)
        posk = ab(TOPK)
        locf = ab(TOPK)
        loc2 = ab(TOPK)
        loc = v2(ab(2 * TOPK, U32), 2)
        rst = v2(ab(2 * 6), 2)
        rmv = v2(ab(2 * 4), 2)
        rsm = v2(ab(2 * 4), 2)
        vbuf = ab(2 * 2 * HD).rearrange("p (m s d) -> p m s d", m=2, s=2)
        Pn = ab(2 * 512).rearrange("p (r a s) -> p r a s", r=2, a=2)
        qTh = ab(2 * 2 * L).rearrange("p (m u t) -> p m u t", m=2, u=2)
        sm = ab(2 * 512).rearrange("p (r a s) -> p r a s", r=2, a=2)
        pe_ = ab(2 * 512).rearrange("p (r a s) -> p r a s", r=2, a=2)
        pT = ab(2 * 512).rearrange("p (r a s) -> p r a s", r=2, a=2)
        attT = ab(4 * L).rearrange("p (m u t) -> p m u t", m=2, u=2)
        wo_sb = v2(ab(NH * DM), NH)
        mx, nm, sume, rc = v2(ab(4), 2), v2(ab(4), 2), v2(ab(4), 2), v2(ab(4), 2)
        maskb = v2(ab(NB * L), NB)
        mask_now = ab(L)
        valid = ab(NB)

        ra = carver(tmp, NTMP - NMORE * SLOTW)

        def place_of(e, low):
            if NSLOT <= low < NSLOT + NMORE:
                return tmp[:, bass.ds((e - NSLOT) * SLOTW + NTMP - NMORE * SLOTW, 2 * SLOTW)]
            return weights[:, bass.ds((e - (NSLOT + NMORE if low >= NSLOT + NMORE else 0)) * SLOTW, 2 * SLOTW)]

        xg = v2(ra(8 * REC), 8)
        xgT = ra(2 * DM).rearrange("p (r c t) -> p r c t", r=2, c=ND)
        sil = v2(ra(2 * FE), 2)
        hh = v2(ra(2 * FE), 2)
        hT = v2(ra(2 * CAP), 2)
        ysb = v2(ra(8 * DM), 8)
        wsl = v2(ra(8), 8)
        msc = v2(ra(8 * 2), 8)
        junk = v2(ra(2 * 16), 2)
        row = v2(ra(8, U32), 8)
        yall = v2(weights[:, 0:4 * TOPK * DM], 4)
        ysum = v2(ra(2 * DM), 2)
        initrec = sbuf("initrec", [P, REC])
        zeros = sbuf("zeros", [P, 1024])
        wq_sb = zeros[:, :].rearrange("p (m c d) -> p m c d", m=2, c=ND)
        mask_sb = initrec[:, 0:NB * L // 4].bitcast(U8)

        ps = stack.enter_context(nc.psum_tensor("ps", [P, 8 * 512], F32))
        bank = lambda k, n=1: ps[:, 512 * k:512 * (k + n)]

        ld_ctx, ld_small, ld_x, ld_kv = sem("ld_ctx"), sem("ld_small"), sem("ld_x"), sem("ld_kv")
        ld_vec = sem("ld_vec")
        ld_gates, ld_mask, ld_mlp = sem("ld_gates"), sem("ld_mask"), sem("ld_mlp")
        ld_wo, ld_preA, ld_preB, ld_more = sem("ld_wo"), sem("ld_preA"), sem("ld_preB"), sem("ld_more")
        init_done = sem("init_done")
        consts, sel_done = sem("consts"), sem("sel_done")
        tanh_done = sem("tanh_done")
        ctxT_ps, smallT_ps, ctxT_sb, smallT_sb = sem("ctxT_ps"), sem("smallT_ps"), sem("ctxT_sb"), sem("smallT_sb")
        xin_ps, upad_sb, conv_done, u_sb = sem("xin_ps"), sem("upad_sb"), sem("conv_done"), sem("u_sb")
        xdbl_ps, xdbl_sb, split_done, stacked = sem("xdbl_ps"), sem("xdbl_sb"), sem("split_done"), sem("stacked")
        dt_ps, sp_done, dt_done = sem("dt_ps"), sem("sp_done"), [sem("dt_done0"), sem("dt_done1")]
        act_sp = sem("act_sp")
        a_exp, a_neg, dskm_done = sem("a_exp"), sem("a_neg"), sem("dskm_done")
        ln1_stats, ln1_rstd, ln1_nb, zs_done = sem("ln1_stats"), sem("ln1_rstd"), sem("ln1_nb"), sem("zs_done")
        kv_ps, kv_act, kv_dve = sem("kv_ps"), sem("kv_act"), sem("kv_dve")
        b_rdy, dbu_done, da_rdy, c_rdy, c_sb = sem("b_rdy"), sem("dbu_done"), sem("da_rdy"), sem("c_rdy"), sem("c_sb")
        scan_done, prod_done, prod_used = sem("scan_done"), sem("prod_done"), sem("prod_used")
        yz_done, yT_ps, x1_done = sem("yz_done"), sem("yT_ps"), sem("x1_done")
        dve_chain, pool_chain = sem("dve_chain"), sem("pool_chain")
        scale_done, wround_done = sem("scale_done"), sem("wround_done")
        wabs_done, wsum_ps, w1_done, w2_done, w2T_ps, w2T_sb = (sem("wabs_done"), sem("wsum_ps"), sem("w1_done"),
                                                                 sem("w2_done"), sem("w2T_ps"), sem("w2T_sb"))
        st_done, rstd_done, xn_done, xT_ps, hi_done, r1_done = (sem("st_done"), sem("rstd_done"), sem("xn_done"),
                                                                sem("xT_ps"), sem("hi_done"), sem("r1_done"))
        mid_done, lo_done, h_ps, relu_done, sq_done, rs_done = (sem("mid_done"), sem("lo_done"), sem("h_ps"),
                                                                sem("relu_done"), sem("sq_done"), sem("rs_done"))
        qf_done, qb_done, qT_ps, qT_sb, o_ps, x2_done = (sem("qf_done"), sem("qb_done"), sem("qT_ps"),
                                                         sem("qT_sb"), sem("o_ps"), sem("x2_done"))
        st3_done, rstd3_done, xn3_done, xT3_ps, xT3_sb = (sem("st3_done"), sem("rstd3_done"), sem("xn3_done"),
                                                          sem("xT3_ps"), sem("xT3_sb"))
        mask_done = sem("mask_done")
        q_ps, q_sb, vb_done = sem("q_ps"), sem("q_sb"), sem("vb_done")
        s_ps, smax_done, nm_done, exp_done, rc_done = (sem("s_ps"), sem("smax_done"), sem("nm_done"),
                                                       sem("exp_done"), sem("rc_done"))
        pn_done, pT_ps, pT_sb, pv_ps, att_sb, ao_ps, x3_done = (sem("pn_done"), sem("pT_ps"), sem("pT_sb"),
                                                                sem("pv_ps"), sem("att_sb"), sem("ao_ps"), sem("x3_done"))
        rc_raw, dve_go, pool_go = sem("rc_raw"), sem("dve_go"), sem("pool_go")
        ld_wq = [sem("ld_wq0"), sem("ld_wq1")]
        st4_done, rstd4_done, rec_done = sem("st4_done"), sem("rstd4_done"), sem("rec_done")
        rT_ps, rT_sb, lg_ps, rmax_done, rexp_done = (sem("rT_ps"), sem("rT_sb"), sem("lg_ps"),
                                                     sem("rmax_done"), sem("rexp_done"))
        fl_done, pos_ps, pos_used, loc_done, dispatched = (sem("fl_done"), sem("pos_ps"), sem("pos_used"),
                                                           sem("loc_done"), sem("dispatched"))
        route_chain, rstd4_sum, cum_done, rec_free = (sem("route_chain"), sem("rstd4_sum"), sem("cum_done"),
                                                      sem("rec_free"))
        xg_ld = [sem(f"xg_ld{r}") for r in range(4)]
        w_ld = [sem(f"w_ld{r}") for r in range(2)]
        scattered = [sem(f"scattered{r}") for r in range(4)]
        xgT_ps, xgT_sb, gu_ps, sil_done, h_done = (sem("xgT_ps"), sem("xgT_sb"), sem("gu_ps"), sem("sil_done"),
                                                   sem("h_done"))
        hT_ps, hT_sb, yd_ps, ysb_done = sem("hT_ps"), sem("hT_sb"), sem("yd_ps"), sem("ysb_done")
        msc1, msc2, row_done = sem("msc1"), sem("msc2"), sem("row_done")
        yk_ld = [sem(f"yk_ld{r}") for r in range(4)]
        ysum_done, out_done, stored = sem("ysum_done"), sem("out_done"), sem("stored")

        block = stack.enter_context(nc.Block())

        NCONST = 18

        NKVG = 2 * NKV * T // 512
        KV_DVE = range(10, 17)

        def wait_kv(eng, g):
            by_dve = sum(i in KV_DVE for i in range(g + 1))
            wait(eng, kv_dve, by_dve)
            wait(eng, kv_act, g + 1 - by_dve)

        def kv_place(g):
            n, h = (g % 16) // 2, g % 2
            at = 2 + g % 2 if g < 19 else 2 - g % 2 if g < 23 else 4 + g % 2 if g < 26 else 1
            return (kT if g < 16 else vS)[:, n, 512 * h:512 * h + 512], bank(at)

        NU = 2 * NKV
        run_units = lambda eng, stages: run_steps(eng, NB * NU, NU, stages, first=NU)

        def tile_at(step, h, fn):
            return step - h, lambda t, r, q, low: fn(h, q, 2 * q + h) if r == h else None

        @block.sync
        def _(sp):
            sp.dma_start(ctxn, ctx_tokens.rearrange("b (h p) c -> p (b h) c", p=P)).then_inc(ld_ctx, 16)
            sp.dma_start(in_n, in_proj_w.rearrange("(e p) c -> p e c", p=P)).then_inc(ld_ctx, 16)
            sp.dma_start(xres[:, :, :], x.rearrange("b (h p) d -> p (b h) d", p=P)).then_inc(ld_x, 16)
            sp.dma_start(xp_n[0:NPROJ, :], x_proj_w).then_inc(ld_small, 16)
            sp.dma_start(dtp_n, dt_proj_w.rearrange("(e p) r -> p e r", p=P)).then_inc(ld_small, 16)
            sp.dma_start(gate_n[0:NE, :], gate_w).then_inc(ld_small, 16)
            sp.dma_start(wk_sb, Wk).then_inc(ld_kv, 16)
            sp.dma_start(wv_sb, Wv).then_inc(ld_kv, 16)
            sp.wait_ge(split_done, 3)
            sp.dma_start(bc_stack[NPROJ:2 * NPROJ, :], bc_mid[0:NPROJ, :]).then_inc(stacked, 16)
            sp.dma_start(bc_stack[2 * NPROJ:3 * NPROJ, :], bc_lo[0:NPROJ, :]).then_inc(stacked, 16)
            sp.wait_ge(consts, NCONST)
            sp.wait_ge(pool_chain, 6)
            sp.dma_start(xg_dram[0:NREC, :].rearrange("(e c) f -> c e f", c=CAP),
                         initrec[:, :].unsqueeze(1).to_broadcast([P, NE, REC])).then_inc(init_done, 16)
            ykz = yk_dram[0:T * TOPK, :].rearrange("(p i r) d -> p i (r d)", p=P, r=4)
            sp.dma_start(ykz, zeros[:, :].unsqueeze(1).to_broadcast([P, T * TOPK // P // 4, 4 * DM])
                         ).then_inc(init_done, 16)

            sp.wait_ge(ctxT_ps, 2)
            sp.wait_ge(dt_ps, 4)
            sp.wait_ge(split_done, 3)
            sp.wait_ge(conv_done, 2)
            for w, src in enumerate((c_fc, c_proj)):
                sp.dma_start(v2(wraw[:, w], ND), src.rearrange("(c p) h -> p c h", p=P)).then_inc(ld_mlp, 16)

            def load_experts(e, low, signal):
                dst = place_of(e, low)
                gu = dst[:, 0:4 * DM].rearrange("p (w g f) -> p w g f", g=2, f=FE)
                for g, w in enumerate((w_gate, w_up)):
                    sp.dma_start(gu[:, :, g, :], w[bass.ds(e, 2)].rearrange("a (c p) f -> p (a c) f", p=P)
                                 ).then_inc(signal, 16)
                sp.dma_start(v2(dst[:, 4 * DM:], 2), w_down[bass.ds(e, 2)].rearrange("a p f -> p a f")
                             ).then_inc(signal, 16)

            wq_cols = Wq.rearrange("(c p) n -> p c n", p=P)

            def load_wq(t, r, q, low, loaded=True):
                if r % 2:
                    return
                j = r // 2
                if low >= 4:
                    sp.wait_ge(q_ps, NKV * q + j - 1)
                elif loaded:
                    return
                sp.dma_start(wq_sb[:, j % 2], wq_cols[:, :, 2 * j * HD:(2 * j + 2) * HD]).then_inc(ld_wq[j % 2], 16)

            sp.wait_ge(x1_done, NB)
            for e in range(0, PRE, 2):
                load_experts(e, e, ld_preA)
            sp.wait_ge(init_done, 32)
            for t in (0, 2):
                load_wq(t, t, 0, t, loaded=False)
            sp.dma_start(mask_sb, mask.rearrange("b s -> (b s)").partition_broadcast(P)).then_inc(ld_mask, 16)
            sp.wait_ge(x2_done, NT)
            sp.dma_start(wo_sb, Wo.rearrange("(h d) n -> d h n", d=HD)).then_inc(ld_wo, 16)

            assert all(SLOTW * (PRE + 2 * q + 2) <= KVCOL + 2 * NKV * HD * (q + 1) for q in range(NB))

            def load_pair(h, q, k):
                sp.wait_ge(vb_done, NKV * (q + 1))
                load_experts(PRE + 2 * q, PRE, ld_preA)

            run_units(sp, [(0, load_wq), tile_at(20, 0, load_pair)])
            sp.wait_ge(x3_done, NB * NKV)
            for e in range(PRE + PREV, NSLOT, 2):
                load_experts(e, e, ld_preB)
            sp.wait_ge(init_done, 32)
            sp.wait_ge(dispatched, 16 * NT * TOPK)

            def load_xg(t, r, q, low):
                if r % 2:
                    return
                if low >= 8:
                    sp.wait_ge(xgT_ps, t - 6)
                    sp.wait_ge(row_done, t - 6)
                src = xg_dram[bass.ds(t * CAP, 2 * CAP), :].rearrange("(a p) f -> p a f", p=P)
                sp.dma_start(xg[:, r:r + 2, :], src).then_inc(xg_ld[r // 2], 16)

            FROM = 24

            def load_more(t, r, q, low):
                if r % 4 == 0 and low < 2 * NMORE:
                    load_experts(NSLOT + 4 * q + r // 2, NSLOT, ld_more)

            def load_next(t, r, q, low):
                if r % 4 == 0 and FROM <= low < FROM + 2 * (NE - NSLOT - NMORE):
                    place = 4 * q + r // 2 - FROM // 2
                    sp.wait_ge(yd_ps, place + 2)
                    if low >= FROM + 8:
                        sp.wait_ge(w_ld[r // 4], 48 * (q - FROM // 8))
                    load_experts(NSLOT + NMORE + place, NSLOT + NMORE, w_ld[r // 4])

            run_steps(sp, NE, 8, [(0, load_xg), (0, load_more), (0, load_next)],
                      cuts=(FROM, 2 * NMORE, FROM + 2 * (NE - NSLOT - NMORE)))

            sp.wait_ge(yd_ps, NE)
            for r in range(4):
                sp.wait_ge(scattered[r], 16 * (NE // 4))
            for t in range(NT):
                if t >= 4:
                    sp.wait_ge(ysum_done, t - 3)
                sp.dma_start(yall[:, t % 4, :],
                             yk_dram[t * P * TOPK:(t + 1) * P * TOPK, :].rearrange("(p k) d -> p (k d)", k=TOPK)
                             ).then_inc(yk_ld[t % 4], 16)
            for t in range(NT):
                sp.wait_ge(out_done, t + 1)
                b, h = t // 2, t % 2
                sp.dma_start(out[b, h * P:(h + 1) * P, :], xres[:, t, :]).then_inc(stored, 16)
            sp.wait_ge(stored, 16 * NT)

        @block.gpsimd
        def _(pool):
            def unit(out_ap):
                return pool.affine_select(out=out_ap, in_=out_ap, compare_op=ALU.not_equal, fill=1.0, base=0,
                                          pattern=[[-1, P]], channel_multiplier=1)

            pool.dma_start(cw, conv_w.rearrange("(e p) a k -> p e (a k)", p=P)).then_inc(ld_vec, 16)
            pool.dma_start(cb, conv_b.rearrange("(e p) -> p e", p=P), allow_slow_non_contiguous=True).then_inc(ld_vec, 16)
            pool.dma_start(dtb, dt_proj_b.rearrange("(e p) -> p e", p=P), allow_slow_non_contiguous=True).then_inc(ld_vec, 16)
            pool.dma_start(dsk, D_skip.rearrange("(e p) -> p e", p=P), allow_slow_non_contiguous=True).then_inc(ld_vec, 16)
            pool.dma_start(alog, A_log.rearrange("(e p) n -> p e n", p=P)).then_inc(ld_vec, 16)
            pool.dma_start(gates[:, 0:2], g_xattn.partition_broadcast(P)).then_inc(ld_gates, 16)
            pool.dma_start(gates[:, 2:4], g_ffn.partition_broadcast(P)).then_inc(ld_gates, 16)

            pool.memset(ident[:, :], 0.0).then_inc(consts, 1)
            pool.memset(identb[:, :], 0.0).then_inc(consts, 1)
            pool.wait_ge(consts, 2)
            unit(ident[:, :]).then_inc(consts, 1)
            unit(identb[:, :]).then_inc(consts, 1)
            pool.memset(upad[:, :, :, 0:NTAP - 1], 0.0).then_inc(consts, 1)
            pool.memset(nhalf[:, :], -0.5).then_inc(consts, 1)
            pool.wait_ge(ln1_stats, 1)
            pool.wait_ge(consts, 6)
            pool.tensor_scalar(rs1, mv1[:, :, 1], EPS, None, ALU.add).then_inc(pool_chain, 1)
            pool.wait_ge(pool_chain, 1)
            pool.tensor_tensor(rs1, rs1, nhalf[:, :], ALU.pow).then_inc(ln1_rstd, 1)
            selv = sel.rearrange("p (n m) -> p n m", m=P)[0:3 * NPROJ]
            pool.memset(sel.bitcast(F32), 0.0).then_inc(pool_chain, 1)
            for n in range(3):
                pool.wait_ge(pool_chain, 2 + n)
                pool.affine_select(out=selv, in_=selv, compare_op=ALU.not_equal, fill=1.0,
                                   base=-(RANK + n * NPROJ), pattern=[[-1, 2 * NST], [0, P]],
                                   channel_multiplier=1).then_inc(pool_chain, 1)
            pool.wait_ge(pool_chain, 5)
            pool.wait_ge(u_sb, 2)
            for e in range(ND):
                pool.memset(dA[:, e].rearrange("p (b l) -> p b l", b=NB)[:, :, 0:1], 0.0).then_inc(sel_done, 1)
            pool.memset(ones[:, :], 1.0).then_inc(consts, 1)
            pool.memset(tri[:, :], 1.0).then_inc(consts, 1)
            pool.wait_ge(consts, 8)
            pool.affine_select(out=tri[:, :], in_=tri[:, :], compare_op=ALU.is_gt, fill=0.0, base=0,
                               pattern=[[1, P]], channel_multiplier=-1).then_inc(consts, 1)
            io = dict(allow_small_or_imprecise_dtypes=True)
            pool.iota(iota_e[:, :], [[1, NE]], base=0, channel_multiplier=0, **io).then_inc(consts, 1)
            pool.iota(rank1[:, :], [[1, TOPK]], base=1, channel_multiplier=0, **io).then_inc(consts, 1)
            pool.iota(drop_row[:, :], [[P, NT * TOPK]], base=NREC, channel_multiplier=1, **io).then_inc(consts, 1)
            pool.iota(tok8[:, :], [[P * TOPK, NT]], base=-1, channel_multiplier=TOPK, **io).then_inc(consts, 1)
            pool.iota(empty_row[:, :], [[CAP, NE]], base=T * TOPK + 1, channel_multiplier=1, **io).then_inc(consts, 1)
            pool.memset(initrec[:, 0:DM], 0.0).then_inc(consts, 1)
            pool.memset(initrec[:, DM:DM + TOPK], -1.0).then_inc(consts, 1)
            pool.memset(initrec[:, DM + TOPK:REC - 1], 0.0).then_inc(consts, 1)
            pool.memset(initrec[:, REC - 1:REC], -1.0).then_inc(consts, 1)
            pool.memset(zeros[:, :], 0.0).then_inc(pool_chain, 1)
            pool.wait_ge(pool_chain, 6)

            pool.wait_ge(act_sp, 7)
            pool.wait_ge(sp_done, 1)
            pool.tensor_tensor(dt[:, 0], dt[:, 0], sp_d[:, 0], ALU.add).then_inc(dt_done[0], 1)

            def prods(t, r, q, low):
                for e in range(ND):
                    m = 2 * t + e
                    pool.wait_ge(scan_done, m + 1)
                    if e == 0:
                        pool.wait_ge(c_sb, t + 1)
                    wait(pool, prod_used, m - 1 if low > 0 or e > 0 else 0)
                    pool.tensor_tensor(prod[:, e], hst[:, e], csb[:, r], ALU.mult).then_inc(prod_done, 1)

            run_steps(pool, NST, 2, [(0, prods)])

            def rstd(src, dst, stats, tmp_count, signal, t):
                pool.wait_ge(stats, t + 1)
                pool.tensor_scalar(dst, src, EPS, None, ALU.add).then_inc(pool_chain, 1)
                tmp_count[0] += 1
                pool.wait_ge(pool_chain, tmp_count[0])
                pool.tensor_tensor(dst, dst, nhalf[:, 0:1], ALU.pow).then_inc(signal, 1)

            chain = [6]

            def rstd2(t, *_):
                r = t % 2
                wait(pool, xn_done, t - 1)
                rstd(mvf[:, 2 * r + 1:2 * r + 2], rsf[:, r:r + 1], st_done, chain, rstd_done, t)

            def square(t, *_):
                pool.wait_ge(relu_done, t + 1)
                wait(pool, qf_done, t - 1)
                pool.tensor_tensor(sq[:, t % 2], rl[:, t % 2], rl[:, t % 2], ALU.mult).then_inc(sq_done, 1)

            def rstd3(t, *_):
                r = t % 2
                wait(pool, xn3_done, t - 1)
                rstd(mv3[:, 2 * r + 1:2 * r + 2], rs3[:, r:r + 1], st3_done, chain, rstd3_done, t)

            run_steps(pool, NT, NT, [(6, rstd3), (0, rstd2), (2, square)])

            def vcopy(t, r, q, low):
                if r % 2:
                    return
                j = r // 2
                if low >= 4:
                    pool.wait_ge(pv_ps, t - 2)
                pool.tensor_copy(vbuf[:, j % 2], vS[:, bass.ds(2 * q, 2), j * HD:(j + 1) * HD]).then_inc(vb_done, 1)

            def rstd4(h, q, k):
                pool.wait_ge(st4_done, k + 1)
                pool.sem_inc(pool_go, 1)
                pool.tensor_scalar(rmv[:, h, 2:3], rmv[:, h, 1:2], EPS, None, ALU.add).then_inc(rstd4_sum, 1)
                pool.wait_ge(rstd4_sum, k + 1)
                pool.tensor_tensor(rmv[:, h, 2:3], rmv[:, h, 2:3], nhalf[:, 0:1], ALU.pow).then_inc(rstd4_done, 1)

            def dispatch(ranks):
                def fn(h, q, k):
                    pool.wait_ge(loc_done, k + 1)
                    pool.sem_inc(pool_go, 1)
                    for i in ranks:
                        pool.indirect_dma_start(xg_dram, bass.IndirectOffsetOnAxis(loc[:, h, i:i + 1], 0), rec[:, h, :],
                                                None).then_inc(dispatched, 16)
                    if h == 1 and ranks[-1] == TOPK - 1:
                        pool.wait_ge(dispatched, 16 * 2 * TOPK * (q + 1))
                        pool.sem_inc(rec_free, 1)

                return fn

            third = (range(0, 3), range(3, 6), range(6, TOPK))
            wait_kv(pool, NKVG - 1)
            pool.wait_ge(x2_done, NT)
            pool.wait_ge(init_done, 32)
            pool.sem_inc(rec_free, 1)
            run_units(pool, [(1, vcopy), tile_at(20, 0, rstd4), tile_at(21, 1, rstd4),
                             *(tile_at(27 + i, 0, dispatch(third[i])) for i in range(3)),
                             *(tile_at(min(30 + i, 31), 1, dispatch(third[i])) for i in range(3))])

            def scatter(t, r, q, low):
                if low >= 4:
                    pool.wait_ge(scattered[r % 4], 16 * (2 * q + r // 4))
                pool.wait_ge(ysb_done, t + 1)
                pool.sem_inc(pool_go, 1)
                pool.indirect_dma_start(yk_dram, bass.IndirectOffsetOnAxis(row[:, r], 0), ysb[:, r, :],
                                        None).then_inc(scattered[r % 4], 16)

            run_steps(pool, NE, 8, [(0, scatter)])

        @block.scalar
        def _(act):
            act.wait_ge(ld_gates, 32)
            act.activation(tg[:, :], gates[:, :], ACT.Tanh).then_inc(tanh_done, 1)
            act.wait_ge(ld_small, 16 * 3)
            act.wait_ge(ld_vec, 16 * 5)
            act.activation(aexp, alog, ACT.Exp).then_inc(a_exp, 1)
            for n in range(2):
                act.wait_ge(ctxT_ps, n + 1)
                act.activation(ctxT[:, 512 * n:512 * n + 512], bank(n), ACT.Copy).then_inc(ctxT_sb, 1)
            act.wait_ge(consts, 5)
            for g in range(4):
                e, h = g // 2, g % 2
                act.wait_ge(xin_ps, g + 1)
                act.activation(upad[:, e, 2 * h:2 * h + 2, NTAP - 1:], v2(bank(4 + g), 2), ACT.Copy).then_inc(upad_sb, 1)

            def kv_evac(*groups):
                for g in groups:
                    act.wait_ge(kv_ps, g + 1)
                    dst, src = kv_place(g)
                    act.activation(dst, src, ACT.Copy).then_inc(kv_act, 1)

            def gate(*tiles):
                for t in tiles:
                    act.activation(zs[:, t], xres[:, t, :], ACT.Silu, bias=nb1[:, t:t + 1],
                                   scale=rs1[:, t:t + 1]).then_inc(zs_done, 1)

            act.preload_act_table(ACT.Silu)
            kv_evac(0, 1, 2, 3)
            act.wait_ge(conv_done, 1)
            act.activation(u[:, 0], conv_acc[:, 0], ACT.Silu).then_inc(u_sb, 1)
            kv_evac(4, 5, 6, 7)
            act.wait_ge(conv_done, 2)
            act.activation(u[:, 1], conv_acc[:, 1], ACT.Silu).then_inc(u_sb, 1)
            kv_evac(8, 9)
            act.wait_ge(ln1_nb, 1)
            gate(0, 1)
            for h in range(2):
                act.wait_ge(xdbl_ps, h + 1)
                act.activation(xdbl[0:NPROJ, 512 * h:512 * h + 512], bank(h)[0:NPROJ, :],
                               ACT.Copy).then_inc(xdbl_sb, 1)
            gate(*range(2, NT))
            for e in range(ND):
                act.wait_ge(dt_ps, 2 * e + 2)
                act.activation(sp_z[:, e], bank(4 + 2 * e, 2), ACT.Abs, bias=dtb[:, e:e + 1]).then_inc(act_sp, 1)
            for e in range(ND):
                act.wait_ge(act_sp, 1 + e)
                act.activation(sp_z[:, e], sp_z[:, e], ACT.Exp, scale=-1.0).then_inc(act_sp, 1)
            for e in range(ND):
                act.wait_ge(act_sp, 3 + e)
                act.activation(sp_l[:, e], sp_z[:, e], ACT.Ln, bias=1.0).then_inc(act_sp, 1)
            for e in range(ND):
                act.activation(dt[:, e], bank(4 + 2 * e, 2), ACT.Relu, bias=dtb[:, e:e + 1]).then_inc(act_sp, 1)
            kv_evac(17, 18)
            act.wait_ge(a_neg, 1)
            act.wait_ge(sel_done, 2)
            act.preload_act_table(ACT.Exp)

            def da(t, r, q, low):
                for e in range(ND):
                    m = 2 * t + e
                    wait(act, scan_done, m - 1 if low > 0 or e > 0 else 0)
                    if low == 0:
                        act.wait_ge(dt_done[e], 1)
                    bl = lambda ap: ap.rearrange("p (b l) -> p b l", b=NB)[:, :, 1:]
                    act.activation(bl(dA[:, e]), bl(dt[:, e]), ACT.Exp,
                                   scale=aneg[:, e, bass.ds(t, 1)]).then_inc(da_rdy, 1)

            def ccopy(t, r, q, low):
                act.wait_ge(c_rdy, t + 1)
                wait(act, prod_done, 2 * t - 2 if low > 1 else 0)
                act.activation(csb[:, r], bank(2, 2), ACT.Copy).then_inc(c_sb, 1)

            run_steps(act, NST, 2, [(0, da), (0, ccopy)])

            act.wait_ge(ld_mlp, 32)
            wait_kv(act, 15)
            for w in range(2):
                act.activation(wneg, wraw[:, w], ACT.Abs, accum_out=wsc[:, w:w + 1]).then_inc(wabs_done, 1)
                act.wait_ge(wabs_done, w + 1)
            act.wait_ge(scale_done, 1)
            for w in (1, 0):
                act.activation(wraw[:, w], wraw[:, w], ACT.Identity, bias=wsc[:, 8:9], scale=wsc[:, 4 + w:5 + w]
                               ).then_inc(wround_done, 1)
                kv_evac(*((19, 20) if w == 1 else (21, 22)))

            for g in range(4):
                act.wait_ge(w2T_ps, g + 1)
                act.activation(w2T[:, 2 * g:2 * g + 2, :].rearrange("p a d -> p (a d)"),
                               bank(6 + g % 2).bitcast(BF16)[:, 0:512], ACT.Copy).then_inc(w2T_sb, 1)
            kv_evac(23, 24, 25)

            def x_high(t, *_):
                act.wait_ge(xT_ps, t + 1)
                wait(act, h_ps, t - 1)
                act.activation(xhi[:, t % 2].rearrange("p c t -> p (c t)"), bank(0)[:, 0:DM], ACT.Copy).then_inc(hi_done, 1)

            def x_middle(t, *_):
                act.wait_ge(r1_done, t + 1)
                act.activation(xmid[:, t % 2].rearrange("p c t -> p (c t)"), xr1[:, t % 2], ACT.Copy).then_inc(mid_done, 1)

            def relu(t, *_):
                r = t % 2
                act.wait_ge(h_ps, t + 1)
                wait(act, rs_done, t - 1)
                wait(act, sq_done, t - 1)
                act.activation(rl[:, r], bank(2 + 2 * r, 2), ACT.Relu).then_inc(relu_done, 1)

            def quantise(t, *_):
                r = t % 2
                act.wait_ge(rs_done, t + 1)
                act.wait_ge(sq_done, t + 1)
                wait(act, qb_done, t - 1)
                act.activation(qf[:, r], sq[:, r], ACT.Identity, bias=wsc[:, 8:9],
                               scale=sml[:, 8 * (t % 4) + 3:8 * (t % 4) + 4]).then_inc(qf_done, 1)

            def qT_evac(t, *_):
                act.wait_ge(qT_ps, t + 1)
                wait(act, o_ps, t - 1)
                act.activation(qT[:, t % 2].rearrange("p h t -> p (h t)"), bank(6).bitcast(BF16), ACT.Copy).then_inc(qT_sb, 1)

            def xT3_evac(t, *_):
                act.wait_ge(xT3_ps, t + 1)
                act.activation(xT[:, :, t * P:(t + 1) * P], v2(bank(1)[:, 0:DM], ND), ACT.Copy).then_inc(xT3_sb, 1)

            def last_values(t, *_):
                if t < NKVG - 26:
                    kv_evac(26 + t)

            run_steps(act, NT, NT, [(2, relu), (3, quantise), (6, xT3_evac), (0, x_high), (4, qT_evac), (0, x_middle),
                                    (0, last_values)])

            def q_evac(t, r, q, low):
                if r % 2:
                    return
                j = r // 2
                act.wait_ge(q_ps, NKV * q + j + 1)
                if low >= 4:
                    act.wait_ge(s_ps, t - 2)
                act.activation(qTh[:, j % 2].rearrange("p u t -> p (u t)"), bank(6), ACT.Copy).then_inc(q_sb, 1)

            def exps(t, r, q, low):
                r2 = r % 2
                act.wait_ge(nm_done, t + 1)
                if low >= 2:
                    act.wait_ge(pn_done, t - 1)
                for a in range(2):
                    act.activation(pe_[:, r2, a], sm[:, r2, a], ACT.Exp, bias=nm[:, r2, a:a + 1], scale=HD ** -0.5,
                                   accum_out=sume[:, r2, a:a + 1]).then_inc(exp_done, 1)

            def norm(t, r, q, low):
                r2 = r % 2
                act.wait_ge(rc_done, t + 1)
                if low >= 2:
                    act.wait_ge(pT_ps, t - 1)
                for a in range(2):
                    ins = act.activation(Pn[:, r2, a], pe_[:, r2, a], ACT.Copy, scale=rc[:, r2, a:a + 1])
                ins.then_inc(pn_done, 1)

            def pv_evac(t, r, q, low):
                j, uu = r // 2, r % 2
                act.wait_ge(pv_ps, t + 1)
                if low >= 4:
                    act.wait_ge(ao_ps, NKV * q + j - 1)
                act.activation(attT[:, j % 2, uu], bank(4)[:, uu * L:(uu + 1) * L], ACT.Copy).then_inc(att_sb, 1)

            def rT_evac(h, q, k):
                act.wait_ge(rT_ps, k + 1)
                if h == 1:
                    act.wait_ge(lg_ps, k)
                act.activation(xTr.rearrange("p c t -> p (c t)"), bank(5)[:, 0:DM], ACT.Copy).then_inc(rT_sb, 1)

            def rexp(h, q, k):
                act.wait_ge(rmax_done, k + 1)
                act.activation(rp[:, h], bank(5)[:, DM:DM + NE], ACT.Exp, bias=rsm[:, h, 0:1],
                               accum_out=rsm[:, h, 1:2]).then_inc(rexp_done, 1)

            act.preload_act_table(ACT.Exp)
            run_units(act, [(2, exps), (0, q_evac), (2, norm), (3, pv_evac), tile_at(22, 0, rT_evac),
                            tile_at(23, 0, rexp), tile_at(24, 1, rT_evac), tile_at(25, 1, rexp)])

            def xgT_evac(t, r, q, low):
                act.wait_ge(xgT_ps, t + 1)
                if low >= 2:
                    act.wait_ge(gu_ps, t - 1)
                act.activation(xgT[:, r % 2].rearrange("p c t -> p (c t)"), bank(r % 2)[:, 0:DM], ACT.Copy
                               ).then_inc(xgT_sb, 1)

            def silu(t, r, q, low):
                act.wait_ge(gu_ps, t + 1)
                if low >= 2:
                    act.wait_ge(h_done, t - 1)
                act.activation(sil[:, r % 2], bank(2 + r % 2)[:, 0:FE], ACT.Silu).then_inc(sil_done, 1)

            def hT_evac(t, r, q, low):
                act.wait_ge(hT_ps, t + 1)
                if low >= 2:
                    act.wait_ge(yd_ps, t - 1)
                act.activation(hT[:, r % 2], bank(4 + r % 2)[:, 0:CAP], ACT.Copy).then_inc(hT_sb, 1)

            act.preload_act_table(ACT.Silu)
            run_steps(act, NE, 8, [(0, xgT_evac), (1, silu), (2, hT_evac)])

        @block.tensor
        def _(pe):
            mm = lambda o, a, b, s, e, **k: pe.matmul(o, a, b, start=s, stop=e, **k)
            pe.wait_ge(consts, 4)
            pe.wait_ge(ld_ctx, 32)
            for t in range(NT):
                ins = pe.transpose(bank(t // 4)[:, (t % 4) * P:(t % 4 + 1) * P], ctxn[:, t], ident[:, :])
                if t % 4 == 3:
                    ins.then_inc(ctxT_ps, 1)
            for e in range(ND):
                ins = pe.transpose(bank(2)[:, e * P:(e + 1) * P], in_n[:, e], ident[:, :])
            ins.then_inc(smallT_ps, 1)
            pe.wait_ge(ld_small, 16 * 3)
            pe.wait_ge(ld_vec, 16 * 5)
            for e in range(ND):
                pe.transpose(bank(3)[:, e * NPROJ:(e + 1) * NPROJ], xp_n[0:NPROJ, e * P:(e + 1) * P],
                             ident[0:NPROJ, 0:NPROJ])
                pe.transpose(bank(3)[0:RANK, 128 + e * P:128 + (e + 1) * P], dtp_n[:, e], ident[:, :])
                ins = pe.transpose(bank(3)[:, 384 + e * NE:384 + (e + 1) * NE], gate_n[0:NE, e * P:(e + 1) * P],
                                   ident[0:NE, 0:NE])
            ins.then_inc(smallT_ps, 1)
            pe.wait_ge(ctxT_sb, 2)
            pe.wait_ge(smallT_sb, 1)
            for g in range(4):
                e, h = g // 2, g % 2
                mm(bank(4 + g), inT[:, e * P:(e + 1) * P], ctxT[:, 512 * h:512 * h + 512], True, True).then_inc(xin_ps, 1)

            def kv(g):
                if g == 0:
                    pe.wait_ge(ld_kv, 32)
                if g < 2:
                    pe.wait_ge(smallT_sb, 2)
                else:
                    wait_kv(pe, g - 2 if g < 26 else g - 1)
                n, h = (g % 16) // 2, g % 2
                if g < 16:
                    a, b = wk_sb[:, n * HD:(n + 1) * HD], ctxT[:, 512 * h:512 * h + 512]
                else:
                    a, b = ctxT[:, n * P:(n + 1) * P], wv_sb[:, 512 * h:512 * h + 512]
                mm(kv_place(g)[1], a, b, True, True).then_inc(kv_ps, 1)

            for g in range(10):
                kv(g)
            pe.wait_ge(u_sb, 2)
            for h in range(2):
                for e in range(ND):
                    ins = mm(bank(h)[0:NPROJ, :], xpT[:, e], u[:, e, 512 * h:512 * h + 512], e == 0, e == 1)
                ins.then_inc(xdbl_ps, 1)
            kv(10)
            kv(11)
            pe.wait_ge(upad_sb, 4)
            pe.wait_ge(xdbl_sb, 2)
            for g in range(4):
                e, h = g // 2, g % 2
                mm(bank(4 + g), dtpT[0:RANK, e * P:(e + 1) * P], xdbl[0:RANK, 512 * h:512 * h + 512], True, True
                   ).then_inc(dt_ps, 1)
            for g in range(12, 19):
                kv(g)
            pe.wait_ge(dskm_done, 1)
            pe.wait_ge(act_sp, 8)
            for g in range(4):
                e, h = g // 2, g % 2
                mm(bank(4 + g), dskm[:, e], u[:, e, 512 * h:512 * h + 512], True, False, skip_group_check=True)
            pe.wait_ge(stacked, 32)
            wait_kv(pe, 18)
            pe.wait_ge(pool_chain, 5)

            def bc(t, r, q, low):
                if low > 0:
                    pe.wait_ge(dbu_done, 2 * t)
                for h in range(2):
                    ins = mm(bank(h), sel[0:3 * NPROJ, bass.ds(t * P, P)],
                             bc_stack[0:3 * NPROJ, 512 * h:512 * h + 512], True, True)
                ins.then_inc(b_rdy, 1)
                if low > 0:
                    pe.wait_ge(c_sb, t)
                for h in range(2):
                    ins = mm(bank(2 + h), sel[0:3 * NPROJ, bass.ds(t * P + NST * P, P)],
                             bc_stack[0:3 * NPROJ, 512 * h:512 * h + 512], True, True)
                ins.then_inc(c_rdy, 1)

            def y_add(e):
                def fn(t, r, q, low):
                    pe.wait_ge(prod_done, 2 * t + e + 1)
                    for h in range(2):
                        ins = mm(bank(4 + 2 * e + h), ident[:, :], prod[:, e, 512 * h:512 * h + 512], False,
                                 low == NST - 1, skip_group_check=True)
                    ins.then_inc(prod_used, 1)

                return fn

            run_steps(pe, NST, 2, [(0, bc), (2, y_add(1)), (1, y_add(0))])
            pe.wait_ge(wabs_done, 2)
            pe.wait_ge(c_sb, NST)
            mm(bank(3)[:, 0:2], ones[:, :], wsc[:, 0:2], True, True).then_inc(wsum_ps, 1)
            pe.wait_ge(dbu_done, 2 * NST)
            for g in range(19, 23):
                kv(g)
            pe.wait_ge(yz_done, 2)
            pe.wait_ge(scale_done, 1)
            wait_kv(pe, 22)
            for b in range(NB):
                for h in range(2):
                    for e in range(ND):
                        ins = pe.transpose(bank(b)[:, h * DM + e * P:h * DM + (e + 1) * P],
                                           dtu[:, e, b * L + h * P:b * L + (h + 1) * P], ident[:, :])
                ins.then_inc(yT_ps, 1)
            pe.wait_ge(w2_done, 1)
            for g in range(4):
                wait(pe, w2T_sb, g - 1)
                for n in range(2):
                    for c in range(ND):
                        h = 2 * g + n
                        ins = pe.transpose(bank(6 + g % 2).bitcast(BF16)[:, n * DM + c * P:n * DM + (c + 1) * P],
                                           w2q[:, c, h * P:(h + 1) * P], identb[:, :])
                ins.then_inc(w2T_ps, 1)
            for g in range(23, 26):
                kv(g)
            pe.wait_ge(x1_done, NB)
            pe.wait_ge(w1_done, 1)
            pe.wait_ge(w2T_sb, 4)

            def x_turn(t, *_):
                pe.wait_ge(xn_done, t + 1)
                wait(pe, r1_done, t)
                for c in range(ND):
                    ins = pe.transpose(bank(0)[:, c * P:(c + 1) * P], xn[:, t % 2, c * P:(c + 1) * P], ident[:, :])
                ins.then_inc(xT_ps, 1)

            def hidden(t, *_):
                r = t % 2
                pe.wait_ge(lo_done, t + 1)
                wait(pe, relu_done, t - 1)
                for h in range(2):
                    n = 0
                    for part in (xhi, xmid, xlo):
                        for c in range(ND):
                            ins = mm(bank(2 + 2 * r + h), part[:, r, c], w1q[:, c, 512 * h:512 * h + 512],
                                     n == 0, n == 5)
                            n += 1
                ins.then_inc(h_ps, 1)

            def q_turn(t, *_):
                pe.wait_ge(qb_done, t + 1)
                wait(pe, qT_sb, t)
                for h in range(HID // P):
                    ins = pe.transpose(bank(6).bitcast(BF16)[:, h * P:(h + 1) * P], qb[:, t % 2, h * P:(h + 1) * P],
                                       identb[:, :])
                ins.then_inc(qT_ps, 1)

            def mlp_out(t, *_):
                pe.wait_ge(qT_sb, t + 1)
                wait(pe, x2_done, t)
                for h in range(HID // P):
                    ins = mm(bank(7)[:, 0:DM], qT[:, t % 2, h], w2T[:, h], h == 0, h == HID // P - 1)
                ins.then_inc(o_ps, 1)

            def x3_turn(t, *_):
                if t == 0:
                    wait_kv(pe, NKVG - 1)
                pe.wait_ge(xn3_done, t + 1)
                wait(pe, xT3_sb, t)
                for c in range(ND):
                    ins = pe.transpose(bank(1)[:, c * P:(c + 1) * P], xn3[:, t % 2, c * P:(c + 1) * P], ident[:, :])
                ins.then_inc(xT3_ps, 1)

            def last_values(t, *_):
                if t < NKVG - 26:
                    kv(26 + t)

            run_steps(pe, NT, NT, [(5, mlp_out), (4, q_turn), (6, x3_turn), (0, x_turn), (1, hidden), (0, last_values)])

            def q_proj(t, r, q, low):
                if r % 2:
                    return
                j = r // 2
                pe.wait_ge(ld_wq[j % 2], 16 * (NKV // 2 * q + j // 2 + 1))
                if low == 0:
                    pe.wait_ge(xT3_sb, NT)
                if low >= 2:
                    pe.wait_ge(q_sb, NKV * q + j)
                for uu in range(2):
                    for c in range(ND):
                        ins = mm(bank(6)[:, uu * L:(uu + 1) * L], wq_sb[:, j % 2, c, uu * HD:(uu + 1) * HD],
                                 xT[:, c, bass.ds(q * L, L)], c == 0, c == 1)
                ins.then_inc(q_ps, 1)

            def scores(t, r, q, low):
                j, uu = r // 2, r % 2
                pe.wait_ge(q_sb, NKV * q + j + 1)
                if low >= 2:
                    pe.wait_ge(smax_done, 2 * t - 2)
                for a in range(2):
                    ins = mm(bank(r % 2)[:, a * L:(a + 1) * L], qTh[:, j % 2, uu, a * P:(a + 1) * P],
                             kT[:, j, bass.ds(q * L, L)], True, True)
                ins.then_inc(s_ps, 1)

            def p_turn(t, r, q, low):
                pe.wait_ge(pn_done, t + 1)
                if low >= 2:
                    pe.wait_ge(pT_sb, t - 1)
                for a in range(2):
                    for c in range(2):
                        ins = pe.transpose(bank(2 + r % 2)[:, c * L + a * P:c * L + (a + 1) * P],
                                           Pn[:, r % 2, a, c * P:(c + 1) * P], ident[:, :])
                ins.then_inc(pT_ps, 1)

            def pv(t, r, q, low):
                j, uu = r // 2, r % 2
                pe.wait_ge(pT_sb, t + 1)
                pe.wait_ge(vb_done, NKV * q + j + 1)
                if low >= 1:
                    pe.wait_ge(att_sb, t)
                for c in range(2):
                    ins = mm(bank(4)[:, uu * L:(uu + 1) * L], vbuf[:, j % 2, c], pT[:, r % 2, c], c == 0, c == 1)
                ins.then_inc(pv_ps, 1)

            def att_out(t, r, q, low):
                if r % 2 == 0:
                    return
                j = r // 2
                pe.wait_ge(att_sb, t + 1)
                if low >= 2:
                    pe.wait_ge(x3_done, NKV * q + j)
                else:
                    pe.wait_ge(ld_wo, 16)
                for a in range(2):
                    for uu in range(2):
                        ins = mm(bank(7)[:, a * DM:(a + 1) * DM], attT[:, j % 2, uu, a * P:(a + 1) * P],
                                 wo_sb[:, 2 * j + uu], uu == 0, uu == 1)
                ins.then_inc(ao_ps, 1)

            def r_turn(h, q, k):
                pe.wait_ge(rec_done, k + 1)
                if h == 1:
                    pe.wait_ge(rexp_done, k)
                for c in range(ND):
                    ins = pe.transpose(bank(5)[:, c * P:(c + 1) * P], rec[:, h, c * P:(c + 1) * P], ident[:, :])
                ins.then_inc(rT_ps, 1)

            def logits(h, q, k):
                pe.wait_ge(rT_sb, k + 1)
                for c in range(ND):
                    ins = mm(bank(5)[:, DM:DM + NE], xTr[:, c], gateT[:, c], c == 0, c == 1)
                ins.then_inc(lg_ps, 1)

            def positions(h, q, k):
                pe.wait_ge(fl_done, k + 1)
                pe.wait_ge(cum_done, k + 1)
                if h == 0:
                    pe.wait_ge(rexp_done, k + 2)
                else:
                    pe.wait_ge(pos_used, k)
                mm(bank(5)[:, DM + NE:DM + 2 * NE], tri[:, :], fl[:, h], True, False)
                mm(bank(5)[:, DM + NE:DM + 2 * NE], ones[:, :], cum, False, True).then_inc(pos_ps, 1)

            run_units(pe, [(2, scores), (3, p_turn), (0, q_proj), (4, att_out),
                           tile_at(22, 0, r_turn), tile_at(23, 0, logits), tile_at(24, 1, r_turn),
                           tile_at(25, 1, logits), tile_at(26, 0, positions), tile_at(29, 1, positions), (3, pv)])

            def xg_turn(t, r, q, low):
                pe.wait_ge(xg_ld[r // 2], 16 * (q + 1))
                if low >= 2:
                    pe.wait_ge(xgT_sb, t - 1)
                for c in range(ND):
                    ins = pe.transpose(bank(r % 2)[:, c * P:(c + 1) * P], xg[:, r, c * P:(c + 1) * P], ident[:, :])
                ins.then_inc(xgT_ps, 1)

            def columns(t, r, low, at, width):
                if NSLOT <= low < NSLOT + NMORE:
                    return tmp[:, bass.ds((t - NSLOT - r % 2) * SLOTW + at + NTMP - NMORE * SLOTW, width)]
                e = t - r % 2 - (NSLOT + NMORE if low >= NSLOT + NMORE else 0)
                return weights[:, bass.ds(e * SLOTW + at, width)]

            def gate_up(t, r, q, low):
                if low >= NSLOT + NMORE:
                    pe.wait_ge(w_ld[r // 2 % 2], 48 * (2 * (q - (NSLOT + NMORE) // 8) + r // 4 + 1))
                elif low >= NSLOT:
                    pe.wait_ge(ld_more, 24 * NMORE)
                pe.wait_ge(xgT_sb, t + 1)
                if low >= 2:
                    pe.wait_ge(h_done, t - 1)
                for c in range(ND):
                    ins = mm(bank(2 + r % 2)[:, 0:2 * FE], xgT[:, r % 2, c],
                             columns(t, r, low, r % 2 * 2 * DM + c * 2 * FE, 2 * FE), c == 0, c == 1)
                ins.then_inc(gu_ps, 1)

            def h_turn(t, r, q, low):
                pe.wait_ge(h_done, t + 1)
                if low >= 2:
                    pe.wait_ge(hT_sb, t - 1)
                pe.transpose(bank(4 + r % 2)[:, 0:CAP], hh[:, r % 2], ident[:, :]).then_inc(hT_ps, 1)

            def down(t, r, q, low):
                pe.wait_ge(hT_sb, t + 1)
                if low >= 2:
                    pe.wait_ge(ysb_done, t - 1)
                mm(bank(6 + r % 2)[:, 0:DM], hT[:, r % 2],
                   columns(t, r, low, 4 * DM + r % 2 * DM, DM), True, True).then_inc(yd_ps, 1)

            pe.wait_ge(pos_used, NT)
            pe.wait_ge(ld_preA, 24 * (PRE + PREV))
            pe.wait_ge(ld_preB, 24 * (NSLOT - PRE - PREV))
            run_steps(pe, NE, 8, [(0, xg_turn), (1, gate_up), (2, h_turn), (3, down)], cuts=(NSLOT, NSLOT + NMORE))

        @block.vector
        def _(dve):
            chain = [0]

            def link(ins):
                chain[0] += 1
                ins.then_inc(dve_chain, 1)
                dve.wait_ge(dve_chain, chain[0])

            dve.wait_ge(ld_x, 16)
            for t in range(NT):
                ins = dve.bn_stats(st6[:, t], xres[:, t, :])
            link(ins)
            for t in range(NT):
                ins = dve.bn_aggr(mv1[:, t], st6[:, t])
            ins.then_inc(ln1_stats, 1)
            dve.wait_ge(smallT_ps, 1)
            dve.tensor_copy(inT, bank(2)[:, 0:ND * P]).then_inc(smallT_sb, 1)
            dve.wait_ge(smallT_ps, 2)
            dve.tensor_copy(xpT.rearrange("p e k -> p (e k)"), bank(3)[:, 0:ND * NPROJ])
            dve.tensor_copy(dtpT[0:RANK, :], bank(3)[0:RANK, 128:384])
            dve.tensor_copy(gateT[:, :, :].rearrange("p e k -> p (e k)"), bank(3)[:, 384:384 + ND * NE]
                            ).then_inc(smallT_sb, 1)
            dve.wait_ge(ln1_rstd, 1)
            dve.scalar_tensor_tensor(out=nb1, in0=mv1[:, :, 0], scalar=-1.0, in1=rs1, op0=ALU.mult,
                                     op1=ALU.mult).then_inc(ln1_nb, 1)
            tap = lambda e, j: upad[:, e, :, j:j + L]
            cav = lambda e: conv_acc[:, e].rearrange("p (b l) -> p b l", b=NB)
            dve.wait_ge(ld_small, 16 * 3)
            dve.wait_ge(ld_vec, 16 * 5)
            dve.wait_ge(consts, 6)
            for e in range(ND):
                dve.wait_ge(upad_sb, 2 * e + 2)
                link(dve.tensor_scalar(cav(e), tap(e, NTAP - 1), cw[:, e, NTAP - 1:NTAP], cb[:, e:e + 1], ALU.mult,
                                       ALU.add))
                for j in range(NTAP - 1):
                    ins = dve.scalar_tensor_tensor(out=cav(e), in0=tap(e, j), scalar=cw[:, e, j:j + 1], in1=cav(e),
                                                   op0=ALU.mult, op1=ALU.add)
                    if j < NTAP - 2:
                        link(ins)
                ins.then_inc(conv_done, 1)
            dve.wait_ge(a_exp, 1)
            dve.tensor_scalar(aneg, aexp, -1.0, None, ALU.mult).then_inc(a_neg, 1)
            for e in range(ND):
                ins = dve.tensor_scalar(dskm[:, e], ident[:, :], dsk[:, e:e + 1], None, ALU.mult)
            ins.then_inc(dskm_done, 1)
            for g in (10, 11):
                dve.wait_ge(kv_ps, g + 1)
                dve.tensor_copy(*kv_place(g)).then_inc(kv_dve, 1)
            dve.wait_ge(xdbl_sb, 2)
            n = slice(0, NPROJ)
            dve.tensor_copy(bc_stack[n, :], xdbl[n, :]).then_inc(split_done, 1)
            dve.wait_ge(split_done, 1)
            link(dve.tensor_tensor(xdbl_r[n, :], xdbl[n, :], bc_stack[n, :], ALU.subtract))
            dve.tensor_copy(bc_mid[n, :], xdbl_r[n, :]).then_inc(split_done, 1)
            dve.wait_ge(split_done, 2)
            dve.tensor_tensor(bc_lo[n, :], xdbl_r[n, :], bc_mid[n, :], ALU.subtract).then_inc(split_done, 1)
            def kv_evac(*groups):
                for g in groups:
                    dve.wait_ge(kv_ps, g + 1)
                    dst, src = kv_place(g)
                    dve.tensor_copy(dst, src).then_inc(kv_dve, 1)

            dve.wait_ge(split_done, 3)
            kv_evac(12, 13, 14)
            for e in range(ND):
                dve.wait_ge(act_sp, 3 + e)
                link(dve.tensor_scalar(sp_d[:, e], sp_z[:, e], 1.0, -1.0, ALU.add, ALU.add))
                kv_evac(15 + e)
                link(dve.tensor_tensor(sp_d[:, e], sp_z[:, e], sp_d[:, e], ALU.subtract))
            for e in range(ND):
                dve.wait_ge(act_sp, 5 + e)
                dve.tensor_tensor(sp_d[:, e], sp_d[:, e], sp_l[:, e], ALU.add).then_inc(sp_done, 1)
            dve.wait_ge(act_sp, 8)
            dve.wait_ge(sp_done, 2)
            dve.tensor_tensor(dt[:, 1], dt[:, 1], sp_d[:, 1], ALU.add).then_inc(dt_done[1], 1)
            for e in (1, 0):
                dve.wait_ge(dt_done[e], 1)
                link(dve.tensor_tensor(dtu[:, e], dt[:, e], u[:, e], ALU.mult))

            def dbu(t, r, q, low):
                dve.wait_ge(b_rdy, t + 1)
                for e in range(ND):
                    wait(dve, scan_done, 2 * t + e - 1 if low > 0 else 0)
                    dve.tensor_tensor(dBu[:, e], dtu[:, e], bank(0, 2), ALU.mult).then_inc(dbu_done, 1)

            def scan(t, r, q, low):
                for e in range(ND):
                    dve.wait_ge(dbu_done, 2 * t + e + 1)
                    dve.wait_ge(da_rdy, 2 * t + e + 1)
                    wait(dve, prod_done, 2 * t + e - 1 if low > 0 else 0)
                    dve.tensor_tensor_scan(hst[:, e], dA[:, e], dBu[:, e], 0.0, ALU.mult, ALU.add).then_inc(scan_done, 1)

            run_steps(dve, NST, 2, [(0, dbu), (0, scan)])
            dve.wait_ge(tanh_done, 1)
            link(dve.memset(wsc[:, 8:9], ROUND))
            dve.wait_ge(wsum_ps, 1)
            link(dve.tensor_scalar(wsc[:, 2:4], bank(3)[:, 0:2], 1.0 / (DM * HID), EPS, ALU.mult, ALU.max))
            dve.reciprocal(wsc[:, 4:6], wsc[:, 2:4]).then_inc(scale_done, 1)
            link(dve.tensor_tensor(wsc[:, 9:10], wsc[:, 2:3], wsc[:, 2:3], ALU.mult))
            link(dve.tensor_scalar(wsc[:, 6:7], wsc[:, 9:10], 255.0, None, ALU.mult))
            link(dve.tensor_tensor(wsc[:, 10:11], wsc[:, 3:4], tg[:, 2:3], ALU.mult))
            link(dve.tensor_scalar(wsc[:, 7:8], wsc[:, 10:11], 1.0 / 255.0, None, ALU.mult))

            def ternary(w, dst, turn, signal):
                dve.wait_ge(wround_done, turn)
                link(dve.tensor_scalar(wraw[:, w], wraw[:, w], ROUND + 1, ROUND - 1, ALU.min, ALU.max))
                dve.tensor_scalar(dst.rearrange("p c h -> p (c h)"), wraw[:, w], -ROUND, None, ALU.add
                                  ).then_inc(signal, 1)

            dve.wait_ge(zs_done, NT)
            for e in range(ND):
                dve.wait_ge(prod_used, 2 * NST - 1 + e)
                dve.tensor_tensor(v2(dtu[:, e], NB), v2(bank(4 + 2 * e, 2), NB), zs[:, e:NT:2, :], ALU.mult
                                  ).then_inc(yz_done, 1)
            ternary(1, w2q, 1, w2_done)
            ternary(0, w1q, 2, w1_done)
            for b in range(NB):
                dve.wait_ge(yT_ps, b + 1)
                xv = xres[:, 2 * b:2 * b + 2, :].rearrange("p a d -> p (a d)")
                dve.scalar_tensor_tensor(out=xv, in0=bank(b), scalar=tg[:, 0:1], in1=xv, op0=ALU.mult,
                                         op1=ALU.add).then_inc(x1_done, 1)
            dve.wait_ge(x1_done, NB)

            marks = {}

            def mark(name, ins):
                chain[0] += 1
                ins.then_inc(dve_chain, 1)
                marks[name] = chain[0]

            after = lambda name: dve.wait_ge(dve_chain, marks[name])
            v = lambda t, k: sml[:, 8 * (t % 4) + k:8 * (t % 4) + k + 1]

            def stats2(t, *_):
                mark("stats2", dve.bn_stats(stf[:, 8 * (t % 2):8 * (t % 2) + 6], xres[:, t, :]))

            def aggr2(t, *_):
                after("stats2")
                wait(dve, xn_done, t - 1)
                dve.bn_aggr(mvf[:, 2 * (t % 2):2 * (t % 2) + 2], stf[:, 8 * (t % 2):8 * (t % 2) + 6]).then_inc(st_done, 1)

            def norm2(t, *_):
                r = t % 2
                dve.wait_ge(rstd_done, t + 1)
                wait(dve, xT_ps, t - 1)
                dve.tensor_scalar(xn[:, r], xres[:, t, :], mvf[:, 2 * r:2 * r + 1], rsf[:, r:r + 1], ALU.subtract,
                                  ALU.mult).then_inc(xn_done, 1)

            def x_rest(t, *_):
                dve.wait_ge(hi_done, t + 1)
                wait(dve, mid_done, t - 1)
                dve.tensor_tensor(xr1[:, t % 2], bank(0)[:, 0:DM], xhi[:, t % 2].rearrange("p c t -> p (c t)"),
                                  ALU.subtract).then_inc(r1_done, 1)

            def x_low(t, *_):
                dve.wait_ge(mid_done, t + 1)
                wait(dve, h_ps, t - 1)
                dve.tensor_tensor(xlo[:, t % 2].rearrange("p c t -> p (c t)"), xr1[:, t % 2],
                                  xmid[:, t % 2].rearrange("p c t -> p (c t)"), ALU.subtract).then_inc(lo_done, 1)

            def row_max(t, *_):
                dve.wait_ge(relu_done, t + 1)
                wait(dve, qf_done, t - 3)
                wait(dve, x2_done, t - 3)
                mark("max", dve.tensor_reduce(v(t, 0), rl[:, t % 2], AX.X, ALU.max))

            def row_square(t, *_):
                after("max")
                mark("square", dve.tensor_tensor(v(t, 1), v(t, 0), v(t, 0), ALU.mult))

            def row_xmax(t, *_):
                after("square")
                mark("xmax", dve.tensor_scalar(v(t, 1), v(t, 1), wsc[:, 9:10], EPS, ALU.mult, ALU.max))

            def row_recip(t, *_):
                after("xmax")
                mark("recip", dve.reciprocal(v(t, 2), v(t, 1)))

            def row_scales(t, *_):
                after("recip")
                dve.tensor_scalar(v(t, 4), v(t, 1), wsc[:, 7:8], None, ALU.mult)
                dve.tensor_scalar(v(t, 3), v(t, 2), wsc[:, 6:7], None, ALU.mult).then_inc(rs_done, 1)

            def q_bf16(t, *_):
                dve.wait_ge(qf_done, t + 1)
                wait(dve, qT_ps, t - 1)
                dve.tensor_scalar(qb[:, t % 2], qf[:, t % 2], -ROUND, None, ALU.add).then_inc(qb_done, 1)

            def x2(t, *_):
                dve.wait_ge(o_ps, t + 1)
                dve.scalar_tensor_tensor(out=xres[:, t, :], in0=bank(7)[:, 0:DM], scalar=v(t, 4), in1=xres[:, t, :],
                                         op0=ALU.mult, op1=ALU.add).then_inc(x2_done, 1)

            def stats3(t, *_):
                dve.wait_ge(x2_done, t + 1)
                mark("stats3", dve.bn_stats(st3[:, 8 * (t % 2):8 * (t % 2) + 6], xres[:, t, :]))

            def aggr3(t, *_):
                after("stats3")
                dve.bn_aggr(mv3[:, 2 * (t % 2):2 * (t % 2) + 2], st3[:, 8 * (t % 2):8 * (t % 2) + 6]).then_inc(st3_done, 1)

            def norm3(t, *_):
                r = t % 2
                dve.wait_ge(rstd3_done, t + 1)
                wait(dve, xT3_ps, t - 1)
                dve.tensor_scalar(xn3[:, r], xres[:, t, :], mv3[:, 2 * r:2 * r + 1], rs3[:, r:r + 1],
                                  ALU.subtract, ALU.mult).then_inc(xn3_done, 1)

            run_steps(dve, NT, NT, [(0, stats2), (3, row_recip), (0, aggr2), (1, x_low), (3, row_scales), (4, q_bf16),
                                    (5, x2), (6, norm3), (0, norm2), (2, row_max), (5, stats3), (0, x_rest),
                                    (2, row_square), (5, aggr3), (2, row_xmax)])

            dve.wait_ge(ld_mask, 16)
            link(dve.tensor_scalar(maskb.rearrange("p b s -> p (b s)"), mask_sb, -1.0, 1e30, ALU.add, ALU.mult))
            link(dve.tensor_reduce(valid, maskb, AX.X, ALU.max))
            link(dve.tensor_scalar(valid, valid, -1.0, None, ALU.is_gt))

            dve.memset(cum, 0.0).then_inc(cum_done, 1)
            dve.wait_ge(consts, NCONST)

            def smax(t, r, q, low):
                r2 = r % 2
                if r == 0:
                    if low >= 2:
                        dve.wait_ge(smax_done, 2 * t)
                    dve.tensor_copy(mask_now, maskb[:, bass.ds(q, 1)].rearrange("p a s -> p (a s)")).then_inc(mask_done, 1)
                    dve.wait_ge(mask_done, q + 1)
                dve.wait_ge(s_ps, t + 1)
                if low >= 2:
                    dve.wait_ge(exp_done, 2 * t - 2)
                dve.sem_inc(dve_go, 1)
                for a in range(2):
                    dve.tensor_tensor_reduce(sm[:, r2, a], bank(r2)[:, a * L:(a + 1) * L], mask_now, 1.0, -3e38,
                                             ALU.add, ALU.max, mx[:, r2, a:a + 1]).then_inc(smax_done, 1)
                dve.wait_ge(smax_done, 2 * t + 2)
                dve.tensor_scalar(nm[:, r2], mx[:, r2], -(HD ** -0.5), None, ALU.mult).then_inc(nm_done, 1)

            def pT_evac(t, r, q, low):
                dve.wait_ge(pT_ps, t + 1)
                if low >= 2:
                    dve.wait_ge(pv_ps, t - 1)
                dve.tensor_copy(pT[:, r % 2].rearrange("p a s -> p (a s)"), bank(2 + r % 2)).then_inc(pT_sb, 1)

            def recips(t, r, q, low):
                r2 = r % 2
                dve.wait_ge(exp_done, 2 * t + 2)
                if low >= 2:
                    dve.wait_ge(pn_done, t - 1)
                dve.reciprocal(rc[:, r2], sume[:, r2]).then_inc(rc_raw, 1)
                dve.wait_ge(rc_raw, t + 1)
                dve.tensor_scalar(rc[:, r2], rc[:, r2], valid[:, bass.ds(q, 1)], None, ALU.mult).then_inc(rc_done, 1)

            def x3(t, r, q, low):
                if r % 2 == 0:
                    return
                j = r // 2
                dve.wait_ge(ao_ps, NKV * q + j + 1)
                if low >= 2:
                    dve.wait_ge(x3_done, NKV * q + j)
                xv = xres[:, bass.ds(2 * q, 2), :].rearrange("p a d -> p (a d)")
                dve.scalar_tensor_tensor(out=xv, in0=bank(7), scalar=tg[:, 1:2], in1=xv, op0=ALU.mult,
                                         op1=ALU.add).then_inc(x3_done, 1)

            LINKS = 24
            links = [0]

            def rlink(q, ins):
                links[0] += 1
                ins.then_inc(route_chain, 1)
                dve.wait_ge(route_chain, LINKS * q + links[0])

            xk = lambda k: xres[:, bass.ds(k, 1), :].rearrange("p a d -> p (a d)")

            def stats4(h, q, k):
                if h == 0:
                    links[0] = 0
                dve.wait_ge(rec_free, q + 1)
                dve.wait_ge(x3_done, NKV * (q + 1))
                dve.sem_inc(dve_go, 1)
                rlink(q, dve.bn_stats(rst[:, h], xk(k)))
                dve.sem_inc(dve_go, 1)
                dve.bn_aggr(rmv[:, h, 0:2], rst[:, h]).then_inc(st4_done, 1)

            def norm4(h, q, k):
                dve.wait_ge(rstd4_done, k + 1)
                dve.tensor_copy(rec[:, h, REC - 1:REC], tok8[:, bass.ds(k, 1)])
                dve.tensor_scalar(rec[:, h, 0:DM], xk(k), rmv[:, h, 0:1], rmv[:, h, 2:3], ALU.subtract, ALU.mult
                                  ).then_inc(rec_done, 1)

            def rmax(h, q, k):
                dve.wait_ge(lg_ps, k + 1)
                dve.tensor_reduce(rsm[:, h, 0:1], bank(5)[:, DM:DM + NE], AX.X, ALU.max, negate=True
                                  ).then_inc(rmax_done, 1)

            def choose(h, q, k):
                top_i, top_w = rec[:, h, DM:DM + TOPK], rec[:, h, DM + TOPK:DM + 2 * TOPK]
                dve.wait_ge(rexp_done, k + 1)
                rlink(q, dve.reciprocal(rsm[:, h, 2:3], rsm[:, h, 1:2]))
                rlink(q, dve.tensor_scalar(rp[:, h], rp[:, h], rsm[:, h, 2:3], None, ALU.mult))
                dve.sem_inc(dve_go, 1)
                rlink(q, dve.max(top_w, rp[:, h]))
                dve.sem_inc(dve_go, 1)
                rlink(q, dve.max_index(idxu[:, h], top_w, rp[:, h]))
                rlink(q, dve.tensor_copy(top_i, idxu[:, h]))

            def one_hot(h, q, k):
                top_i = rec[:, h, DM:DM + TOPK]
                rlink(q, dve.tensor_tensor(v2(oh[:, h], TOPK), iota_e[:, :].unsqueeze(1).to_broadcast([P, TOPK, NE]),
                                           top_i.unsqueeze(2).to_broadcast([P, TOPK, NE]), ALU.is_equal))
                dve.tensor_reduce(fl[:, h], oh[:, h].rearrange("p (k e) -> p e k", k=TOPK), AX.X, ALU.add
                                  ).then_inc(fl_done, 1)

            def place(h, q, k):
                dve.wait_ge(pos_ps, k + 1)
                dve.tensor_tensor(v2(ohp, TOPK), v2(oh[:, h], TOPK),
                                  bank(5)[:, DM + NE:DM + 2 * NE].unsqueeze(1).to_broadcast([P, TOPK, NE]), ALU.mult
                                  ).then_inc(pos_used, 1)
                dve.wait_ge(fl_done, k + 1)
                dve.tensor_tensor(cum, cum, fl[:, h], ALU.add).then_inc(cum_done, 1)
                dve.wait_ge(pos_used, k + 1)
                rlink(q, dve.tensor_reduce(posk, v2(ohp, TOPK), AX.X, ALU.add))

            def slots(h, q, k):
                drop = drop_row[:, bass.ds(k * TOPK, TOPK)]
                rlink(q, dve.scalar_tensor_tensor(out=locf, in0=rec[:, h, DM:DM + TOPK], scalar=float(CAP), in1=posk,
                                                  op0=ALU.mult, op1=ALU.add))
                rlink(q, dve.tensor_tensor(loc2, locf, drop, ALU.subtract))
                rlink(q, dve.scalar_tensor_tensor(out=locf, in0=posk, scalar=float(CAP), in1=loc2, op0=ALU.is_lt,
                                                  op1=ALU.mult))
                rlink(q, dve.tensor_tensor(loc[:, h], locf, drop, ALU.add))
                dve.sem_inc(loc_done, 1)

            run_units(dve, [(2, smax), (3, pT_evac), (2, recips),
                            tile_at(20, 0, stats4), tile_at(21, 0, norm4), tile_at(21, 1, stats4),
                            tile_at(22, 1, norm4), tile_at(23, 0, rmax), tile_at(24, 0, choose),
                            tile_at(25, 0, one_hot), tile_at(25, 1, rmax), tile_at(26, 0, place), tile_at(26, 0, slots),
                            tile_at(27, 1, choose), tile_at(28, 1, one_hot), tile_at(29, 1, place),
                            tile_at(30, 1, slots), (4, x3)])

            def rows(t, r, q, low):
                ru = r % 2
                top_i, top_w = xg[:, r, DM:DM + TOPK], xg[:, r, DM + TOPK:DM + 2 * TOPK]
                me = iota_e[:, bass.ds(t, 1)]
                dve.wait_ge(xg_ld[r // 2], 16 * (q + 1))
                if low >= 8:
                    dve.wait_ge(scattered[r % 4], 16 * (2 * q + r // 4 - 1))
                    dve.wait_ge(ysb_done, t - 7)
                if low >= 2:
                    dve.wait_ge(msc1, 2 * t - 2)
                dve.scalar_tensor_tensor(out=junk[:, ru, 0:8], in0=top_i, scalar=me, in1=top_w, op0=ALU.is_equal,
                                         op1=ALU.mult, accum_out=wsl[:, r]).then_inc(msc1, 1)
                dve.scalar_tensor_tensor(out=junk[:, ru, 8:16], in0=top_i, scalar=me, in1=rank1[:, :],
                                         op0=ALU.is_equal, op1=ALU.mult, accum_out=msc[:, r, 0:1]).then_inc(msc1, 1)
                dve.wait_ge(msc1, 2 * t + 2)
                dve.scalar_tensor_tensor(out=msc[:, r, 1:2], in0=msc[:, r, 0:1], scalar=0.0,
                                         in1=empty_row[:, bass.ds(t, 1)], op0=ALU.is_equal, op1=ALU.mult
                                         ).then_inc(msc2, 1)
                dve.wait_ge(msc2, t + 1)
                dve.scalar_tensor_tensor(out=row[:, r], in0=xg[:, r, REC - 1:REC], scalar=msc[:, r, 0:1],
                                         in1=msc[:, r, 1:2], op0=ALU.add, op1=ALU.add).then_inc(row_done, 1)

            def gated(t, r, q, low):
                dve.wait_ge(sil_done, t + 1)
                if low >= 2:
                    dve.wait_ge(hT_ps, t - 1)
                dve.tensor_tensor(hh[:, r % 2], sil[:, r % 2], bank(2 + r % 2)[:, FE:2 * FE], ALU.mult
                                  ).then_inc(h_done, 1)

            def weigh(t, r, q, low):
                dve.wait_ge(yd_ps, t + 1)
                dve.wait_ge(row_done, t + 1)
                dve.tensor_scalar(ysb[:, r], bank(6 + r % 2)[:, 0:DM], wsl[:, r], None, ALU.mult).then_inc(ysb_done, 1)

            run_steps(dve, NE, 8, [(1, gated), (2, rows), (3, weigh)])

            for t in range(NT):
                dve.wait_ge(yk_ld[t % 4], 16 * (t // 4 + 1))
                dve.tensor_reduce(ysum[:, t % 2], yall[:, t % 4].rearrange("p (k d) -> p d k", k=TOPK), AX.X, ALU.add
                                  ).then_inc(ysum_done, 1)
                dve.wait_ge(ysum_done, t + 1)
                dve.scalar_tensor_tensor(out=xres[:, t, :], in0=ysum[:, t % 2], scalar=tg[:, 3:4], in1=xres[:, t, :],
                                         op0=ALU.mult, op1=ALU.add).then_inc(out_done, 1)



_INS = ['x', 'ctx_1024', 'mask_BxS2_bf1', 'g_xattn', 'g_ffn', 'L0_xattn_in_proj_w', 'L0_xattn_conv_w',
        'L0_xattn_conv_b', 'L0_xattn_x_proj_w', 'L0_xattn_dt_proj_w', 'L0_xattn_dt_proj_b', 'L0_xattn_A_log',
        'L0_xattn_D', 'L0_ffn_c_fc', 'L0_ffn_c_proj', 'L1_xattn_Wq', 'L1_xattn_Wk', 'L1_xattn_Wv', 'L1_xattn_Wo',
        'L1_ffn_gate_w', 'L1_ffn_w_gate', 'L1_ffn_w_up', 'L1_ffn_w_down']


def kernel(**inputs):
    import numpy as _np
    import concourse.bacc as _bacc
    from concourse import mybir as _mybir
    from concourse.bass_utils import run_bass_kernel_spmd as _run

    nc = _bacc.Bacc("TRN2", target_bir_lowering=False, num_devices=1)
    arrays, args = {}, []
    for name in _INS:
        a = _np.ascontiguousarray(inputs[name])
        arrays[f"in_{name}"] = a
        args.append(nc.dram_tensor(f"in_{name}", a.shape, _mybir.dt.from_np(a.dtype), kind="ExternalInput").ap())
    args.append(nc.dram_tensor("out_0", (NB, L, DM), F32, kind="ExternalOutput").ap())
    flamingo_kernel(nc, *args)
    r = _run(nc, [arrays], core_ids=[0])
    return r.results[0]["out_0"]
```
